# Optimizing a Trainium2 kernel written in Bass

```python
import numpy as np
import jax
import jax.numpy as jnp

def _softmax(x, axis=-1):
    return jax.nn.softmax(x, axis=axis)

def _gelu(x):
    return jax.nn.gelu(x, approximate=True)

def _silu(x):
    return jax.nn.silu(x)

def _sigmoid(x):
    return jax.nn.sigmoid(x)

def _layernorm(x, axis=-1, eps=1e-05):
    m = jnp.mean(x, axis=axis, keepdims=True)
    v = jnp.var(x, axis=axis, keepdims=True)
    return (x - m) / jnp.sqrt(v + eps)

def _scatter_add(tgt, idx, src, axis=0):
    return tgt.at[idx].add(src)

def _segment_sum(src, seg, n):
    return jax.ops.segment_sum(src, seg, n)
kernel_name = 'mk_gnn_ffn_d2_gnn_r16_5087fe'

def setup_inputs(seed: int=0):
    np.random.seed(seed)
    _w = jnp.asarray

    def _rec_inputs():
        import jax
        import jax.numpy as jnp
        _gk = jax.random.key(seed)
        x = -0.0003713 + 1 * jax.random.normal(jax.random.fold_in(_gk, 1), (3125, 256), jnp.float32)
        src = jax.random.randint(jax.random.fold_in(_gk, 2), (100000,), 0, 3125, jnp.int32)
        dst = jax.random.randint(jax.random.fold_in(_gk, 3), (100000,), 0, 3125, jnp.int32)
        _o = jnp.argsort(dst, stable=True)
        src = src[_o]
        dst = dst[_o]
        node_type_24 = jax.random.randint(jax.random.fold_in(_gk, 12), (3125,), 0, 24, jnp.int32)
        return (x, src, dst, node_type_24)
    x, src, dst, node_type_24 = _rec_inputs()

    def _L0_gnn_setup():
        import jax, jax.numpy as jnp
        import numpy as np
        N = 3125
        E = 50000
        F_IN = 256
        HID = 64
        H = 4
        NC = 23
        NEG_SLOPE = 0.2

        def _gat_layer(h, W, attn_l, attn_r, bias, src, dst):
            feat = (h @ W.T).reshape(-1, H, HID)
            el = jnp.einsum('nhd,hd->nh', feat, attn_l)
            er = jnp.einsum('nhd,hd->nh', feat, attn_r)
            e = jax.nn.leaky_relu(el[src] + er[dst], NEG_SLOPE)
            m = jax.ops.segment_max(e, dst, num_segments=N)
            m = jnp.where(jnp.isfinite(m), m, 0.0)
            ex = jnp.exp(e - m[dst])
            den = jax.ops.segment_sum(ex, dst, num_segments=N)
            a = ex / jnp.maximum(den[dst], 1e-09)
            out = jax.ops.segment_sum(a[:, :, None] * feat[src], dst, num_segments=N)
            out = out + bias.reshape(1, H, HID)
            return jax.nn.relu(out).reshape(-1, H * HID)
        key = jax.random.key(seed)
        ks = jax.random.split(key, 18)
        s = 0.05
        emb = jax.random.normal(ks[4], (NC + 1, F_IN), jnp.float32) * s
        emb = emb.at[NC].set(0.0)
        return {'features': jax.random.normal(ks[0], (N, F_IN), jnp.float32), 'input_labels': jax.random.randint(ks[1], (N,), 0, NC + 1), 'src': jax.random.randint(ks[2], (E,), 0, N), 'dst': jax.random.randint(ks[3], (E,), 0, N), 'emb': emb, 'le_W1': jax.random.normal(ks[5], (4 * F_IN, 2 * F_IN), jnp.float32) * s, 'le_b1': jnp.zeros((4 * F_IN,), jnp.float32), 'ln_g': jnp.ones((4 * F_IN,), jnp.float32), 'ln_b': jnp.zeros((4 * F_IN,), jnp.float32), 'le_W2': jax.random.normal(ks[6], (F_IN, 4 * F_IN), jnp.float32) * s, 'le_b2': jnp.zeros((F_IN,), jnp.float32), 'W1': jax.random.normal(ks[7], (H * HID, F_IN), jnp.float32) * s, 'al1': jax.random.normal(ks[8], (H, HID), jnp.float32) * s, 'ar1': jax.random.normal(ks[9], (H, HID), jnp.float32) * s, 'b1': jnp.zeros((H * HID,), jnp.float32), 'W2': jax.random.normal(ks[10], (H * HID, H * HID), jnp.float32) * s, 'al2': jax.random.normal(ks[11], (H, HID), jnp.float32) * s, 'ar2': jax.random.normal(ks[12], (H, HID), jnp.float32) * s, 'b2': jnp.zeros((H * HID,), jnp.float32)}
    _L0_gnn_all = _L0_gnn_setup()
    _L0_gnn_in = {k: v for k, v in _L0_gnn_all.items() if k in ('emb', 'le_W1', 'le_b1', 'ln_g', 'ln_b', 'le_W2', 'le_b2', 'W1', 'al1', 'ar1', 'b1', 'W2', 'al2', 'ar2', 'b2')}
    del _L0_gnn_all

    def _L0_ffn_setup():
        import math
        import jax, jax.numpy as jnp
        import numpy as np
        CAPACITY_FACTOR = 1.25
        key = jax.random.key(seed)
        ks = jax.random.split(key, 5)
        B, L, D, F, E = (8, 512, 256, 1024, 8)
        h = jax.random.normal(ks[0], (B, L, D), dtype=jnp.float32)
        gate_w = jax.random.normal(ks[1], (D, E), dtype=jnp.float32) * 0.02
        gate_b = jnp.zeros((E,), dtype=jnp.float32)
        w1 = jax.random.normal(ks[2], (E, D, F), dtype=jnp.float32) * (1.0 / math.sqrt(D))
        b1 = jnp.zeros((E, F), dtype=jnp.float32)
        w2 = jax.random.normal(ks[3], (E, F, D), dtype=jnp.float32) * (1.0 / math.sqrt(F))
        b2 = jnp.zeros((E, D), dtype=jnp.float32)
        return {'h': h, 'gate_w': gate_w, 'gate_b': gate_b, 'w1': w1, 'b1': b1, 'w2': w2, 'b2': b2}
    _L0_ffn_all = _L0_ffn_setup()
    _L0_ffn_in = {k: v for k, v in _L0_ffn_all.items() if k in ('gate_w', 'gate_b', 'w1', 'b1', 'w2', 'b2')}
    del _L0_ffn_all

    def _L1_gnn_setup():
        import jax, jax.numpy as jnp
        import numpy as np
        N, E, D = (3125, 50000, 256)
        key = jax.random.key(seed)
        ks = jax.random.split(key, 12)
        s = 1.0 / np.sqrt(D)
        return {'x': jax.random.normal(ks[0], (N, D), dtype=jnp.float32), 'src': jax.random.randint(ks[1], (E,), 0, N, dtype=jnp.int64), 'dst': jax.random.randint(ks[2], (E,), 0, N, dtype=jnp.int64), 'W_w': jax.random.normal(ks[3], (D, D), dtype=jnp.float32) * s, 'W_b': jnp.zeros((D,), dtype=jnp.float32), 'U_w': jax.random.normal(ks[4], (D, D), dtype=jnp.float32) * s, 'U_b': jnp.zeros((D,), dtype=jnp.float32), 'V_w': jax.random.normal(ks[5], (D, D), dtype=jnp.float32) * s, 'V_b': jnp.zeros((D,), dtype=jnp.float32), 'attn_l': jax.random.normal(ks[6], (D,), dtype=jnp.float32) * s, 'attn_r': jax.random.normal(ks[7], (D,), dtype=jnp.float32) * s, 'gamma': jnp.ones((D,), dtype=jnp.float32), 'beta': jnp.zeros((D,), dtype=jnp.float32)}
    _L1_gnn_all = _L1_gnn_setup()
    _L1_gnn_in = {k: v for k, v in _L1_gnn_all.items() if k in ('W_w', 'W_b', 'U_w', 'U_b', 'V_w', 'V_b', 'attn_l', 'attn_r', 'gamma', 'beta')}
    del _L1_gnn_all

    def _L1_ffn_setup():
        import jax, jax.numpy as jnp
        import numpy as np
        C = 256
        HID = 1024
        E = 8
        TEMP = 1.0
        key = jax.random.key(seed)
        ks = jax.random.split(key, 7)
        x = jax.random.normal(ks[0], (8, 1024, C), dtype=jnp.float32)
        W1 = jax.random.normal(ks[1], (C, HID), dtype=jnp.float32) * 0.02
        b1 = jnp.zeros((HID,), dtype=jnp.float32)
        Wg = jax.random.normal(ks[2], (HID, E), dtype=jnp.float32) * 0.02
        bg = jnp.zeros((E,), dtype=jnp.float32)
        Wd = jax.random.normal(ks[3], (E, HID, C), dtype=jnp.float32) * 0.02
        bd = jnp.zeros((E, C), dtype=jnp.float32)
        return {'x': x, 'W1': W1, 'b1': b1, 'Wg': Wg, 'bg': bg, 'Wd': Wd, 'bd': bd}
    _L1_ffn_all = _L1_ffn_setup()
    _L1_ffn_in = {k: v for k, v in _L1_ffn_all.items() if k in ('W1', 'b1', 'Wg', 'bg', 'Wd', 'bd')}
    del _L1_ffn_all
    return {'x': x, 'src': src, 'dst': dst, 'node_type_24': node_type_24, 'L0_gnn_emb': _L0_gnn_in['emb'], 'L0_gnn_le_W1': _L0_gnn_in['le_W1'], 'L0_gnn_le_b1': _L0_gnn_in['le_b1'], 'L0_gnn_ln_g': _L0_gnn_in['ln_g'], 'L0_gnn_ln_b': _L0_gnn_in['ln_b'], 'L0_gnn_le_W2': _L0_gnn_in['le_W2'], 'L0_gnn_le_b2': _L0_gnn_in['le_b2'], 'L0_gnn_W1': _L0_gnn_in['W1'], 'L0_gnn_al1': _L0_gnn_in['al1'], 'L0_gnn_ar1': _L0_gnn_in['ar1'], 'L0_gnn_b1': _L0_gnn_in['b1'], 'L0_gnn_W2': _L0_gnn_in['W2'], 'L0_gnn_al2': _L0_gnn_in['al2'], 'L0_gnn_ar2': _L0_gnn_in['ar2'], 'L0_gnn_b2': _L0_gnn_in['b2'], 'L0_ffn_gate_w': _L0_ffn_in['gate_w'], 'L0_ffn_gate_b': _L0_ffn_in['gate_b'], 'L0_ffn_w1': _L0_ffn_in['w1'], 'L0_ffn_b1': _L0_ffn_in['b1'], 'L0_ffn_w2': _L0_ffn_in['w2'], 'L0_ffn_b2': _L0_ffn_in['b2'], 'L1_gnn_W_w': _L1_gnn_in['W_w'], 'L1_gnn_W_b': _L1_gnn_in['W_b'], 'L1_gnn_U_w': _L1_gnn_in['U_w'], 'L1_gnn_U_b': _L1_gnn_in['U_b'], 'L1_gnn_V_w': _L1_gnn_in['V_w'], 'L1_gnn_V_b': _L1_gnn_in['V_b'], 'L1_gnn_attn_l': _L1_gnn_in['attn_l'], 'L1_gnn_attn_r': _L1_gnn_in['attn_r'], 'L1_gnn_gamma': _L1_gnn_in['gamma'], 'L1_gnn_beta': _L1_gnn_in['beta'], 'L1_ffn_W1': _L1_ffn_in['W1'], 'L1_ffn_b1': _L1_ffn_in['b1'], 'L1_ffn_Wg': _L1_ffn_in['Wg'], 'L1_ffn_bg': _L1_ffn_in['bg'], 'L1_ffn_Wd': _L1_ffn_in['Wd'], 'L1_ffn_bd': _L1_ffn_in['bd']}

def reference(x, src, dst, node_type_24, L0_gnn_emb, L0_gnn_le_W1, L0_gnn_le_b1, L0_gnn_ln_g, L0_gnn_ln_b, L0_gnn_le_W2, L0_gnn_le_b2, L0_gnn_W1, L0_gnn_al1, L0_gnn_ar1, L0_gnn_b1, L0_gnn_W2, L0_gnn_al2, L0_gnn_ar2, L0_gnn_b2, L0_ffn_gate_w, L0_ffn_gate_b, L0_ffn_w1, L0_ffn_b1, L0_ffn_w2, L0_ffn_b2, L1_gnn_W_w, L1_gnn_W_b, L1_gnn_U_w, L1_gnn_U_b, L1_gnn_V_w, L1_gnn_V_b, L1_gnn_attn_l, L1_gnn_attn_r, L1_gnn_gamma, L1_gnn_beta, L1_ffn_W1, L1_ffn_b1, L1_ffn_Wg, L1_ffn_bg, L1_ffn_Wd, L1_ffn_bd):
    import jax
    import jax.numpy as jnp

    def _L0_gnn_ref(features, emb, le_W1, le_b1, ln_g, ln_b, le_W2, le_b2, W1, al1, ar1, b1, W2, al2, ar2, b2, input_labels, src, dst):
        import jax, jax.numpy as jnp
        import numpy as np
        N = 3125
        E = 50000
        F_IN = 256
        HID = 64
        H = 4
        NC = 23
        NEG_SLOPE = 0.2

        def _gat_layer(h, W, attn_l, attn_r, bias, src, dst):
            feat = (h @ W.T).reshape(-1, H, HID)
            el = jnp.einsum('nhd,hd->nh', feat, attn_l)
            er = jnp.einsum('nhd,hd->nh', feat, attn_r)
            e = jax.nn.leaky_relu(el[src] + er[dst], NEG_SLOPE)
            m = jax.ops.segment_max(e, dst, num_segments=N)
            m = jnp.where(jnp.isfinite(m), m, 0.0)
            ex = jnp.exp(e - m[dst])
            den = jax.ops.segment_sum(ex, dst, num_segments=N)
            a = ex / jnp.maximum(den[dst], 1e-09)
            out = jax.ops.segment_sum(a[:, :, None] * feat[src], dst, num_segments=N)
            out = out + bias.reshape(1, H, HID)
            return jax.nn.relu(out).reshape(-1, H * HID)
        lab = emb[input_labels]
        x = jnp.concatenate([features, lab], axis=-1)
        x = x @ le_W1.T + le_b1
        mu = jnp.mean(x, axis=-1, keepdims=True)
        var = jnp.var(x, axis=-1, keepdims=True)
        x = (x - mu) * jax.lax.rsqrt(var + 1e-05) * ln_g + ln_b
        x = jax.nn.relu(x)
        h = x @ le_W2.T + le_b2
        h = _gat_layer(h, W1, al1, ar1, b1, src, dst)
        h = _gat_layer(h, W2, al2, ar2, b2, src, dst)
        return h

    def _L0_ffn_ref(h, gate_w, gate_b, w1, b1, w2, b2):
        import math
        import jax, jax.numpy as jnp
        import numpy as np
        CAPACITY_FACTOR = 1.25
        B, L, D = h.shape
        E = gate_w.shape[1]
        T = B * L
        C = max(1, math.ceil(CAPACITY_FACTOR * T / E))
        x = h.reshape(T, D)
        logits = x @ gate_w + gate_b
        probs = jax.nn.softmax(logits, axis=-1)
        idx = jnp.argmax(probs, axis=-1)
        prb = jnp.take_along_axis(probs, idx[:, None], axis=1)[:, 0]
        one_hot = jax.nn.one_hot(idx, E, dtype=jnp.float32)
        pos = (jnp.cumsum(one_hot, axis=0) * one_hot).sum(-1).astype(jnp.int32) - 1
        kept = pos < C
        pos_safe = jnp.where(kept, pos, C)
        buf = jnp.zeros((E, C, D), dtype=h.dtype).at[idx, pos_safe].set(x, mode='drop')
        hmid = jax.nn.relu(jnp.einsum('ecd,edf->ecf', buf, w1) + b1[:, None, :])
        ybuf = jnp.einsum('ecf,efd->ecd', hmid, w2) + b2[:, None, :]
        pos_g = jnp.minimum(pos, C - 1)
        y_tok = ybuf[idx, pos_g] * (prb * kept)[:, None]
        y = y_tok.reshape(B, L, D)
        y = jnp.nan_to_num(y, nan=0.0, posinf=10000.0, neginf=-10000.0)
        return y

    def _L1_gnn_ref(x, src, dst, W_w, W_b, U_w, U_b, V_w, V_b, attn_l, attn_r, gamma, beta):
        import jax, jax.numpy as jnp
        import numpy as np
        N, E, D = (3125, 50000, 256)
        Wh = x @ W_w + W_b
        Uh = x @ U_w + U_b
        Vh = x @ V_w + V_b
        out_src = Wh * attn_l
        out_dst = Wh * attn_r
        sigma = jax.nn.sigmoid(out_src[src] + out_dst[dst])
        sum_sigma_h = jax.ops.segment_sum(Vh[src] * sigma, dst, num_segments=N)
        sum_sigma = jax.ops.segment_sum(sigma, dst, num_segments=N)
        h = Uh + sum_sigma_h / (sum_sigma + 1e-06)
        mu = jnp.mean(h, axis=-1, keepdims=True)
        var = jnp.mean((h - mu) ** 2, axis=-1, keepdims=True)
        h = (h - mu) / jnp.sqrt(var + 1e-06) * gamma + beta
        h = jax.nn.relu(h)
        return x + h

    def _L1_ffn_ref(x, W1, b1, Wg, bg, Wd, bd):
        import jax, jax.numpy as jnp
        import numpy as np
        C = 256
        HID = 1024
        E = 8
        TEMP = 1.0
        orig_shape = x.shape
        xf = x.reshape(-1, orig_shape[-1])
        H = jax.nn.gelu(xf @ W1 + b1, approximate=False)
        probs = jax.nn.softmax((H @ Wg + bg) / TEMP, axis=-1)
        assign = jnp.argmax(probs, axis=-1)
        out = jnp.zeros_like(xf)
        for e in range(Wd.shape[0]):
            y = H @ Wd[e] + bd[e]
            sel = (assign == e)[:, None]
            out = out + jnp.where(sel, probs[:, e:e + 1] * y, 0.0)
        return out.reshape(orig_shape)
    x = x + _L0_gnn_ref(_layernorm(x, axis=-1), L0_gnn_emb, L0_gnn_le_W1, L0_gnn_le_b1, L0_gnn_ln_g, L0_gnn_ln_b, L0_gnn_le_W2, L0_gnn_le_b2, L0_gnn_W1, L0_gnn_al1, L0_gnn_ar1, L0_gnn_b1, L0_gnn_W2, L0_gnn_al2, L0_gnn_ar2, L0_gnn_b2, node_type_24, src, dst)
    x = x + _L0_ffn_ref(_layernorm(x, axis=-1)[None], L0_ffn_gate_w, L0_ffn_gate_b, L0_ffn_w1, L0_ffn_b1, L0_ffn_w2, L0_ffn_b2)[0]
    x = x + _L1_gnn_ref(_layernorm(x, axis=-1), src, dst, L1_gnn_W_w, L1_gnn_W_b, L1_gnn_U_w, L1_gnn_U_b, L1_gnn_V_w, L1_gnn_V_b, L1_gnn_attn_l, L1_gnn_attn_r, L1_gnn_gamma, L1_gnn_beta)
    x = x + _L1_ffn_ref(_layernorm(x, axis=-1)[None], L1_ffn_W1, L1_ffn_b1, L1_ffn_Wg, L1_ffn_bg, L1_ffn_Wd, L1_ffn_bd)[0]
    return x

_drawn_inputs = setup_inputs


def setup_inputs(seed=0):
    import zlib

    import numpy as np

    out = dict(_drawn_inputs(seed))
    spreads = {'L0_gnn_le_b1': (0.0, 0.1),
     'L0_gnn_ln_g': (1.0, 0.2),
     'L0_gnn_ln_b': (0.0, 0.1),
     'L0_gnn_le_b2': (0.0, 0.1),
     'L0_gnn_b1': (0.0, 0.1),
     'L0_gnn_b2': (0.0, 0.1),
     'L0_ffn_gate_b': (0.0, 0.1),
     'L0_ffn_b1': (0.0, 0.623),
     'L0_ffn_b2': (0.0, 0.445),
     'L1_gnn_W_b': (0.0, 0.8),
     'L1_gnn_U_b': (0.0, 0.1),
     'L1_gnn_V_b': (0.0, 0.1),
     'L1_gnn_gamma': (1.0, 0.2),
     'L1_gnn_beta': (0.0, 0.1),
     'L1_ffn_b1': (0.0, 0.8),
     'L1_ffn_bg': (0.0, 0.8),
     'L1_ffn_bd': (0.0, 0.8)}
    factors = {'L0_gnn_emb': 7.79,
     'L0_gnn_al1': 3.169,
     'L0_gnn_ar1': 8.0,
     'L0_gnn_al2': 8.0,
     'L0_gnn_ar2': 128.099,
     'L1_gnn_W_w': 8.0,
     'L1_gnn_attn_l': 8.0,
     'L1_gnn_attn_r': 8.0,
     'L1_ffn_W1': 5.692,
     'L1_ffn_Wg': 5.885,
     'L1_ffn_Wd': 6.923}
    for name, (base, spread) in spreads.items():
        noise = np.random.default_rng([zlib.crc32(name.encode()), seed]).standard_normal(out[name].shape)
        drawn = base * np.exp(spread * noise) if base else spread * noise
        out[name] = jnp.asarray(drawn.astype(out[name].dtype))
    for name, factor in factors.items():
        out[name] = (out[name] * factor).astype(out[name].dtype)
    return out
```

```python
from contextlib import ExitStack

import numpy as np

import concourse.bass as bass
from concourse import mybir

F32 = mybir.dt.float32
BF16 = mybir.dt.bfloat16
I32 = mybir.dt.int32
U32 = mybir.dt.uint32
ALU = mybir.AluOpType
ACT = mybir.ActivationFunctionType
AX = mybir.AxisListType
ds = bass.ds

P = 128
N = 3125
D = 256
NB = -(-N // P)
NP = NB * P
TAIL = N - (NB - 1) * P
E = 100000
EC = -(-E // P)
ET = 4
EG = ET * P
NG = (E + NB * (EG - 1)) // EG
UN = 4
NG = -(-NG // UN) * UN
GC = -(-NG // P)
H = 4
HD = D // H
HW = HD + 1
NC = 24
F = 1024
FC = F // P
KC = D // P
NE = 8
CAP = max(1, -(-5 * N // (4 * NE)))
CS = -(-CAP // P) * P
TW = D + 3 * H
SPREAD = 20.0
SLOPE = 0.2
BIG = float(2.0 ** 100)


def skewed(eng, count, unroll, front, back, peel=0):
    def step(n, k):
        front(n + 1, (k + 1) % unroll)
        back(n, k)

    front(0, 0)
    for n in range(peel):
        step(n, n % unroll)
    whole = (count - 1) // unroll
    with eng.Fori(peel // unroll, whole) as i:
        for k in range(unroll):
            step(i * unroll + k, k)
    for n in range(whole * unroll, count - 1):
        step(n, n % unroll)
    back(count - 1, (count - 1) % unroll)


def hold(eng, sem, value, gate):
    eng.wait_ge(sem, value)
    eng.sem_inc(gate, 1)


class Consts:
    pass


def alloc(nc, ctx, stage=""):
    def sb(name, shape, dt=F32):
        return ctx.enter_context(nc.sbuf_tensor(stage + name, shape, dt))

    def ps(name, shape, dt=F32):
        return ctx.enter_context(nc.psum_tensor(stage + name, shape, dt))

    sems = []

    def clear():
        if sems:
            nc.clear_and_free_semaphores(sems)
            nc.all_engine_barrier()

    ctx.callback(clear)

    def sem(name):
        sems.append(nc.alloc_semaphore(stage + name))
        return sems[-1]

    return sb, ps, sem


def ln_stats(nc, v, act_std, X, mv, st, rstd, s_st, s_var, s_std, eps):
    with v.Fori(0, NB) as b:
        nc.vector.bn_stats(st[:, ds(b * 6, 6)], X[:, ds(b * D, D)]).then_inc(s_st, 1)
    v.wait_ge(s_st, NB)
    ln_finish(nc, v, mv, st, rstd, s_st, s_var, s_std, eps, NB)


def ln_finish(nc, v, mv, st, rstd, s_st, s_var, s_std, eps, base=0):
    for b in range(NB):
        nc.vector.bn_aggr(mv[:, b * 2:b * 2 + 2], st[:, b * 6:b * 6 + 6]).then_inc(s_st, 1)
    v.wait_ge(s_st, base + NB)
    var = mv[:, :].rearrange("p (b t) -> p b t", t=2)[:, :, 1]
    nc.vector.tensor_scalar(rstd[:, :], var, float(eps), None, ALU.add).then_inc(s_var, 1)
    v.wait_ge(s_std, 1)
    nc.vector.reciprocal(rstd[:, :], rstd[:, :]).then_inc(s_var, 1)
    v.wait_ge(s_var, 2)


def ln_sqrt(nc, act, rstd, s_var, s_std):
    act.wait_ge(s_var, 1)
    nc.scalar.activation(rstd[:, :], rstd[:, :], ACT.Sqrt).then_inc(s_std, 1)


def stage_setup(nc, C, A):
    with ExitStack() as ctx:
        sb, ps, sem = alloc(nc, ctx, "setup_")
        srcs = sb("srcs", [P, EC], I32)
        dsts = sb("dsts", [P, EC], I32)
        pairs = sb("pairs", [P, EC, 2], I32)
        padpair = sb("padpair", [1, EG, 2], I32)
        dstf = sb("dstf", [P, EC])
        below = sb("below", [P, NB + 1])
        junk = sb("junk", [P, 2, EC])
        onesq = sb("onesq", [P, P])
        first = sb("first", [P, NB + 1])
        cnt = sb("cnt", [P, NB])
        cnti = sb("cnti", [P, NB], I32)
        ng = sb("ng", [P, NB])
        gend = sb("gend", [P, NB])
        gfirst = sb("gfirst", [P, NB])
        shift = sb("shift", [P, NB])
        gidi = sb("gidi", [P, GC], I32)
        gid = sb("gid", [P, GC])
        ge = sb("ge", [P, GC, NB])
        gblk = sb("gblk", [P, GC])
        goff = sb("goff", [P, GC])
        gtab = sb("gtab", [P, 2, GC], I32)
        iotai = sb("iotai", [P, P], I32)
        labi = sb("labi", [P, NB], I32)
        zero = sb("zero", [P, D])
        pt = ps("pt", [P, 512])
        s_x = sem("s_x"); s_e = sem("s_e"); s_lab = sem("s_lab"); s_pool = sem("s_pool")
        s_v = sem("s_v"); s_pr = sem("s_pr"); s_cnt = sem("s_cnt"); s_tot = sem("s_tot")
        s_pair = sem("s_pair"); s_gt = sem("s_gt"); s_gtd = sem("s_gtd"); s_tab = sem("s_tab")
        s_z = sem("s_z"); s_zd = sem("s_zd")
        full = E // EC
        rest = E - full * EC

        with nc.Block() as block:
            @block.sync
            def _(sp):
                sp.wait_ge(s_z, 4)
                sp.dma_start(dsts[0:full, :], A["dst"][0:full * EC].rearrange("(p c) -> p c", c=EC)).then_inc(s_e, 16)
                sp.dma_start(dsts[full:full + 1, 0:rest], A["dst"][full * EC:E].rearrange("(p c) -> p c", p=1)).then_inc(s_e, 16)
                sp.dma_start(srcs[0:full, :], A["src"][0:full * EC].rearrange("(p c) -> p c", c=EC)).then_inc(s_e, 16)
                sp.dma_start(srcs[full:full + 1, 0:rest], A["src"][full * EC:E].rearrange("(p c) -> p c", p=1)).then_inc(s_e, 16)
                sp.wait_ge(s_pr, 2)
                sp.dma_start(C.edges[0:P * EC, :].rearrange("(p c) t -> p (c t)", c=EC), pairs[:, :, :].rearrange("p c t -> p (c t)")).then_inc(s_pair, 16)
                sp.dma_start(C.edges[P * EC:C.edge_rows, :].rearrange("(a c) t -> a (c t)", a=1), padpair[0:1, 0:C.edge_rows - P * EC, :].rearrange("p c t -> p (c t)")).then_inc(s_pair, 16)
                sp.wait_ge(s_gt, 1)
                for t in range(2):
                    sp.dma_start(C.gtab_d[t, :].rearrange("(c p) -> p c", p=P), gtab[:, t, :], allow_slow_non_contiguous=True).then_inc(s_gtd, 16)
                sp.wait_ge(s_gtd, 32)
                sp.dma_start(C.gofs[0:1, :], C.gtab_d[1:2, :]).then_inc(s_tab, 16)
                sp.dma_start(C.gblk[0:1, :], C.gtab_d[0:1, :]).then_inc(s_tab, 16)
                sp.dma_start(C.gblkb[:, :], C.gtab_d[0, :].partition_broadcast(P)).then_inc(s_tab, 16)
                sp.wait_ge(s_pair, 32)
                sp.wait_ge(s_tab, 48)
                sp.wait_ge(s_zd, 16)

            @block.scalar
            def _(act):
                act.wait_ge(s_pool, 3)
                act.dma_start(C.X[:, 0:(NB - 1) * D].rearrange("p (b d) -> p b d", d=D),
                              A["x"][0:(NB - 1) * P, :].rearrange("(b p) d -> p b d", p=P)).then_inc(s_x, 16)
                act.dma_start(C.X[0:TAIL, (NB - 1) * D:NB * D], A["x"][(NB - 1) * P:N, :]).then_inc(s_x, 16)
                act.dma_start(labi[:, 0:NB - 1], A["node_type_24"][0:(NB - 1) * P].rearrange("(b p) -> p b", p=P), allow_slow_non_contiguous=True).then_inc(s_lab, 16)
                act.dma_start(labi[0:TAIL, NB - 1:NB], A["node_type_24"][(NB - 1) * P:N].rearrange("(p a) -> p a", a=1)).then_inc(s_lab, 16)
                act.wait_ge(s_z, 4)
                act.dma_start(C.ffn_in[:, :].rearrange("(c p) d -> p c d", p=P), zero[:, :].unsqueeze(1).broadcast_to([P, NE * CS // P, D])).then_inc(s_zd, 16)
                act.wait_ge(s_x, 32)

            @block.gpsimd
            def _(gp):
                nc.gpsimd.memset(C.X[:, (NB - 1) * D:NB * D], 0.0).then_inc(s_pool, 1)
                nc.gpsimd.memset(labi[:, :], 0).then_inc(s_pool, 1)
                nc.gpsimd.memset(C.ident[:, :], 0.0).then_inc(s_pool, 1)
                nc.gpsimd.iota(iotai[:, :], pattern=[[1, P]], base=0, channel_multiplier=0).then_inc(s_pool, 1)
                nc.gpsimd.iota(gidi[:, :], pattern=[[P, GC]], base=0, channel_multiplier=1).then_inc(s_pool, 1)
                gp.wait_ge(s_pool, 5)
                nc.gpsimd.affine_select(out=C.ident[:, :], in_=C.ident[:, :], compare_op=ALU.not_equal, fill=1.0,
                                        base=0, pattern=[[-1, P]], channel_multiplier=1).then_inc(s_pool, 1)

            @block.vector
            def _(v):
                nc.vector.memset(dsts[:, :], -1).then_inc(s_z, 1)
                nc.vector.memset(srcs[:, :], 0).then_inc(s_z, 1)
                nc.vector.memset(padpair[:, :, :], -1).then_inc(s_z, 1)
                nc.vector.memset(zero[:, :], 0.0).then_inc(s_z, 1)
                nc.vector.memset(onesq[:, :], 1.0).then_inc(s_v, 1)
                nc.vector.memset(below[:, 0:1], 0.0).then_inc(s_v, 1)
                v.wait_ge(s_z, 3)
                nc.vector.memset(padpair[:, :, 0], 0).then_inc(s_pr, 1)
                v.wait_ge(s_pool, 6)
                nc.vector.tensor_copy(C.iota[:, :], iotai[:, :]).then_inc(s_v, 1)
                nc.vector.tensor_copy(gid[:, :], gidi[:, :]).then_inc(s_v, 1)
                nc.vector.tensor_scalar(C.bigi[:, :], C.ident[:, :], BIG, None, ALU.mult).then_inc(s_v, 1)
                v.wait_ge(s_lab, 32)
                nc.vector.tensor_copy(C.lab[:, :], labi[:, :]).then_inc(s_v, 1)
                v.wait_ge(s_e, 64)
                nc.vector.tensor_copy(dstf[:, :], dsts[:, :]).then_inc(s_v, 1)
                nc.vector.tensor_copy(pairs[:, :, 1], dsts[:, :]).then_inc(s_v, 1)
                v.wait_ge(s_v, 8)
                nc.vector.tensor_copy(pairs[:, :, 0], srcs[:, :]).then_inc(s_pr, 1)
                nc.vector.tensor_scalar(junk[:, 0, :], dstf[:, :], 0.0, 0.0, ALU.is_ge, ALU.add, accum_out=below[:, NB:NB + 1]).then_inc(s_v, 1)
                for b in range(1, NB):
                    v.wait_ge(s_v, 9 + (b - 1) // 1)
                    nc.vector.tensor_scalar(junk[:, 0, :], dstf[:, :], float(P * b), 0.0, ALU.is_ge, ALU.add,
                                            accum_out=below[:, b:b + 1]).then_inc(s_v, 1)
                v.wait_ge(s_v, 8 + NB)
                nc.vector.tensor_tensor(below[:, 1:NB], below[:, NB:NB + 1].broadcast_to([P, NB - 1]), below[:, 1:NB], ALU.subtract).then_inc(s_cnt, 1)
                v.wait_ge(s_tot, 1)
                nc.vector.tensor_copy(first[:, :], pt[:, 0:NB + 1]).then_inc(s_v, 1)
                base = 8 + NB
                v.wait_ge(s_v, base + 1)
                nc.vector.tensor_tensor(cnt[:, :], first[:, 1:NB + 1], first[:, 0:NB], ALU.subtract).then_inc(s_v, 1)
                v.wait_ge(s_v, base + 2)
                nc.vector.tensor_scalar(cnti[:, :], cnt[:, :], float(EG - 1), None, ALU.add).then_inc(s_v, 1)
                v.wait_ge(s_v, base + 3)
                nc.vector.tensor_scalar(cnti[:, :], cnti[:, :], EG.bit_length() - 1, None, ALU.arith_shift_right).then_inc(s_v, 1)
                v.wait_ge(s_v, base + 4)
                nc.vector.tensor_copy(ng[:, :], cnti[:, :]).then_inc(s_v, 1)
                v.wait_ge(s_v, base + 5)
                nc.vector.tensor_tensor_scan(gend[:, :], ng[:, :], ng[:, :], 0.0, ALU.add, ALU.bypass).then_inc(s_v, 1)
                v.wait_ge(s_v, base + 6)
                nc.vector.tensor_tensor(gfirst[:, :], gend[:, :], ng[:, :], ALU.subtract).then_inc(s_v, 1)
                v.wait_ge(s_v, base + 7)
                nc.vector.scalar_tensor_tensor(out=shift[:, :], in0=gfirst[:, :], scalar=float(-EG), in1=first[:, 0:NB],
                                               op0=ALU.mult, op1=ALU.add).then_inc(s_v, 1)
                v.wait_ge(s_v, base + 8)
                nc.vector.tensor_tensor(ge[:, :, :], gid[:, :].unsqueeze(2).broadcast_to([P, GC, NB]),
                                        gfirst[:, :].unsqueeze(1).broadcast_to([P, GC, NB]), ALU.is_ge).then_inc(s_v, 1)
                v.wait_ge(s_v, base + 9)
                nc.vector.tensor_reduce(gblk[:, :], ge[:, :, :], AX.X, ALU.add).then_inc(s_v, 1)
                nc.vector.tensor_tensor(cnt[:, 1:NB], shift[:, 1:NB], shift[:, 0:NB - 1], ALU.subtract).then_inc(s_v, 1)
                nc.vector.tensor_copy(cnt[:, 0:1], shift[:, 0:1]).then_inc(s_v, 1)
                v.wait_ge(s_v, base + 12)
                nc.vector.tensor_tensor(ge[:, :, :], ge[:, :, :], cnt[:, :].unsqueeze(1).broadcast_to([P, GC, NB]), ALU.mult).then_inc(s_v, 1)
                nc.vector.tensor_scalar(gtab[:, 0, :], gblk[:, :], -1.0, None, ALU.add).then_inc(s_v, 1)
                v.wait_ge(s_v, base + 14)
                nc.vector.tensor_reduce(goff[:, :], ge[:, :, :], AX.X, ALU.add).then_inc(s_v, 1)
                v.wait_ge(s_v, base + 15)
                nc.vector.scalar_tensor_tensor(out=goff[:, :], in0=gid[:, :], scalar=float(EG), in1=goff[:, :],
                                               op0=ALU.mult, op1=ALU.add).then_inc(s_v, 1)
                v.wait_ge(s_v, base + 16)
                nc.vector.tensor_scalar(gtab[:, 1, :], goff[:, :], float(E), None, ALU.min).then_inc(s_gt, 1)
                v.wait_ge(s_tab, 48)
                nc.vector.tensor_scalar(C.gbase[:, :], C.gblkb[:, :], float(P), None, ALU.mult).then_inc(s_v, 1)
                nc.vector.tensor_copy(C.identb[:, :], C.ident[:, :]).then_inc(s_v, 1)

            @block.tensor
            def _(pe):
                pe.wait_ge(s_v, 2)
                pe.wait_ge(s_cnt, 1)
                nc.tensor.matmul(pt[:, 0:NB + 1], onesq[:, :], below[:, :], start=True, stop=True).then_inc(s_tot, 1)


def stage_encode(nc, C, A):
    with ExitStack() as ctx:
        sb, ps, sem = alloc(nc, ctx, "encode_")
        w1 = sb("w1", [P, 2 * KC, F]); w2 = sb("w2", [P, FC, D]); wg = sb("wg", [P, KC, D + 2 * H])
        wgr = sb("wgr", [P, KC, D]); alr = sb("alr", [P, KC, 2 * H])
        embT = sb("embT", [P, KC, NC]); b1 = sb("b1", [1, F]); lab_w = sb("lab_w", [NC, F])
        gcol = sb("gcol", [P, FC]); bcol = sb("bcol", [P, FC]); b2 = sb("b2", [P, KC]); ones1 = sb("ones1", [1, P])
        st = sb("st", [P, NB * 6]); mv = sb("mv", [P, NB * 2]); rstd = sb("rstd", [P, NB])
        xn = [sb(f"xn{k}", [P, D]) for k in range(2)]
        oh = [sb(f"ohl{k}", [P, NC]) for k in range(2)]
        xT = [sb(f"xT{k}", [P, KC * P]) for k in range(2)]
        ohT = [sb(f"ohlT{k}", [NC, P]) for k in range(2)]
        st2 = sb("st2", [P, 2, 6]); mv2 = sb("mv2", [P, 2]); sd2 = sb("sd2", [P, 1]); rs2 = sb("rs2", [P, 1])
        z = sb("z", [P, F]); zT = sb("zT", [P, FC, P]); hT = sb("hT", [P, KC, P])
        row = [sb(f"row{k}", [P, D + H]) for k in range(2)]
        p_x = ps("p_x", [P, 512]); p_u = ps("p_u", [P, 2, 512]); p_z = ps("p_z", [P, 2, 512])
        p_h = ps("p_h", [P, 512]); p_f = ps("p_f", [P, 512])
        s_w = sem("s_w"); s_st = sem("s_st"); s_var = sem("s_var"); s_std = sem("s_std"); s_one = sem("s_one")
        s_lw = sem("s_lw"); s_lwc = sem("s_lwc"); s_wa = sem("s_wa"); s_wac = sem("s_wac")
        s_xn = sem("s_xn"); s_xT = sem("s_xT"); s_xTc = sem("s_xTc"); s_u = sem("s_u"); s_bn = sem("s_bn")
        s_sd = sem("s_sd"); s_rs = sem("s_rs"); s_z = sem("s_z"); s_zT = sem("s_zT"); s_zTc = sem("s_zTc")
        s_h = sem("s_h"); s_hc = sem("s_hc"); s_f = sem("s_f"); s_row = sem("s_row"); s_gate = sem("s_gate")
        s_rowd = [sem(f"s_rowd{k}") for k in range(2)]
        NW = 10

        with nc.Block() as block:
            @block.sync
            def _(sp):
                sp.dma_start(w1[:, :, :], A["le_W1T"].rearrange("(c p) f -> p c f", p=P)).then_inc(s_w, 16)
                sp.dma_start(embT[:, :, :], A["embT"].rearrange("(c p) f -> p c f", p=P)).then_inc(s_w, 16)
                sp.dma_start(b1[:, :], A["le_b1"].rearrange("(a f) -> a f", a=1)).then_inc(s_w, 16)
                sp.dma_start(w2[:, :, :], A["le_W2T"].rearrange("(c p) f -> p c f", p=P)).then_inc(s_w, 16)
                sp.dma_start(wg[:, :, 0:D], A["W1T"].rearrange("(c p) f -> p c f", p=P)).then_inc(s_w, 16)
                sp.dma_start(wgr[:, :, :], A["W1"].rearrange("(c p) f -> p c f", p=P)).then_inc(s_w, 16)
                sp.dma_start(alr[:, :, :], A["alr1"].rearrange("(c p) f -> p c f", p=P)).then_inc(s_w, 16)
                sp.dma_start(gcol[:, :], A["ln_g"].rearrange("(c p) -> p c", p=P), allow_slow_non_contiguous=True).then_inc(s_w, 16)
                sp.dma_start(bcol[:, :], A["ln_b"].rearrange("(c p) -> p c", p=P), allow_slow_non_contiguous=True).then_inc(s_w, 16)
                sp.dma_start(b2[:, :], A["le_b2"].rearrange("(c p) -> p c", p=P), allow_slow_non_contiguous=True).then_inc(s_w, 16)

                def front(b, k):
                    pass

                def back(b, k):
                    sp.wait_ge(s_row, b * 2 + 2)
                    sp.dma_start(C.tab1[ds(b * P, P), 0:D + H], row[k][:, :]).then_inc(s_rowd[k], 16)

                skewed(sp, NB, 2, front, back)
                sp.wait_ge(s_rowd[0], 16 * ((NB + 1) // 2))
                sp.wait_ge(s_rowd[1], 16 * (NB // 2))

            @block.vector
            def _(v):
                nc.vector.memset(ones1[:, :], 1.0).then_inc(s_one, 1)
                ln_stats(nc, v, None, C.X, mv, st, rstd, s_st, s_var, s_std, 1e-5)
                v.wait_ge(s_wa, 1)
                nc.vector.tensor_copy(wg[:, :, D:D + 2 * H], p_h[:, 0:KC * 2 * H].rearrange("p (c h) -> p c h", c=KC)).then_inc(s_wac, 1)

                def front(b, k):
                    nc.vector.tensor_scalar(xn[k][:, :], C.X[:, ds(b * D, D)], mv[:, ds(b * 2, 1)], rstd[:, ds(b, 1)],
                                            ALU.subtract, ALU.mult).then_inc(s_xn, 1)
                    nc.vector.tensor_scalar(oh[k][:, :], C.iota[:, 0:NC], C.lab[:, ds(b, 1)], None, ALU.is_equal).then_inc(s_xn, 1)

                def back(b, k):
                    v.wait_ge(s_u, b * 2 + 1)
                    nc.vector.bn_stats(st2[:, 0, :], p_u[:, 0, :]).then_inc(s_bn, 1)
                    v.wait_ge(s_u, b * 2 + 2)
                    nc.vector.bn_stats(st2[:, 1, :], p_u[:, 1, :]).then_inc(s_bn, 1)
                    hold(v, s_bn, b * 4 + 2, s_gate)
                    nc.vector.bn_aggr(mv2[:, :], st2[:, :, :].rearrange("p a s -> p (a s)")).then_inc(s_bn, 1)
                    v.wait_ge(s_bn, b * 4 + 3)
                    nc.vector.tensor_scalar(sd2[:, :], mv2[:, 1:2], 1e-5, None, ALU.add).then_inc(s_bn, 1)
                    v.wait_ge(s_sd, b + 1)
                    nc.vector.reciprocal(rs2[:, :], sd2[:, :]).then_inc(s_rs, 1)
                    v.wait_ge(s_rs, b + 1)
                    for c in range(2):
                        nc.vector.tensor_scalar(z[:, c * 512:c * 512 + 512], p_u[:, c, :], mv2[:, 0:1], rs2[:, 0:1],
                                                ALU.subtract, ALU.mult).then_inc(s_z, 1)
                    v.wait_ge(s_f, b + 1)
                    if not isinstance(b, int) or b >= 2:
                        v.wait_ge(s_rowd[k], (b - k) * 8)
                    nc.vector.tensor_copy(row[k][:, :], p_f[:, 0:D + H]).then_inc(s_row, 1)
                    nc.vector.tensor_copy(C.ler[:, ds(b * 2 * H, 2 * H)], p_f[:, D:D + 2 * H]).then_inc(s_row, 1)

                skewed(v, NB, 2, front, back, peel=2)

            @block.scalar
            def _(act):
                ln_sqrt(nc, act, rstd, s_var, s_std)
                act.wait_ge(s_lw, 2)
                nc.scalar.copy(lab_w[:, :], p_u[0:NC, :, :].rearrange("p a f -> p (a f)")).then_inc(s_lwc, 1)

                def front(b, k):
                    act.wait_ge(s_xT, b + 1)
                    nc.scalar.copy(xT[k][:, :], p_x[:, 0:KC * P]).then_inc(s_xTc, 1)
                    nc.scalar.copy(ohT[k][:, :], p_x[0:NC, KC * P:KC * P + P]).then_inc(s_xTc, 1)

                def back(b, k):
                    act.wait_ge(s_bn, b * 4 + 4)
                    nc.scalar.activation(sd2[:, :], sd2[:, :], ACT.Sqrt).then_inc(s_sd, 1)
                    for c in range(FC):
                        if c % 4 == 0:
                            act.wait_ge(s_zT, b * 2 + c // 4 + 1)
                        nc.scalar.activation(zT[:, c, :], p_z[:, c // 4, (c % 4) * P:(c % 4) * P + P], ACT.Relu,
                                             bias=bcol[:, c:c + 1], scale=gcol[:, c:c + 1]).then_inc(s_zTc, 1)
                    act.wait_ge(s_h, b + 1)
                    for c in range(KC):
                        nc.scalar.activation(hT[:, c, :], p_h[:, c * P:c * P + P], ACT.Identity, bias=b2[:, c:c + 1]).then_inc(s_hc, 1)

                skewed(act, NB, 2, front, back)

            @block.tensor
            def _(pe):
                pe.wait_ge(s_w, 16 * NW)
                pe.wait_ge(s_one, 1)
                for c in range(2):
                    for kc in range(KC):
                        nc.tensor.matmul(p_u[0:NC, c, :], embT[:, kc, :], w1[:, KC + kc, c * 512:c * 512 + 512], start=(kc == 0), stop=False)
                    nc.tensor.matmul(p_u[0:NC, c, :], ones1[0:1, 0:NC], b1[0:1, c * 512:c * 512 + 512], start=False, stop=True).then_inc(s_lw, 1)
                project_attention_vectors(nc, p_h, wgr, alr, s_wa)
                pe.wait_ge(s_lwc, 1)
                pe.wait_ge(s_wac, 1)

                def front(b, k):
                    pe.wait_ge(s_xn, b * 2 + 2)
                    if not isinstance(b, int) or b > 0:
                        pe.wait_ge(s_xTc, b * 2)
                    for c in range(KC):
                        nc.tensor.transpose(p_x[:, c * P:c * P + P], xn[k][:, c * P:c * P + P], C.ident[:, :])
                    nc.tensor.transpose(p_x[0:NC, KC * P:KC * P + P], oh[k][:, :], C.ident[:, :]).then_inc(s_xT, 1)
                    pe.wait_ge(s_xTc, b * 2 + 2)
                    for c in range(2):
                        if not isinstance(b, int) or b > 0:
                            pe.wait_ge(s_z, (b - 1) * 2 + c + 1)
                        for kc in range(KC):
                            nc.tensor.matmul(p_u[:, c, :], xT[k][:, kc * P:kc * P + P], w1[:, kc, c * 512:c * 512 + 512], start=(kc == 0), stop=False)
                        nc.tensor.matmul(p_u[:, c, :], ohT[k][:, :], lab_w[:, c * 512:c * 512 + 512], start=False, stop=True).then_inc(s_u, 1)

                def back(b, k):
                    for c in range(FC):
                        if c % 4 == 0:
                            pe.wait_ge(s_z, b * 2 + c // 4 + 1)
                        t = nc.tensor.transpose(p_z[:, c // 4, (c % 4) * P:(c % 4) * P + P], z[:, c * P:c * P + P], C.ident[:, :])
                        if c % 4 == 3:
                            t.then_inc(s_zT, 1)
                    pe.wait_ge(s_zTc, b * FC + FC)
                    for m in range(KC):
                        for c in range(FC):
                            t = nc.tensor.matmul(p_h[:, m * P:m * P + P], w2[:, c, m * P:m * P + P], zT[:, c, :], start=(c == 0), stop=(c == FC - 1))
                    t.then_inc(s_h, 1)
                    pe.wait_ge(s_hc, b * KC + KC)
                    if not isinstance(b, int) or b > 0:
                        pe.wait_ge(s_row, b * 2)
                    for kc in range(KC):
                        t = nc.tensor.matmul(p_f[:, 0:D + 2 * H], hT[:, kc, :], wg[:, kc, :], start=(kc == 0), stop=(kc == KC - 1))
                    t.then_inc(s_f, 1)

                skewed(pe, NB, 2, front, back)


def project_attention_vectors(nc, p, w_rows, alr, s_done):
    for m in range(KC):
        for kc in range(KC):
            t = nc.tensor.matmul(p[:, m * 2 * H:(m + 1) * 2 * H], w_rows[:, kc, m * P:m * P + P], alr[:, kc, :], start=(kc == 0), stop=(kc == KC - 1))
    t.then_inc(s_done, 1)


def when_near(C, eng, want):
    return eng.If(eng.value_load(C.near[0:1, 0:1], min_val=0, max_val=1) == want)


def stage_scores(nc, C, table, layer):
    with ExitStack() as ctx:
        sb, ps, sem = alloc(nc, ctx, f"scores{layer}_")
        ext = sb("ext", [P, 2 * H]); top = sb("top", [2 * H, 1]); diag = sb("diag", [2 * H, 2 * H]); ones = sb("ones", [2 * H, P])
        lim = sb("lim", [P, 2 * H]); span = sb("span", [P, H]); fits = sb("fits", [P, 1])
        dd = sb("dd", [P, NB, H]); y = sb("y", [P, NB, H]); lk = sb("lk", [P, NB, H])
        ac = sb("ac", [P, NB, 2 * H]); bg = sb("bg", [P, NB, 2 * H])
        p_t = ps("p_t", [P, 512]); p_b = ps("p_b", [P, 512])
        s_v = sem("s_v"); s_t = sem("s_t"); s_bc = sem("s_bc"); s_arg = sem("s_arg"); s_ac = sem("s_ac"); s_bg = sem("s_bg"); s_tab = sem("s_tab")
        ler = C.ler[:, :].rearrange("p (b t) -> p b t", t=2 * H)
        bg3 = C.bg3[:, :].rearrange("p (b s t) -> p b s t", s=3, t=2 * H)

        with nc.Block() as block:
            @block.sync
            def _(sp):
                sp.wait_ge(s_ac, 2)
                sp.dma_start(table[:, D + H:TW].rearrange("(b p) t -> p b t", p=P), ac[:, :, :], allow_slow_non_contiguous=True).then_inc(s_tab, 16)
                sp.wait_ge(s_tab, 16)

            @block.vector
            def _(v):
                nc.vector.memset(ones[:, :], 1.0).then_inc(s_v, 1)
                nc.vector.tensor_copy(C.em[:, :].rearrange("p (b t) -> p b t", t=2 * H)[:, :, 0:H], ler[:, :, H:2 * H]).then_inc(s_v, 1)
                by_head = C.ler[:, :].rearrange("p (b t) -> p t b", t=2 * H)[:, 0:H, :]
                nc.vector.tensor_reduce(ext[:, 0:H], by_head, AX.X, ALU.max).then_inc(s_v, 1)
                nc.vector.tensor_reduce(ext[:, H:2 * H], by_head, AX.X, ALU.min).then_inc(s_v, 1)
                v.wait_ge(s_v, 4)
                nc.vector.tensor_scalar(ext[:, H:2 * H], ext[:, H:2 * H], -1.0, None, ALU.mult).then_inc(s_v, 1)
                v.wait_ge(s_t, 1)
                nc.vector.tensor_reduce(top[:, :], p_t[0:2 * H, 0:P], AX.X, ALU.max).then_inc(s_v, 1)
                v.wait_ge(s_v, 6)
                nc.vector.tensor_scalar(diag[:, :], C.ident[0:2 * H, 0:2 * H], top[:, 0:1], None, ALU.mult).then_inc(s_v, 1)
                v.wait_ge(s_bc, 1)
                nc.vector.tensor_copy(lim[:, :], p_b[:, 0:2 * H]).then_inc(s_v, 1)
                v.wait_ge(s_v, 8)
                most = lim[:, 0:H].unsqueeze(1).broadcast_to([P, NB, H])
                nc.vector.tensor_tensor(dd[:, :, :], ler[:, :, 0:H], most, ALU.subtract).then_inc(s_arg, 1)
                nc.vector.tensor_tensor(y[:, :, :], ler[:, :, H:2 * H], most, ALU.add).then_inc(s_v, 1)
                nc.vector.tensor_tensor(span[:, :], lim[:, 0:H], lim[:, H:2 * H], ALU.add).then_inc(s_v, 1)
                v.wait_ge(s_v, 10)
                nc.vector.scalar_tensor_tensor(out=lk[:, :, :], in0=y[:, :, :], scalar=SLOPE, in1=y[:, :, :], op0=ALU.mult, op1=ALU.max).then_inc(s_v, 1)
                nc.vector.tensor_scalar(span[:, :], span[:, :], SPREAD, None, ALU.is_le).then_inc(s_v, 1)
                v.wait_ge(s_v, 12)
                nc.vector.tensor_tensor(bg[:, :, 0:H], y[:, :, :], lk[:, :, :], ALU.subtract).then_inc(s_arg, 1)
                nc.vector.scalar_tensor_tensor(out=bg[:, :, H:2 * H], in0=y[:, :, :], scalar=SLOPE, in1=lk[:, :, :], op0=ALU.mult, op1=ALU.subtract).then_inc(s_arg, 1)
                nc.vector.tensor_reduce(fits[:, :], span[:, :], AX.X, ALU.min).then_inc(s_v, 1)
                v.wait_ge(s_v, 13)
                nc.vector.tensor_copy(C.near[:, :], fits[:, :]).then_inc(s_v, 1)
                v.wait_ge(s_bg, 1)
                for s in range(3):
                    nc.vector.tensor_copy(bg3[:, :, s, :], bg[:, :, :]).then_inc(s_v, 1)
                    v.wait_ge(s_v, 15 + 2 * s)
                    if s < 2:
                        nc.vector.tensor_tensor(bg[:, :, :], bg[:, :, :], bg3[:, :, s, :], ALU.subtract).then_inc(s_v, 1)
                        v.wait_ge(s_v, 16 + 2 * s)

            @block.scalar
            def _(act):
                act.wait_ge(s_arg, 1)
                nc.scalar.activation(ac[:, :, 0:H], dd[:, :, :], ACT.Exp).then_inc(s_ac, 1)
                nc.scalar.activation(ac[:, :, H:2 * H], dd[:, :, :], ACT.Exp, scale=SLOPE).then_inc(s_ac, 1)
                act.wait_ge(s_arg, 3)
                nc.scalar.activation(bg[:, :, :], bg[:, :, :], ACT.Exp).then_inc(s_bg, 1)

            @block.tensor
            def _(pe):
                pe.wait_ge(s_v, 5)
                nc.tensor.transpose(p_t[0:2 * H, 0:P], ext[:, :], C.ident[:, :]).then_inc(s_t, 1)
                pe.wait_ge(s_v, 7)
                nc.tensor.matmul(p_b[:, 0:2 * H], ones[:, :], diag[:, :], start=True, stop=True).then_inc(s_bc, 1)


def stage_attend_near(nc, C, table, layer):
    with ExitStack() as ctx:
        sb, ps, sem = alloc(nc, ctx, f"near{layer}_")
        ix = [sb(f"ix{k}", [P, ET, 2], I32) for k in range(UN)]
        G = [sb(f"G{k}", [P, ET, TW]) for k in range(UN)]
        dl = [sb(f"dl{k}", [P, ET]) for k in range(2)]
        ohb = [sb(f"ohb{k}", [P, ET, P], BF16) for k in range(2)]
        oh = [sb(f"oh{k}", [P, ET, P]) for k in range(2)]
        ohT = [sb(f"ohT{k}", [P, EG], BF16) for k in range(2)]
        w2 = sb("w2", [P, ET, 2 * H])
        Gw = [sb(f"Gw{k}", [P, ET, H, HW]) for k in range(2)]
        p_oT = [ps(f"p_oT{k}", [P, 1024], BF16) for k in range(2)]; p_ex = [ps(f"p_ex{k}", [P, 512]) for k in range(2)]
        p_sg = [ps(f"p_sg{k}", [P, H * HW]) for k in range(2)]
        s_ix = [sem(f"s_ix{k}") for k in range(UN)]; s_g = [sem(f"s_g{k}") for k in range(UN)]
        s_go = sem("s_go"); s_init = sem("s_init"); s_dl = sem("s_dl"); s_ohb = sem("s_ohb"); s_oh = sem("s_oh"); s_T = sem("s_T"); s_cp = sem("s_cp")
        s_ex = sem("s_ex"); s_w = sem("s_w"); s_p = sem("s_p"); s_use = sem("s_use"); s_sg = sem("s_sg"); s_acc = sem("s_acc")
        HD4 = H * HW

        def block_of(eng, g):
            return eng.value_load(C.gblk[0:1, ds(g, 1)], min_val=0, max_val=NB - 1)

        def after_first(eng, sem, g, value):
            if not isinstance(g, int) or g > 0:
                eng.wait_ge(sem, value)

        with nc.Block() as block:
            @block.sync
            def _(sp):
                with when_near(C, sp, 1):
                    def load(g, k):
                        off = sp.value_load(C.gofs[0:1, ds(g, 1)], min_val=0, max_val=E)
                        sp.dma_start(ix[k][:, :, :].rearrange("p c t -> p (c t)"),
                                     C.edges[ds(off, EG), :].rearrange("(p c) t -> p (c t)", c=ET)).then_inc(s_ix[k], 16)
                    for k in range(UN):
                        load(k, k)
                    with sp.Fori(1, NG // UN) as i:
                        for k in range(UN):
                            sp.wait_ge(s_use, i * UN + k - UN + 1)
                            load(i * UN + k, k)

            @block.gpsimd
            def _(gp):
                with when_near(C, gp, 1):
                    with gp.Fori(0, NG // UN) as i:
                        for k in range(UN):
                            hold(gp, s_ix[k], i * 16 + 16, s_go)
                            for j in range(ET):
                                gp.indirect_dma_start(out=G[k][:, j, :], out_offset=None, in_=table[:, :],
                                                      in_offset=bass.IndirectOffsetOnAxis(ap=ix[k][:, j, 0:1], axis=0)).then_inc(s_g[k], 16)

            @block.vector
            def _(v):
                with when_near(C, v, 1):
                    nc.vector.memset(C.acc[:, :], 0.0).then_inc(s_init, 1)
                    v.wait_ge(s_init, 1)

                    def one_hot(g, k):
                        v.wait_ge(s_ix[k], (g - k) * 4 + 16)
                        nc.vector.tensor_scalar(dl[k % 2][:, :], ix[k][:, :, 1], C.gbase[:, ds(g, 1)], None, ALU.subtract).then_inc(s_dl, 1)
                        v.wait_ge(s_dl, g + 1)
                        after_first(v, s_oh, g, g)
                        nc.vector.tensor_tensor(ohb[k % 2][:, :, :], C.iota[:, :].unsqueeze(1).broadcast_to([P, ET, P]),
                                                dl[k % 2][:, :].unsqueeze(2).broadcast_to([P, ET, P]), ALU.is_equal).then_inc(s_ohb, 1)

                    def accumulate(g, k, blk):
                        a = C.acc[:, ds(blk * HD4, HD4)]
                        v.wait_ge(s_sg, g + 1)
                        nc.vector.tensor_tensor(a, a, p_sg[k % 2][:, :], ALU.add).then_inc(s_acc, 1)
                        v.wait_ge(s_acc, g + 1)

                    def step(g, k, last=False):
                        v.wait_ge(s_g[k], (g - k) * 16 + 64)
                        v.wait_ge(s_ex, g + 1)
                        nc.vector.tensor_tensor(w2[:, :, :], G[k][:, :, D + H:TW], p_ex[k % 2][:, 0:ET * 2 * H].rearrange("p (c t) -> p c t", c=ET), ALU.mult).then_inc(s_w, 1)
                        if not last:
                            one_hot(g + 1, (k + 1) % UN)
                        v.wait_ge(s_w, g + 1)
                        nc.vector.tensor_tensor(Gw[k % 2][:, :, :, HD], w2[:, :, 0:H], w2[:, :, H:2 * H], ALU.max).then_inc(s_p, 1)
                        if not isinstance(g, int) or g > 0:
                            accumulate(g - 1, (k - 1) % UN, block_of(v, g - 1))
                        v.wait_ge(s_p, g + 1)
                        nc.vector.tensor_tensor(Gw[k % 2][:, :, :, 0:HD], G[k][:, :, 0:D].rearrange("p c (h d) -> p c h d", h=H),
                                                Gw[k % 2][:, :, :, HD:HW].broadcast_to([P, ET, H, HD]), ALU.mult).then_inc(s_use, 1)

                    one_hot(0, 0)
                    for g in range(UN):
                        step(g, g)
                    with v.Fori(1, NG // UN - 1) as i:
                        for k in range(UN):
                            step(i * UN + k, k)
                    for g in range(NG - UN, NG):
                        step(g, g % UN, last=g == NG - 1)
                    accumulate(NG - 1, (NG - 1) % UN, block_of(v, NG - 1))

            @block.scalar
            def _(act):
                with when_near(C, act, 1):
                    def step(g, k):
                        act.wait_ge(s_T, g + 1)
                        nc.scalar.copy(ohT[k % 2][:, :], p_oT[k % 2][:, 0:EG]).then_inc(s_cp, 1)
                        if not isinstance(g, int) or g >= 2:
                            act.wait_ge(s_sg, g - 1)
                        nc.scalar.copy(oh[k % 2][:, :, :], ohb[k % 2][:, :, :]).then_inc(s_oh, 1)

                    for g in range(UN):
                        step(g, g)
                    with act.Fori(1, NG // UN) as i:
                        for k in range(UN):
                            step(i * UN + k, k)

            @block.tensor
            def _(pe):
                with when_near(C, pe, 1):
                    def transposes(g, k):
                        pe.wait_ge(s_ohb, g + 1)
                        for j in range(ET):
                            t = nc.tensor.transpose(p_oT[k % 2][:, j * P:j * P + P], ohb[k % 2][:, j, :], C.identb[:, :])
                        t.then_inc(s_T, 1)

                    def expand(g, k, blk):
                        pe.wait_ge(s_cp, g + 1)
                        if not isinstance(g, int) or g >= 2:
                            pe.wait_ge(s_w, g - 1)
                        for j in range(ET):
                            for s in range(3):
                                t = nc.tensor.matmul(p_ex[k % 2][:, j * 2 * H:(j + 1) * 2 * H], ohT[k % 2][:, j * P:j * P + P],
                                                     C.bg3[:, ds(blk * 6 * H + s * 2 * H, 2 * H)], start=(s == 0), stop=(s == 2))
                        t.then_inc(s_ex, 1)

                    def sums(g, k):
                        pe.wait_ge(s_use, g + 1)
                        if not isinstance(g, int) or g >= 2:
                            pe.wait_ge(s_acc, g - 1)
                        for j in range(ET):
                            t = nc.tensor.matmul(p_sg[k % 2][:, :], oh[k % 2][:, j, :], Gw[k % 2][:, j, :, :].rearrange("p h d -> p (h d)"),
                                                 start=(j == 0), stop=(j == ET - 1))
                        t.then_inc(s_sg, 1)

                    def step(g, k, last=False):
                        if not last:
                            transposes(g + 1, (k + 1) % UN)
                            expand(g + 1, (k + 1) % UN, block_of(pe, g + 1))
                        pe.wait_ge(s_oh, g + 1)
                        sums(g, k)

                    transposes(0, 0)
                    expand(0, 0, block_of(pe, 0))
                    for g in range(UN):
                        step(g, g)
                    with pe.Fori(1, NG // UN - 1) as i:
                        for k in range(UN):
                            step(i * UN + k, k)
                    for g in range(NG - UN, NG):
                        step(g, g % UN, last=g == NG - 1)


def stage_attend(nc, C, table, layer):
    with ExitStack() as ctx:
        sb, ps, sem = alloc(nc, ctx, f"attend{layer}_")
        ix = [sb(f"ix{k}", [P, ET, 2], I32) for k in range(UN)]
        G = [sb(f"G{k}", [P, ET, TW]) for k in range(UN)]
        dl = [sb(f"dl{k}", [P, ET]) for k in range(2)]
        oh = [sb(f"oh{k}", [P, ET, P]) for k in range(2)]
        ohT = [sb(f"ohT{k}", [P, EG]) for k in range(2)]
        pen = [sb(f"pen{k}", [P, EG], BF16) for k in range(2)]
        elT = [sb(f"elT{k}", [H, EG]) for k in range(2)]
        selh = sb("selh", [H, H, P])
        mx = sb("mx", [P, NB * H])
        gm = [sb(f"gm{k}", [P, H]) for k in range(2)]
        e1 = sb("e1", [P, NB * H]); mn = sb("mn", [P, NB * H]); dm = sb("dm", [P, H])
        resc = [sb(f"resc{k}", [P, H]) for k in range(2)]
        sc = sb("sc", [P, ET, H]); sl = sb("sl", [P, ET, H])
        Gw = [sb(f"Gw{k}", [P, ET, H, HW]) for k in range(2)]
        p_oT = ps("p_oT", [P, 512]); p_eT = ps("p_eT", [P, 512]); p_bc = ps("p_bc", [P, 2, 512])
        p_ex = ps("p_ex", [P, ET, 2 * H]); p_sg = [ps(f"p_sg{k}", [P, H * HW]) for k in range(2)]
        s_ix = [sem(f"s_ix{k}") for k in range(UN)]
        s_g = [sem(f"s_g{k}") for k in range(UN)]
        s_use = sem("s_use"); s_init = sem("s_init"); s_sel = sem("s_sel"); s_go = sem("s_go")
        s_dl = sem("s_dl"); s_oh = sem("s_oh"); s_T = sem("s_T"); s_cp = sem("s_cp"); s_bc = sem("s_bc")
        s_red = sem("s_red"); s_m = sem("s_m"); s_em = sem("s_em"); s_dm = sem("s_dm"); s_rc = sem("s_rc")
        s_ex = sem("s_ex"); s_sc = sem("s_sc"); s_sl = sem("s_sl"); s_p = sem("s_p"); s_pm = sem("s_pm"); s_gw = sem("s_gw")
        s_sg = sem("s_sg"); s_acc = sem("s_acc")
        HD4 = H * HW
        em3 = C.em[:, :].rearrange("p (b t) -> p b t", t=2 * H)

        with nc.Block() as block:
            @block.sync
            def _(sp):
                with when_near(C, sp, 0):
                    def load(g, k, i):
                        off = sp.value_load(C.gofs[0:1, ds(g, 1)], min_val=0, max_val=E)
                        sp.dma_start(ix[k][:, :, :].rearrange("p c t -> p (c t)"),
                                     C.edges[ds(off, EG), :].rearrange("(p c) t -> p (c t)", c=ET)).then_inc(s_ix[k], 16)
                    for k in range(UN):
                        load(k, k, 0)
                    with sp.Fori(1, NG // UN) as i:
                        for k in range(UN):
                            g = i * UN + k
                            sp.wait_ge(s_use, g - UN + 1)
                            load(g, k, i)

            @block.gpsimd
            def _(gp):
                with when_near(C, gp, 0):
                    nc.gpsimd.memset(selh[:, :, :], 0.0).then_inc(s_sel, 1)
                    gp.wait_ge(s_sel, 1)
                    nc.gpsimd.affine_select(out=selh[:, :, :], in_=selh[:, :, :], compare_op=ALU.not_equal, fill=1.0, base=0,
                                            pattern=[[-1, H], [0, P]], channel_multiplier=1).then_inc(s_sel, 1)
                    with gp.Fori(0, NG // UN) as i:
                        for k in range(UN):
                            hold(gp, s_ix[k], i * 16 + 16, s_go)
                            for j in range(ET):
                                gp.indirect_dma_start(out=G[k][:, j, :], out_offset=None, in_=table[:, :],
                                                      in_offset=bass.IndirectOffsetOnAxis(ap=ix[k][:, j, 0:1], axis=0)).then_inc(s_g[k], 16)

            @block.vector
            def _(v):
                with when_near(C, v, 0):
                    nc.vector.memset(mx[:, :], -BIG).then_inc(s_init, 1)
                    nc.vector.memset(C.acc[:, :], 0.0).then_inc(s_init, 1)
                    v.wait_ge(s_init, 2)
                    mx3 = mx[:, :].rearrange("p (b h) -> p b h", h=H)
                    e13 = e1[:, :].rearrange("p (b h) -> p b h", h=H)
                    nc.vector.tensor_tensor(e13, mx3, em3[:, :, 0:H], ALU.add).then_inc(s_init, 1)
                    v.wait_ge(s_init, 3)
                    nc.vector.scalar_tensor_tensor(out=em3[:, :, H:2 * H], in0=e13, scalar=SLOPE, in1=e13, op0=ALU.mult, op1=ALU.max).then_inc(s_init, 1)
                    v.wait_ge(s_init, 4)
                    v.sem_inc(s_red, 2)

                    def i_of(g, k):
                        return (g - k) * 4

                    def one_hot(g, k):
                        v.wait_ge(s_ix[k], i_of(g, k) + 16)
                        nc.vector.tensor_scalar(dl[k % 2][:, :], ix[k][:, :, 1], C.gbase[:, ds(g, 1)], None, ALU.subtract).then_inc(s_dl, 1)
                        v.wait_ge(s_dl, g + 1)
                        nc.vector.tensor_tensor(oh[k % 2][:, :, :], C.iota[:, :].unsqueeze(1).broadcast_to([P, ET, P]),
                                                dl[k % 2][:, :].unsqueeze(2).broadcast_to([P, ET, P]), ALU.is_equal).then_inc(s_oh, 1)

                    def group_max(g, k):
                        for h in range(H):
                            v.wait_ge(s_bc, g * H + h + 1)
                            nc.vector.tensor_reduce(gm[k % 2][:, h:h + 1], p_bc[:, h % 2, :], AX.X, ALU.max).then_inc(s_red, 1)

                    def new_max(g, k, blk):
                        mxb = mx[:, ds(blk * H, H)]
                        erb = C.em[:, ds(blk * 2 * H, H)]
                        mb = C.em[:, ds(blk * 2 * H + H, H)]
                        v.wait_ge(s_red, g * H + H + 2)
                        nc.vector.tensor_tensor(mxb, mxb, gm[k % 2][:, :], ALU.max).then_inc(s_m, 1)
                        v.wait_ge(s_m, g * 4 + 1)
                        nc.vector.tensor_tensor(e1[:, 0:H], mxb, erb, ALU.add).then_inc(s_m, 1)
                        v.wait_ge(s_m, g * 4 + 2)
                        nc.vector.scalar_tensor_tensor(out=mn[:, 0:H], in0=e1[:, 0:H], scalar=SLOPE, in1=e1[:, 0:H], op0=ALU.mult, op1=ALU.max).then_inc(s_m, 1)
                        v.wait_ge(s_m, g * 4 + 3)
                        if not isinstance(g, int) or g > 0:
                            v.wait_ge(s_rc, g)
                        nc.vector.tensor_tensor(dm[:, :], mb, mn[:, 0:H], ALU.subtract).then_inc(s_m, 1)
                        v.wait_ge(s_m, g * 4 + 4)
                        nc.vector.tensor_scalar(mb, mn[:, 0:H], 1.0, None, ALU.mult).then_inc(s_em, 1)

                    def scores(g, k):
                        v.wait_ge(s_ex, g + 1)
                        nc.vector.tensor_tensor(sc[:, :, :], G[k][:, :, D:D + H], p_ex[:, :, 0:H], ALU.add).then_inc(s_sc, 1)
                        v.wait_ge(s_sc, g + 1)
                        nc.vector.scalar_tensor_tensor(out=sl[:, :, :], in0=sc[:, :, :], scalar=SLOPE, in1=sc[:, :, :], op0=ALU.mult, op1=ALU.max).then_inc(s_sl, 1)
                        v.wait_ge(s_sl, g * 2 + 1)
                        nc.vector.tensor_tensor(sl[:, :, :], sl[:, :, :], p_ex[:, :, H:2 * H], ALU.subtract).then_inc(s_sl, 1)

                    def weigh(g, k):
                        v.wait_ge(s_p, g + 1)
                        pk = Gw[k % 2][:, :, :, HD]
                        nc.vector.tensor_scalar(pk, pk, 1.0, None, ALU.min).then_inc(s_pm, 1)
                        v.wait_ge(s_pm, g + 1)
                        nc.vector.tensor_tensor(Gw[k % 2][:, :, :, 0:HD], G[k][:, :, 0:D].rearrange("p c (h d) -> p c h d", h=H),
                                                Gw[k % 2][:, :, :, HD:HW].broadcast_to([P, ET, H, HD]), ALU.mult).then_inc(s_use, 1)

                    def accumulate(g, k, blk):
                        a = C.acc[:, ds(blk * HD4, HD4)]
                        v.wait_ge(s_rc, g + 1)
                        nc.vector.tensor_tensor(a.rearrange("p (h d) -> p h d", h=H), a.rearrange("p (h d) -> p h d", h=H),
                                                resc[k % 2][:, :].unsqueeze(2).broadcast_to([P, H, HW]), ALU.mult).then_inc(s_acc, 1)
                        v.wait_ge(s_acc, g * 2 + 1)
                        v.wait_ge(s_sg, g + 1)
                        nc.vector.tensor_tensor(a, a, p_sg[k % 2][:, :], ALU.add).then_inc(s_acc, 1)

                    def block_of(g):
                        return v.value_load(C.gblk[0:1, ds(g, 1)], min_val=0, max_val=NB - 1)

                    def step(g, k, last=False):
                        new_max(g, k, block_of(g))
                        if not last:
                            one_hot(g + 1, (k + 1) % UN)
                        scores(g, k)
                        if not isinstance(g, int) or g > 0:
                            accumulate(g - 1, (k - 1) % UN, block_of(g - 1))
                        weigh(g, k)
                        if not last:
                            group_max(g + 1, (k + 1) % UN)

                    one_hot(0, 0)
                    group_max(0, 0)
                    for g in range(UN):
                        step(g, g)
                    with v.Fori(1, NG // UN - 1) as i:
                        for k in range(UN):
                            step(i * UN + k, k)
                    for g in range(NG - UN, NG):
                        step(g, g % UN, last=g == NG - 1)
                    accumulate(NG - 1, (NG - 1) % UN, block_of(NG - 1))

            @block.scalar
            def _(act):
                with when_near(C, act, 0):
                    def front(g, k):
                        act.wait_ge(s_T, g + 1)
                        nc.scalar.copy(ohT[k % 2][:, :], p_oT[:, :]).then_inc(s_cp, 1)
                        nc.scalar.copy(elT[k % 2][:, :], p_eT[0:H, :]).then_inc(s_cp, 1)
                        nc.scalar.activation(pen[k % 2][:, :], p_oT[:, :], ACT.Copy, bias=-1.0).then_inc(s_cp, 1)

                    def back(g, k):
                        act.wait_ge(s_m, g * 4 + 4)
                        nc.scalar.activation(resc[k % 2][:, :], dm[:, :], ACT.Exp).then_inc(s_rc, 1)
                        act.wait_ge(s_sl, g * 2 + 2)
                        nc.scalar.activation(Gw[k % 2][:, :, :, HD], sl[:, :, :], ACT.Exp).then_inc(s_p, 1)

                    front(0, 0)
                    with act.Fori(0, NG // UN - 1) as i:
                        for k in range(UN):
                            g = i * UN + k
                            back(g, k)
                            front(g + 1, (k + 1) % UN)
                    for g in range(NG - UN, NG):
                        back(g, g % UN)
                        if g + 1 < NG:
                            front(g + 1, (g + 1) % UN)

            @block.tensor
            def _(pe):
                with when_near(C, pe, 0):
                    pe.wait_ge(s_sel, 2)

                    def transposes(g, k):
                        pe.wait_ge(s_oh, g + 1)
                        if not isinstance(g, int) or g > 0:
                            pe.wait_ge(s_cp, g * 3)
                        for j in range(ET):
                            nc.tensor.transpose(p_oT[:, j * P:j * P + P], oh[k % 2][:, j, :], C.ident[:, :])
                        pe.wait_ge(s_g[k], (g - k) * 16 + 64)
                        for j in range(ET):
                            t = nc.tensor.transpose(p_eT[0:H, j * P:j * P + P], G[k][:, j, D:D + H], C.ident[:, :])
                        t.then_inc(s_T, 1)

                    def spread(g, k, h):
                        if h == 0:
                            pe.wait_ge(s_cp, g * 3 + 3)
                        pe.wait_ge(s_red, g * H + h + 1)
                        nc.tensor.matmul(p_bc[:, h % 2, :], C.bigi[:, :], pen[k % 2][:, :], start=True, stop=False)
                        nc.tensor.matmul(p_bc[:, h % 2, :], selh[:, h, :], elT[k % 2][:, :], start=False, stop=True).then_inc(s_bc, 1)

                    def expand(g, k, blk):
                        pe.wait_ge(s_em, g + 1)
                        for j in range(ET):
                            t = nc.tensor.matmul(p_ex[:, j, :], ohT[k % 2][:, j * P:j * P + P], C.em[:, ds(blk * 2 * H, 2 * H)], start=True, stop=True)
                        t.then_inc(s_ex, 1)

                    def sums(g, k):
                        pe.wait_ge(s_use, g + 1)
                        for j in range(ET):
                            t = nc.tensor.matmul(p_sg[k % 2][:, :], oh[k % 2][:, j, :], Gw[k % 2][:, j, :, :].rearrange("p h d -> p (h d)"),
                                                 start=(j == 0), stop=(j == ET - 1))
                        t.then_inc(s_sg, 1)

                    def step(g, k, last=False):
                        expand(g, k, pe.value_load(C.gblk[0:1, ds(g, 1)], min_val=0, max_val=NB - 1))
                        if not last:
                            transposes(g + 1, (k + 1) % UN)
                            spread(g + 1, (k + 1) % UN, 0)
                            spread(g + 1, (k + 1) % UN, 1)
                        sums(g, k)
                        if not last:
                            spread(g + 1, (k + 1) % UN, 2)
                            spread(g + 1, (k + 1) % UN, 3)

                    transposes(0, 0)
                    for h in range(H):
                        spread(0, 0, h)
                    with pe.Fori(0, NG // UN - 1) as i:
                        for k in range(UN):
                            step(i * UN + k, k)
                    for g in range(NG - UN, NG):
                        step(g, g % UN, last=g == NG - 1)


def stage_between(nc, C, A):
    with ExitStack() as ctx:
        sb, ps, sem = alloc(nc, ctx, "between_")
        wg = sb("wg2", [P, KC, D + 2 * H]); wgr = sb("wgr2", [P, KC, D]); alr = sb("alr2", [P, KC, 2 * H])
        bias = sb("bias1", [P, D]); den = sb("den", [P, NB * H])
        h1 = [sb(f"h1_{k}", [P, D]) for k in range(2)]
        hT = sb("h1T", [P, KC * P])
        row = [sb(f"rowb{k}", [P, D + H]) for k in range(2)]
        p_a = ps("p_a", [P, 512]); p_t = ps("p_t", [P, 512]); p_f = ps("p_fb", [P, 512])
        s_w = sem("s_w"); s_wa = sem("s_wa"); s_wac = sem("s_wac"); s_den = sem("s_den"); s_h = sem("s_h"); s_hs = sem("s_hs")
        s_t = sem("s_t"); s_tc = sem("s_tc"); s_f = sem("s_f"); s_row = sem("s_row")
        s_rowd = [sem(f"s_rowd{k}") for k in range(2)]

        with nc.Block() as block:
            @block.sync
            def _(sp):
                sp.dma_start(wg[:, :, 0:D], A["W2T"].rearrange("(c p) f -> p c f", p=P)).then_inc(s_w, 16)
                sp.dma_start(wgr[:, :, :], A["W2"].rearrange("(c p) f -> p c f", p=P)).then_inc(s_w, 16)
                sp.dma_start(alr[:, :, :], A["alr2"].rearrange("(c p) f -> p c f", p=P)).then_inc(s_w, 16)
                sp.dma_start(bias[:, :], A["b1"].partition_broadcast(P)).then_inc(s_w, 16)

                def back(b, k):
                    sp.wait_ge(s_row, b * 2 + 2)
                    sp.dma_start(C.tab2[ds(b * P, P), 0:D + H], row[k][:, :]).then_inc(s_rowd[k], 16)

                skewed(sp, NB, 2, lambda b, k: None, back)
                sp.wait_ge(s_rowd[0], 16 * ((NB + 1) // 2))
                sp.wait_ge(s_rowd[1], 16 * (NB // 2))

            @block.vector
            def _(v):
                acc4 = C.acc[:, :].rearrange("p (b h d) -> p b h d", h=H, d=HW)
                nc.vector.tensor_scalar(den[:, :].rearrange("p (b h) -> p b h", h=H), acc4[:, :, :, HD], 1e-9, None, ALU.max).then_inc(s_den, 1)
                v.wait_ge(s_den, 1)
                nc.vector.reciprocal(den[:, :], den[:, :]).then_inc(s_den, 1)
                v.wait_ge(s_w, 64)
                v.wait_ge(s_wa, 1)
                nc.vector.tensor_copy(wg[:, :, D:D + 2 * H], p_a[:, 0:KC * 2 * H].rearrange("p (c h) -> p c h", c=KC)).then_inc(s_wac, 1)
                v.wait_ge(s_den, 2)

                def front(b, k):
                    a = C.acc[:, ds(b * H * HW, H * HW)].rearrange("p (h d) -> p h d", h=H)[:, :, 0:HD]
                    h4 = h1[k][:, :].rearrange("p (h d) -> p h d", h=H)
                    nc.vector.tensor_tensor(h4, a, den[:, ds(b * H, H)].unsqueeze(2).broadcast_to([P, H, HD]), ALU.mult).then_inc(s_hs, 1)
                    v.wait_ge(s_hs, b * 2 + 1)
                    nc.vector.tensor_tensor(h1[k][:, :], h1[k][:, :], bias[:, :], ALU.add).then_inc(s_hs, 1)
                    v.wait_ge(s_hs, b * 2 + 2)
                    nc.vector.tensor_scalar(h1[k][:, :], h1[k][:, :], 0.0, None, ALU.max).then_inc(s_h, 1)

                def back(b, k):
                    v.wait_ge(s_f, b + 1)
                    if not isinstance(b, int) or b >= 2:
                        v.wait_ge(s_rowd[k], (b - k) * 8)
                    nc.vector.tensor_copy(row[k][:, :], p_f[:, 0:D + H]).then_inc(s_row, 1)
                    nc.vector.tensor_copy(C.ler[:, ds(b * 2 * H, 2 * H)], p_f[:, D:D + 2 * H]).then_inc(s_row, 1)

                skewed(v, NB, 2, front, back, peel=2)

            @block.scalar
            def _(act):
                def back(b, k):
                    act.wait_ge(s_t, b + 1)
                    nc.scalar.copy(hT[:, :], p_t[:, 0:KC * P]).then_inc(s_tc, 1)

                skewed(act, NB, 2, lambda b, k: None, back)

            @block.tensor
            def _(pe):
                pe.wait_ge(s_w, 64)
                project_attention_vectors(nc, p_a, wgr, alr, s_wa)
                pe.wait_ge(s_wac, 1)

                def back(b, k):
                    pe.wait_ge(s_h, b + 1)
                    if not isinstance(b, int) or b > 0:
                        pe.wait_ge(s_tc, b)
                    for c in range(KC):
                        t = nc.tensor.transpose(p_t[:, c * P:c * P + P], h1[k][:, c * P:c * P + P], C.ident[:, :])
                    t.then_inc(s_t, 1)
                    pe.wait_ge(s_tc, b + 1)
                    if not isinstance(b, int) or b > 0:
                        pe.wait_ge(s_row, b * 2)
                    for kc in range(KC):
                        t = nc.tensor.matmul(p_f[:, 0:D + 2 * H], hT[:, kc * P:kc * P + P], wg[:, kc, :], start=(kc == 0), stop=(kc == KC - 1))
                    t.then_inc(s_f, 1)

                skewed(pe, NB, 2, lambda b, k: None, back)


def stage_route(nc, C, A):
    with ExitStack() as ctx:
        sb, ps, sem = alloc(nc, ctx, "route_")
        bias = sb("bias2", [P, D]); den = sb("den2", [P, NB * H])
        gw = sb("gw", [P, KC, NE]); gb = sb("gb", [P, NE])
        t1 = sb("t1", [P, D])
        st = sb("st", [P, NB * 6]); mv = sb("mv", [P, NB * 2]); rstd = sb("rstd", [P, NB])
        xa = [sb(f"xa{b}", [P, D]) for b in range(NB)]
        xT = sb("xTr", [P, KC * P])
        lg = sb("lg", [P, NB, NE]); mx8 = sb("mx8", [P, NB, 8]); ix8 = sb("ix8", [P, NB, 8], U32)
        ixf = sb("ixf", [P, NB]); ex = sb("ex", [P, NB, NE]); sm = sb("sm", [P, NB])
        one = sb("one", [P, NB, NE]); up = sb("up", [P, P]); onesq = sb("onesq2", [P, P])
        tot = sb("tot", [P, NB, NE]); run = sb("run", [P, NE, NB]); pos3 = sb("pos3", [P, NB, NE]); pos = sb("pos", [P, NB])
        kept = sb("kept", [P, NB]); drop = sb("drop", [P, NB]); base = sb("base", [P, NB])
        slf = sb("slf", [P, NB]); sloti = sb("sloti", [P, NB], I32); vali = sb("vali", [P, NB], I32); val = sb("val", [P, NB])
        p_t = ps("p_tr", [P, 512]); p_l = ps("p_l", [P, 512]); p_c = ps("p_c", [P, 2, 512])
        s_w = sem("s_w"); s_pl = sem("s_pl"); s_v = sem("s_v"); s_a = sem("s_a"); s_st = sem("s_st"); s_var = sem("s_var"); s_std = sem("s_std")
        s_xa = sem("s_xa"); s_t = sem("s_t"); s_tc = sem("s_tc"); s_l = sem("s_l"); s_lc = sem("s_lc"); s_one = sem("s_one"); s_cs = sem("s_cs")
        s_ex0 = sem("s_ex0"); s_ex1 = sem("s_ex1"); s_slot = sem("s_slot"); s_sc = sem("s_sc")

        with nc.Block() as block:
            @block.sync
            def _(sp):
                sp.dma_start(bias[:, :], A["b2"].partition_broadcast(P)).then_inc(s_w, 16)
                sp.dma_start(gw[:, :, :], A["gate_w"].rearrange("(c p) e -> p c e", p=P)).then_inc(s_w, 16)
                sp.dma_start(gb[:, :], A["gate_b"].partition_broadcast(P)).then_inc(s_w, 16)

            @block.gpsimd
            def _(gp):
                nc.gpsimd.memset(up[:, :], 1.0).then_inc(s_pl, 1)
                nc.gpsimd.iota(vali[:, :], pattern=[[P, NB]], base=0, channel_multiplier=1).then_inc(s_pl, 1)
                gp.wait_ge(s_pl, 2)
                nc.gpsimd.affine_select(out=up[:, :], in_=up[:, :], compare_op=ALU.is_gt, fill=0.0, base=0,
                                        pattern=[[1, P]], channel_multiplier=-1).then_inc(s_pl, 1)
                gp.wait_ge(s_slot, 1)
                for b in range(NB):
                    gp.indirect_dma_start(out=C.ffn_in[:, :], out_offset=bass.IndirectOffsetOnAxis(ap=sloti[:, b:b + 1], axis=0),
                                          in_=xa[b][:, :], in_offset=None, bounds_check=NE * CS - 1, oob_is_err=False).then_inc(s_sc, 16)
                gp.wait_ge(s_sc, 16 * NB)

            @block.vector
            def _(v):
                acc4 = C.acc[:, :].rearrange("p (b h d) -> p b h d", h=H, d=HW)
                nc.vector.tensor_scalar(den[:, :].rearrange("p (b h) -> p b h", h=H), acc4[:, :, :, HD], 1e-9, None, ALU.max).then_inc(s_v, 1)
                v.wait_ge(s_v, 1)
                nc.vector.reciprocal(den[:, :], den[:, :]).then_inc(s_v, 1)
                nc.vector.memset(onesq[:, :], 1.0).then_inc(s_v, 1)
                v.wait_ge(s_w, 48)
                v.wait_ge(s_v, 3)
                with v.Fori(0, NB) as b:
                    a = C.acc[:, ds(b * H * HW, H * HW)].rearrange("p (h d) -> p h d", h=H)[:, :, 0:HD]
                    x = C.X[:, ds(b * D, D)]
                    v.wait_ge(s_a, b * 4)
                    nc.vector.tensor_tensor(t1[:, :].rearrange("p (h d) -> p h d", h=H), a, den[:, ds(b * H, H)].unsqueeze(2).broadcast_to([P, H, HD]), ALU.mult).then_inc(s_a, 1)
                    v.wait_ge(s_a, b * 4 + 1)
                    nc.vector.tensor_tensor(t1[:, :], t1[:, :], bias[:, :], ALU.add).then_inc(s_a, 1)
                    v.wait_ge(s_a, b * 4 + 2)
                    nc.vector.scalar_tensor_tensor(out=x, in0=t1[:, :], scalar=0.0, in1=x, op0=ALU.max, op1=ALU.add).then_inc(s_a, 1)
                    v.wait_ge(s_a, b * 4 + 3)
                    nc.vector.bn_stats(st[:, ds(b * 6, 6)], x).then_inc(s_a, 1)
                v.wait_ge(s_a, 4 * NB)
                ln_finish(nc, v, mv, st, rstd, s_st, s_var, s_std, 1e-5)
                for b in range(NB):
                    nc.vector.tensor_scalar(xa[b][:, :], C.X[:, b * D:b * D + D], mv[:, 2 * b:2 * b + 1], rstd[:, b:b + 1], ALU.subtract, ALU.mult).then_inc(s_xa, 1)
                v.wait_ge(s_pl, 3)
                nc.vector.tensor_scalar(val[:, :], vali[:, :], float(N), None, ALU.is_lt).then_inc(s_v, 1)
                v.wait_ge(s_l, NB)
                nc.vector.tensor_tensor(lg[:, :, :], p_l[:, 0:NB * NE].rearrange("p (b e) -> p b e", e=NE),
                                        gb[:, :].unsqueeze(1).broadcast_to([P, NB, NE]), ALU.add).then_inc(s_lc, NB)
                v.wait_ge(s_lc, NB)
                for b in range(NB):
                    nc.vector.max(mx8[:, b, :], lg[:, b, :]).then_inc(s_lc, 1)
                v.wait_ge(s_lc, 2 * NB)
                for b in range(NB):
                    nc.vector.max_index(ix8[:, b, :], mx8[:, b, :], lg[:, b, :]).then_inc(s_lc, 1)
                nc.vector.tensor_tensor(ex[:, :, :], lg[:, :, :], mx8[:, :, 0:1].broadcast_to([P, NB, NE]), ALU.subtract).then_inc(s_ex0, 1)
                v.wait_ge(s_lc, 3 * NB)
                nc.vector.tensor_copy(ixf[:, :], ix8[:, :, 0]).then_inc(s_v, 1)
                v.wait_ge(s_v, 5)
                nc.vector.tensor_tensor(one[:, :, :], C.iota[:, 0:NE].unsqueeze(1).broadcast_to([P, NB, NE]),
                                        ixf[:, :].unsqueeze(2).broadcast_to([P, NB, NE]), ALU.is_equal).then_inc(s_v, 1)
                v.wait_ge(s_v, 6)
                nc.vector.tensor_tensor(one[:, :, :], one[:, :, :], val[:, :].unsqueeze(2).broadcast_to([P, NB, NE]), ALU.mult).then_inc(s_one, 1)
                v.wait_ge(s_ex1, 1)
                nc.vector.tensor_reduce(sm[:, :], ex[:, :, :], AX.X, ALU.add).then_inc(s_v, 1)
                v.wait_ge(s_v, 7)
                nc.vector.reciprocal(sm[:, :], sm[:, :]).then_inc(s_v, 1)
                v.wait_ge(s_cs, 1)
                nc.vector.tensor_copy(tot[:, :, :], p_c[:, 1, 0:NB * NE].rearrange("p (b e) -> p b e", e=NE)).then_inc(s_v, 1)
                v.wait_ge(s_v, 9)
                for e in range(NE):
                    nc.vector.tensor_tensor_scan(run[:, e, :], tot[:, :, e], tot[:, :, e], 0.0, ALU.add, ALU.bypass).then_inc(s_v, 1)
                v.wait_ge(s_v, 9 + NE)
                nc.vector.tensor_tensor(pos3[:, :, :], run[:, :, :].rearrange("p e b -> p b e"), tot[:, :, :], ALU.subtract).then_inc(s_v, 1)
                v.wait_ge(s_v, 10 + NE)
                nc.vector.tensor_tensor(pos3[:, :, :], pos3[:, :, :], p_c[:, 0, 0:NB * NE].rearrange("p (b e) -> p b e", e=NE), ALU.add).then_inc(s_v, 1)
                v.wait_ge(s_v, 11 + NE)
                nc.vector.tensor_tensor(pos3[:, :, :], pos3[:, :, :], one[:, :, :], ALU.mult).then_inc(s_v, 1)
                v.wait_ge(s_v, 12 + NE)
                nc.vector.tensor_reduce(pos[:, :], pos3[:, :, :], AX.X, ALU.add).then_inc(s_v, 1)
                nc.vector.tensor_scalar(base[:, :], ixf[:, :], float(CS), None, ALU.mult).then_inc(s_v, 1)
                v.wait_ge(s_v, 14 + NE)
                nc.vector.scalar_tensor_tensor(out=kept[:, :], in0=pos[:, :], scalar=float(CAP), in1=val[:, :], op0=ALU.is_lt, op1=ALU.mult).then_inc(s_v, 1)
                nc.vector.tensor_tensor(slf[:, :], base[:, :], pos[:, :], ALU.add).then_inc(s_v, 1)
                v.wait_ge(s_v, 16 + NE)
                nc.vector.tensor_scalar(drop[:, :], kept[:, :], float(-NE * CS), float(NE * CS), ALU.mult, ALU.add).then_inc(s_v, 1)
                nc.vector.tensor_tensor(C.gate[:, :], sm[:, :], kept[:, :], ALU.mult).then_inc(s_v, 1)
                v.wait_ge(s_v, 18 + NE)
                nc.vector.tensor_tensor(sloti[:, :], slf[:, :], drop[:, :], ALU.add).then_inc(s_slot, 1)
                nc.vector.tensor_scalar(pos[:, :], pos[:, :], float(CAP - 1), None, ALU.min).then_inc(s_v, 1)
                v.wait_ge(s_v, 19 + NE)
                nc.vector.tensor_tensor(C.back[:, :], base[:, :], pos[:, :], ALU.add).then_inc(s_v, 1)

            @block.scalar
            def _(act):
                ln_sqrt(nc, act, rstd, s_var, s_std)
                for b in range(NB):
                    act.wait_ge(s_t, b + 1)
                    nc.scalar.copy(xT[:, :], p_t[:, 0:KC * P]).then_inc(s_tc, 1)
                act.wait_ge(s_ex0, 1)
                nc.scalar.activation(ex[:, :, :], ex[:, :, :], ACT.Exp).then_inc(s_ex1, 1)

            @block.tensor
            def _(pe):
                pe.wait_ge(s_w, 48)
                for b in range(NB):
                    pe.wait_ge(s_xa, b + 1)
                    if b > 0:
                        pe.wait_ge(s_tc, b)
                    for c in range(KC):
                        t = nc.tensor.transpose(p_t[:, c * P:c * P + P], xa[b][:, c * P:c * P + P], C.ident[:, :])
                    t.then_inc(s_t, 1)
                    pe.wait_ge(s_tc, b + 1)
                    for kc in range(KC):
                        t = nc.tensor.matmul(p_l[:, b * NE:b * NE + NE], xT[:, kc * P:kc * P + P], gw[:, kc, :], start=(kc == 0), stop=(kc == KC - 1))
                    t.then_inc(s_l, 1)
                pe.wait_ge(s_pl, 3)
                pe.wait_ge(s_v, 3)
                pe.wait_ge(s_one, 1)
                o = one[:, :, :].rearrange("p b e -> p (b e)")
                nc.tensor.matmul(p_c[:, 0, 0:NB * NE], up[:, :], o, start=True, stop=True)
                nc.tensor.matmul(p_c[:, 1, 0:NB * NE], onesq[:, :], o, start=True, stop=True).then_inc(s_cs, 1)


def stage_experts(nc, C, A):
    with ExitStack() as ctx:
        sb, ps, sem = alloc(nc, ctx, "experts_")
        TS = CS // P
        w1 = [sb(f"ew1_{k}", [P, KC, F]) for k in range(2)]
        w2 = [sb(f"ew2_{k}", [P, FC, D]) for k in range(2)]
        b1 = sb("eb1", [P, NE, FC]); b2 = sb("eb2", [P, NE * D])
        xi = [sb(f"xi{k}", [P, TS, D]) for k in range(2)]
        xT = sb("xTe", [P, KC, CS]); hT = sb("hTe", [P, FC, CS])
        y = [sb(f"ye{k}", [P, TS, D]) for k in range(2)]
        p_t = ps("p_te", [P, KC, CS]); p_h = ps("p_he", [P, 2, 512]); p_y = ps("p_ye", [P, 2, 512])
        s_b = sem("s_b"); s_in = [sem(f"s_in{k}") for k in range(2)]; s_t = sem("s_t"); s_tc = sem("s_tc")
        s_h = sem("s_h"); s_hc = sem("s_hc"); s_y = sem("s_y"); s_yc = sem("s_yc"); s_yd = [sem(f"s_yd{k}") for k in range(2)]

        def experts(eng, body):
            for e in range(2):
                body(e, e)
            with eng.Fori(1, NE // 2) as i:
                for k in range(2):
                    body(i * 2 + k, k)

        with nc.Block() as block:
            @block.sync
            def _(sp):
                sp.dma_start(b1[:, :, :], A["eb1"].rearrange("e (c p) -> p e c", p=P), allow_slow_non_contiguous=True).then_inc(s_b, 16)
                sp.dma_start(b2[:, :], A["eb2"].rearrange("e d -> (e d)").partition_broadcast(P)).then_inc(s_b, 16)

                def body(e, k):
                    if not isinstance(e, int) or e >= 2:
                        sp.wait_ge(s_yc, (e - 1) * TS)
                    sp.dma_start(w1[k][:, :, :], A["ew1"][ds(e * D, D), :].rearrange("(c p) f -> p c f", p=P)).then_inc(s_in[k], 16)
                    sp.dma_start(w2[k][:, :, :], A["ew2"][ds(e * F, F), :].rearrange("(c p) f -> p c f", p=P)).then_inc(s_in[k], 16)
                    sp.dma_start(xi[k][:, :, :], C.ffn_in[ds(e * CS, CS), :].rearrange("(t p) d -> p t d", p=P)).then_inc(s_in[k], 16)

                experts(sp, body)

            @block.gpsimd
            def _(gp):
                def body(e, k):
                    gp.wait_ge(s_yc, e * TS + TS)
                    gp.dma_start(C.ffn_out[ds(e * CS, CS), :].rearrange("(t p) d -> p t d", p=P), y[k][:, :, :]).then_inc(s_yd[k], 16)
                for e in range(NE):
                    body(e, e % 2)
                gp.wait_ge(s_yd[0], 16 * NE // 2)
                gp.wait_ge(s_yd[1], 16 * NE // 2)

            @block.vector
            def _(v):
                v.wait_ge(s_b, 32)

                def body(e, k):
                    if not isinstance(e, int) or e >= 2:
                        v.wait_ge(s_yd[k], (e - k) * 8)
                    for t in range(TS):
                        v.wait_ge(s_y, e * TS + t + 1)
                        nc.vector.tensor_tensor(y[k][:, t, :], p_y[:, t % 2, 0:D], b2[:, ds(e * D, D)], ALU.add).then_inc(s_yc, 1)

                experts(v, body)

            @block.scalar
            def _(act):
                act.wait_ge(s_b, 32)

                def body(e, k):
                    act.wait_ge(s_t, e + 1)
                    nc.scalar.copy(xT[:, :, :], p_t[:, :, :]).then_inc(s_tc, 1)
                    for c in range(FC):
                        act.wait_ge(s_h, e * FC + c + 1)
                        nc.scalar.activation(hT[:, c, :], p_h[:, c % 2, :], ACT.Relu, bias=b1[:, ds(e, 1), c:c + 1].rearrange("p a b -> p (a b)")).then_inc(s_hc, 1)

                experts(act, body)

            @block.tensor
            def _(pe):
                def body(e, k):
                    later = not isinstance(e, int) or e > 0
                    pe.wait_ge(s_in[k], (e - k) * 24 + 48)
                    if later:
                        pe.wait_ge(s_tc, e)
                    for t in range(TS):
                        for c in range(KC):
                            m = nc.tensor.transpose(p_t[:, c, t * P:t * P + P], xi[k][:, t, c * P:c * P + P], C.ident[:, :])
                    m.then_inc(s_t, 1)
                    pe.wait_ge(s_tc, e + 1)
                    for c in range(FC):
                        if later or c >= 2:
                            pe.wait_ge(s_hc, e * FC + c - 1)
                        for kc in range(KC):
                            m = nc.tensor.matmul(p_h[:, c % 2, :], w1[k][:, kc, c * P:c * P + P], xT[:, kc, :], start=(kc == 0), stop=(kc == KC - 1))
                        m.then_inc(s_h, 1)
                    pe.wait_ge(s_hc, e * FC + FC)
                    for t in range(TS):
                        if later or t >= 2:
                            pe.wait_ge(s_yc, e * TS + t - 1)
                        for c in range(FC):
                            m = nc.tensor.matmul(p_y[:, t % 2, 0:D], hT[:, c, t * P:t * P + P], w2[k][:, c, :], start=(c == 0), stop=(c == FC - 1))
                        m.then_inc(s_y, 1)

                experts(pe, body)


def stage_gated_in(nc, C, A):
    with ExitStack() as ctx:
        sb, ps, sem = alloc(nc, ctx, "gated_in_")
        w3 = sb("w3", [P, KC, 3 * D]); b3 = sb("b3", [1, 3 * D]); al = sb("al", [P, D]); ar = sb("ar", [P, D]); ones1 = sb("ones1g", [1, P])
        yb = [sb(f"yb{k}", [P, D]) for k in range(4)]
        fin = sb("fin", [P, D], U32); nn = sb("nn", [P, D], U32); cl = sb("cl", [P, D]); ysafe = sb("ysafe", [P, D])
        st = sb("st", [P, NB * 6]); mv = sb("mv", [P, NB * 2]); rstd = sb("rstd", [P, NB])
        xn = [sb(f"xng{k}", [P, D]) for k in range(2)]; xT = sb("xTg", [P, KC * P])
        row = [sb(f"rowg{k}", [P, 2 * D]) for k in range(2)]; us = [sb(f"us{k}", [P, D]) for k in range(2)]
        p_t = ps("p_tg", [P, 512]); p_a = ps("p_ag", [P, 2, 512])
        s_w = sem("s_w"); s_yb = [sem(f"s_yb{k}") for k in range(4)]; s_y = sem("s_y"); s_ya = sem("s_ya"); s_st = sem("s_st"); s_var = sem("s_var"); s_std = sem("s_std")
        s_one = sem("s_one"); s_xn = sem("s_xn"); s_t = sem("s_t"); s_tc = sem("s_tc"); s_a = sem("s_a"); s_row = sem("s_row"); s_x = sem("s_x")
        s_rowd = [sem(f"s_rowd{k}") for k in range(2)]

        with nc.Block() as block:
            @block.sync
            def _(sp):
                sp.dma_start(w3[:, :, :], A["w3"].rearrange("(c p) f -> p c f", p=P)).then_inc(s_w, 16)
                sp.dma_start(b3[:, :], A["b3"].rearrange("(a f) -> a f", a=1)).then_inc(s_w, 16)
                sp.dma_start(al[:, :], A["attn_l"].partition_broadcast(P)).then_inc(s_w, 16)
                sp.dma_start(ar[:, :], A["attn_r"].partition_broadcast(P)).then_inc(s_w, 16)

                def back(b, k):
                    sp.wait_ge(s_row, b * 4 + 4)
                    sp.dma_start(C.tab3[ds(b * P, P), :], row[k][:, :]).then_inc(s_rowd[k], 16)
                    sp.dma_start(C.u_d[ds(b * P, P), :], us[k][:, :]).then_inc(s_rowd[k], 16)

                skewed(sp, NB, 2, lambda b, k: None, back)
                sp.wait_ge(s_rowd[0], 32 * ((NB + 1) // 2))
                sp.wait_ge(s_rowd[1], 32 * (NB // 2))

            @block.gpsimd
            def _(gp):
                for b in range(NB):
                    if b >= 4:
                        gp.wait_ge(s_ya, b - 3)
                    gp.indirect_dma_start(out=yb[b % 4][:, :], out_offset=None, in_=C.ffn_out[:, :],
                                          in_offset=bass.IndirectOffsetOnAxis(ap=C.back[:, b:b + 1], axis=0)).then_inc(s_yb[b % 4], 16)

            @block.vector
            def _(v):
                nc.vector.memset(ones1[:, :], 1.0).then_inc(s_one, 1)
                for b in range(NB):
                    yk = yb[b % 4]
                    x = C.X[:, b * D:b * D + D]
                    v.wait_ge(s_yb[b % 4], 16 * (b // 4 + 1))
                    nc.vector.tensor_scalar(yk[:, :], yk[:, :], C.gate[:, b:b + 1], None, ALU.mult).then_inc(s_y, 1)
                    nc.vector.memset(ysafe[:, :], 0.0).then_inc(s_y, 1)
                    v.wait_ge(s_y, 8 * b + 2)
                    nc.vector.tensor_scalar(fin[:, :], yk[:, :], 0.0, 0.0, ALU.mult, ALU.is_equal).then_inc(s_y, 1)
                    nc.vector.tensor_tensor(nn[:, :], yk[:, :], yk[:, :], ALU.is_equal).then_inc(s_y, 1)
                    nc.vector.tensor_scalar(cl[:, :], yk[:, :], -1e4, 1e4, ALU.max, ALU.min).then_inc(s_y, 1)
                    v.wait_ge(s_y, 8 * b + 5)
                    nc.vector.copy_predicated(ysafe[:, :], nn[:, :], cl[:, :]).then_inc(s_y, 1)
                    v.wait_ge(s_y, 8 * b + 6)
                    nc.vector.copy_predicated(ysafe[:, :], fin[:, :], yk[:, :]).then_inc(s_y, 1)
                    v.wait_ge(s_y, 8 * b + 7)
                    nc.vector.tensor_tensor(x, x, ysafe[:, :], ALU.add).then_inc(s_ya, 1)
                    v.wait_ge(s_ya, b + 1)
                    nc.vector.bn_stats(st[:, b * 6:b * 6 + 6], x).then_inc(s_y, 1)
                v.wait_ge(s_y, 8 * NB)
                ln_finish(nc, v, mv, st, rstd, s_st, s_var, s_std, 1e-5)
                v.wait_ge(s_w, 64)

                def front(b, k):
                    if not isinstance(b, int) or b >= 2:
                        v.wait_ge(s_x, b - 1)
                    nc.vector.tensor_scalar(xn[k][:, :], C.X[:, ds(b * D, D)], mv[:, ds(b * 2, 1)], rstd[:, ds(b, 1)],
                                            ALU.subtract, ALU.mult).then_inc(s_xn, 1)

                def back(b, k):
                    x = C.X[:, ds(b * D, D)]
                    v.wait_ge(s_xn, b + 1)
                    nc.vector.tensor_tensor(x, x, xn[k][:, :], ALU.add).then_inc(s_x, 1)
                    v.wait_ge(s_a, b * 2 + 1)
                    if not isinstance(b, int) or b >= 2:
                        v.wait_ge(s_rowd[k], (b - k) * 16)
                    nc.vector.tensor_tensor(row[k][:, 0:D], p_a[:, 0, 0:D], al[:, :], ALU.mult).then_inc(s_row, 1)
                    nc.vector.tensor_tensor(C.wr[:, ds(b * D, D)], p_a[:, 0, 0:D], ar[:, :], ALU.mult).then_inc(s_row, 1)
                    v.wait_ge(s_a, b * 2 + 2)
                    nc.vector.tensor_copy(us[k][:, :], p_a[:, 0, D:2 * D]).then_inc(s_row, 1)
                    nc.vector.tensor_copy(row[k][:, D:2 * D], p_a[:, 1, 0:D]).then_inc(s_row, 1)

                skewed(v, NB, 2, front, back, peel=2)

            @block.scalar
            def _(act):
                ln_sqrt(nc, act, rstd, s_var, s_std)

                def back(b, k):
                    act.wait_ge(s_t, b + 1)
                    nc.scalar.copy(xT[:, :], p_t[:, 0:KC * P]).then_inc(s_tc, 1)

                skewed(act, NB, 2, lambda b, k: None, back)

            @block.tensor
            def _(pe):
                pe.wait_ge(s_w, 64)
                pe.wait_ge(s_one, 1)

                def back(b, k):
                    later = not isinstance(b, int) or b > 0
                    pe.wait_ge(s_xn, b + 1)
                    if later:
                        pe.wait_ge(s_tc, b)
                    for c in range(KC):
                        t = nc.tensor.transpose(p_t[:, c * P:c * P + P], xn[k][:, c * P:c * P + P], C.ident[:, :])
                    t.then_inc(s_t, 1)
                    pe.wait_ge(s_tc, b + 1)
                    if later:
                        pe.wait_ge(s_row, b * 4)
                    for a, lo, w in ((0, 0, 2 * D), (1, 2 * D, D)):
                        for kc in range(KC):
                            nc.tensor.matmul(p_a[:, a, 0:w], xT[:, kc * P:kc * P + P], w3[:, kc, lo:lo + w], start=(kc == 0), stop=False)
                        nc.tensor.matmul(p_a[:, a, 0:w], ones1[0:1, :], b3[0:1, lo:lo + w], start=False, stop=True).then_inc(s_a, 1)

                skewed(pe, NB, 2, lambda b, k: None, back)


def stage_gated(nc, C):
    with ExitStack() as ctx:
        sb, ps, sem = alloc(nc, ctx, "gated_")
        ix = [sb(f"jx{k}", [P, ET, 2], I32) for k in range(UN)]
        G = [sb(f"J{k}", [P, ET, 2 * D]) for k in range(UN)]
        dl = [sb(f"jdl{k}", [P, ET]) for k in range(2)]
        oh = [sb(f"joh{k}", [P, ET, P]) for k in range(UN)]
        ohT = [sb(f"johT{k}", [P, EG]) for k in range(2)]
        tv = sb("tv", [P, ET, D])
        sv = [sb(f"sv{k}", [P, ET, 2 * D]) for k in range(2)]
        p_oT = ps("p_joT", [P, 512]); p_b = ps("p_jb", [P, ET, D]); p_sg = [ps(f"p_jsg{k}", [P, 2 * D]) for k in range(2)]
        s_ix = [sem(f"s_ix{k}") for k in range(UN)]; s_g = [sem(f"s_g{k}") for k in range(UN)]
        s_go = sem("s_go"); s_init = sem("s_init"); s_dl = sem("s_dl"); s_oh = sem("s_oh"); s_T = sem("s_T"); s_cp = sem("s_cp")
        s_b = sem("s_b"); s_t = sem("s_t"); s_s = sem("s_s"); s_use = sem("s_use"); s_sg = sem("s_sg"); s_acc = sem("s_acc")

        def block_of(eng, g):
            return eng.value_load(C.gblk[0:1, ds(g, 1)], min_val=0, max_val=NB - 1)

        with nc.Block() as block:
            @block.sync
            def _(sp):
                def load(g, k):
                    off = sp.value_load(C.gofs[0:1, ds(g, 1)], min_val=0, max_val=E)
                    sp.dma_start(ix[k][:, :, :].rearrange("p c t -> p (c t)"),
                                 C.edges[ds(off, EG), :].rearrange("(p c) t -> p (c t)", c=ET)).then_inc(s_ix[k], 16)
                for k in range(UN):
                    load(k, k)
                with sp.Fori(1, NG // UN) as i:
                    for k in range(UN):
                        sp.wait_ge(s_use, i * UN + k - UN + 1)
                        load(i * UN + k, k)

            @block.gpsimd
            def _(gp):
                with gp.Fori(0, NG // UN) as i:
                    for k in range(UN):
                        hold(gp, s_ix[k], i * 16 + 16, s_go)
                        for j in range(ET):
                            gp.indirect_dma_start(out=G[k][:, j, :], out_offset=None, in_=C.tab3[:, :],
                                                  in_offset=bass.IndirectOffsetOnAxis(ap=ix[k][:, j, 0:1], axis=0)).then_inc(s_g[k], 16)

            @block.vector
            def _(v):
                nc.vector.memset(C.acc3[:, :], 0.0).then_inc(s_init, 1)
                v.wait_ge(s_init, 1)

                def one_hot(g, k):
                    v.wait_ge(s_ix[k], (g - k) * 4 + 16)
                    nc.vector.tensor_scalar(dl[k % 2][:, :], ix[k][:, :, 1], C.gbase[:, ds(g, 1)], None, ALU.subtract).then_inc(s_dl, 1)
                    v.wait_ge(s_dl, g + 1)
                    nc.vector.tensor_tensor(oh[k][:, :, :], C.iota[:, :].unsqueeze(1).broadcast_to([P, ET, P]),
                                            dl[k % 2][:, :].unsqueeze(2).broadcast_to([P, ET, P]), ALU.is_equal).then_inc(s_oh, 1)

                def accumulate(g, k, blk):
                    a = C.acc3[:, ds(blk * 2 * D, 2 * D)]
                    v.wait_ge(s_sg, g + 1)
                    nc.vector.tensor_tensor(a, a, p_sg[k % 2][:, :], ALU.add).then_inc(s_acc, 1)
                    v.wait_ge(s_acc, g + 1)

                def step(g, k, last=False):
                    v.wait_ge(s_g[k], (g - k) * 16 + 64)
                    v.wait_ge(s_b, g + 1)
                    if not isinstance(g, int) or g > 0:
                        v.wait_ge(s_s, g)
                    nc.vector.tensor_tensor(tv[:, :, :], G[k][:, :, 0:D], p_b[:, :, :], ALU.add).then_inc(s_t, 1)
                    if not last:
                        one_hot(g + 1, (k + 1) % UN)
                    if not isinstance(g, int) or g > 0:
                        accumulate(g - 1, (k - 1) % UN, block_of(v, g - 1))
                    v.wait_ge(s_s, g + 1)
                    nc.vector.tensor_tensor(sv[k % 2][:, :, 0:D], G[k][:, :, D:2 * D], sv[k % 2][:, :, D:2 * D], ALU.mult).then_inc(s_use, 1)

                one_hot(0, 0)
                for g in range(UN):
                    step(g, g)
                with v.Fori(1, NG // UN - 1) as i:
                    for k in range(UN):
                        step(i * UN + k, k)
                for g in range(NG - UN, NG):
                    step(g, g % UN, last=g == NG - 1)
                accumulate(NG - 1, (NG - 1) % UN, block_of(v, NG - 1))

            @block.scalar
            def _(act):
                def front(g, k):
                    act.wait_ge(s_T, g + 1)
                    nc.scalar.copy(ohT[k % 2][:, :], p_oT[:, :]).then_inc(s_cp, 1)

                def back(g, k):
                    act.wait_ge(s_t, g + 1)
                    nc.scalar.activation(sv[k % 2][:, :, D:2 * D], tv[:, :, :], ACT.Sigmoid).then_inc(s_s, 1)

                front(0, 0)
                with act.Fori(0, NG // UN - 1) as i:
                    for k in range(UN):
                        g = i * UN + k
                        back(g, k)
                        front(g + 1, (k + 1) % UN)
                for g in range(NG - UN, NG):
                    back(g, g % UN)
                    if g + 1 < NG:
                        front(g + 1, (g + 1) % UN)

            @block.tensor
            def _(pe):
                def transposes(g, k):
                    pe.wait_ge(s_oh, g + 1)
                    if not isinstance(g, int) or g > 0:
                        pe.wait_ge(s_cp, g)
                    for j in range(ET):
                        t = nc.tensor.transpose(p_oT[:, j * P:j * P + P], oh[k][:, j, :], C.ident[:, :])
                    t.then_inc(s_T, 1)

                def expand(g, k, blk):
                    pe.wait_ge(s_cp, g + 1)
                    if not isinstance(g, int) or g > 0:
                        pe.wait_ge(s_t, g)
                    for j in range(ET):
                        t = nc.tensor.matmul(p_b[:, j, :], ohT[k % 2][:, j * P:j * P + P], C.wr[:, ds(blk * D, D)], start=True, stop=True)
                    t.then_inc(s_b, 1)

                def sums(g, k):
                    pe.wait_ge(s_use, g + 1)
                    for j in range(ET):
                        t = nc.tensor.matmul(p_sg[k % 2][:, :], oh[k][:, j, :], sv[k % 2][:, j, :], start=(j == 0), stop=(j == ET - 1))
                    t.then_inc(s_sg, 1)

                transposes(0, 0)
                expand(0, 0, block_of(pe, 0))

                def step(g, k, last=False):
                    if not last:
                        transposes(g + 1, (k + 1) % UN)
                        expand(g + 1, (k + 1) % UN, block_of(pe, g + 1))
                    sums(g, k)

                with pe.Fori(0, NG // UN - 1) as i:
                    for k in range(UN):
                        step(i * UN + k, k)
                for g in range(NG - UN, NG):
                    step(g, g % UN, last=g == NG - 1)


def stage_dense(nc, C, A, out):
    with ExitStack() as ctx:
        sb, ps, sem = alloc(nc, ctx, "dense_")
        w1 = sb("fw1", [P, KC, F]); b1 = sb("fb1", [P, FC]); wgt = sb("fwg", [P, FC, NE]); bg = sb("fbg", [P, NE]); bd = sb("fbd", [NE, D])
        gam = sb("gam", [P, D]); bet = sb("bet", [P, D])
        U = [sb(f"U{k}", [P, D]) for k in range(2)]; t1 = sb("t1d", [P, D]); t2 = sb("t2d", [P, D])
        st = sb("st", [P, NB * 6]); mv = sb("mv", [P, NB * 2]); rstd = sb("rstd", [P, NB])
        st2 = sb("st2d", [P, NB * 6]); mv2 = sb("mv2d", [P, NB * 2]); rstd2 = sb("rstd2", [P, NB])
        s_w = sem("s_w"); s_u = [sem(f"s_u{k}") for k in range(2)]; s_r = sem("s_r"); s_c = sem("s_c"); s_ur = sem("s_ur")
        s_st = sem("s_st"); s_var = sem("s_var"); s_std = sem("s_std"); s_st2 = sem("s_st2"); s_var2 = sem("s_var2"); s_std2 = sem("s_std2"); s_n = sem("s_n")
        xn = [sb(f"xnd{k}", [P, D]) for k in range(2)]
        xT = sb("xTd", [P, KC * P])
        HT = [sb(f"HT{k}", [P, FC * P]) for k in range(2)]
        lg = sb("lgd", [P, NB, NE]); mx8 = sb("mx8d", [P, NB, 8]); ix8 = sb("ix8d", [P, NB, 8], U32); ixf = sb("ixfd", [P, NB])
        ex = sb("exd", [P, NB, NE]); sm = sb("smd", [P, NB]); pr = sb("prd", [P, NB * NE])
        s_xn = sem("s_xn"); s_t = sem("s_t"); s_tc = sem("s_tc"); s_h = sem("s_h"); s_hc = sem("s_hc"); s_l = sem("s_l"); s_lc = sem("s_lc")
        s_m = sem("s_m"); s_e0 = sem("s_e0"); s_e1 = sem("s_e1"); s_pr = sem("s_pr"); s_y = sem("s_y"); s_ya = sem("s_ya"); s_pT = sem("s_pT"); s_pTc = sem("s_pTc"); s_wd = sem("s_wd")
        s_out = sem("s_out")

        with nc.Block() as block:
            @block.sync
            def _(sp):
                sp.dma_start(gam[:, :], A["gamma"].partition_broadcast(P)).then_inc(s_w, 16)
                sp.dma_start(bet[:, :], A["beta"].partition_broadcast(P)).then_inc(s_w, 16)

                def body(b, k):
                    if not isinstance(b, int) or b >= 2:
                        sp.wait_ge(s_ur, b - 1)
                    sp.dma_start(U[k][:, :], C.u_d[ds(b * P, P), :]).then_inc(s_u[k], 16)
                skewed(sp, NB, 2, lambda b, k: None, body, peel=2)

            @block.vector
            def _(v):
                v.wait_ge(s_w, 32)

                def body(b, k):
                    a = C.acc3[:, ds(b * 2 * D, D)]
                    d = C.acc3[:, ds(b * 2 * D + D, D)]
                    v.wait_ge(s_u[k], (b - k) * 8 + 16)
                    nc.vector.tensor_scalar(t1[:, :], d, 1e-6, None, ALU.add).then_inc(s_r, 1)
                    v.wait_ge(s_r, b * 4 + 1)
                    nc.vector.reciprocal(t1[:, :], t1[:, :]).then_inc(s_r, 1)
                    v.wait_ge(s_r, b * 4 + 2)
                    nc.vector.tensor_tensor(a, a, t1[:, :], ALU.mult).then_inc(s_r, 1)
                    v.wait_ge(s_r, b * 4 + 3)
                    nc.vector.tensor_tensor(a, a, U[k][:, :], ALU.add).then_inc(s_ur, 1)
                    v.wait_ge(s_ur, b + 1)
                    nc.vector.bn_stats(st[:, ds(b * 6, 6)], a).then_inc(s_r, 1)

                skewed(v, NB, 2, lambda b, k: None, body)
                v.wait_ge(s_r, 4 * NB)
                ln_finish(nc, v, mv, st, rstd, s_st, s_var, s_std, 1e-6)

                with v.Fori(0, NB) as b:
                    a = C.acc3[:, ds(b * 2 * D, D)]
                    x = C.X[:, ds(b * D, D)]
                    nc.vector.tensor_scalar(a, a, mv[:, ds(b * 2, 1)], rstd[:, ds(b, 1)], ALU.subtract, ALU.mult).then_inc(s_c, 1)
                    v.wait_ge(s_c, b * 5 + 1)
                    nc.vector.tensor_tensor(a, a, gam[:, :], ALU.mult).then_inc(s_c, 1)
                    v.wait_ge(s_c, b * 5 + 2)
                    nc.vector.tensor_tensor(a, a, bet[:, :], ALU.add).then_inc(s_c, 1)
                    v.wait_ge(s_c, b * 5 + 3)
                    nc.vector.scalar_tensor_tensor(out=x, in0=a, scalar=0.0, in1=x, op0=ALU.max, op1=ALU.add).then_inc(s_c, 1)
                    v.wait_ge(s_c, b * 5 + 4)
                    nc.vector.bn_stats(st2[:, ds(b * 6, 6)], x).then_inc(s_c, 1)
                v.wait_ge(s_c, 5 * NB)
                ln_finish(nc, v, mv2, st2, rstd2, s_st2, s_var2, s_std2, 1e-5)
                with v.Fori(0, NB) as b:
                    nc.vector.tensor_scalar(C.acc3[:, ds(b * 2 * D, D)], C.X[:, ds(b * D, D)], mv2[:, ds(b * 2, 1)], rstd2[:, ds(b, 1)],
                                            ALU.subtract, ALU.mult).then_inc(s_n, 1)
                v.wait_ge(s_n, NB)

            @block.scalar
            def _(act):
                ln_sqrt(nc, act, rstd, s_var, s_std)
                ln_sqrt(nc, act, rstd2, s_var2, s_std2)

        with ExitStack() as c2:
            sb2, ps2, _ = alloc(nc, c2, "dense_")
            p_t = ps2("p_td", [P, 512]); p_h = ps2("p_hd", [P, 2, 512]); p_l = ps2("p_ld", [P, 512])
            with nc.Block() as block:
                @block.sync
                def _(sp):
                    sp.dma_start(w1[:, :, :], A["fW1"].rearrange("(c p) f -> p c f", p=P)).then_inc(s_wd, 16)
                    sp.dma_start(b1[:, :], A["fb1"].rearrange("(c p) -> p c", p=P), allow_slow_non_contiguous=True).then_inc(s_wd, 16)
                    sp.dma_start(wgt[:, :, :], A["fWg"].rearrange("(c p) e -> p c e", p=P)).then_inc(s_wd, 16)
                    sp.dma_start(bg[:, :], A["fbg"].partition_broadcast(P)).then_inc(s_wd, 16)
                    sp.dma_start(bd[:, :], A["fbd"]).then_inc(s_wd, 16)

                    def back(b, k):
                        sp.wait_ge(s_hc, b * 2 + 2)
                        sp.dma_start(C.hT_d[ds(b * P, P), :], HT[k][:, :]).then_inc(s_u[k], 16)
                    skewed(sp, NB, 2, lambda b, k: None, back)
                    sp.wait_ge(s_u[0], 16 * 2 * ((NB + 1) // 2))
                    sp.wait_ge(s_u[1], 16 * 2 * (NB // 2))

                @block.vector
                def _(v):
                    def front(b, k):
                        nc.vector.tensor_scalar(xn[k][:, :], C.acc3[:, ds(b * 2 * D, D)], 1.0, None, ALU.mult).then_inc(s_xn, 1)

                    def back(b, k):
                        v.wait_ge(s_l, b + 1)
                        nc.vector.tensor_tensor(lg[:, ds(b, 1), :].rearrange("p a e -> p (a e)"), p_l[:, 0:NE], bg[:, :], ALU.add).then_inc(s_lc, 1)

                    v.wait_ge(s_wd, 80)
                    skewed(v, NB, 2, front, back)
                    v.wait_ge(s_lc, NB)
                    for b in range(NB):
                        nc.vector.max(mx8[:, b, :], lg[:, b, :]).then_inc(s_m, 1)
                    v.wait_ge(s_m, NB)
                    for b in range(NB):
                        nc.vector.max_index(ix8[:, b, :], mx8[:, b, :], lg[:, b, :]).then_inc(s_m, 1)
                    nc.vector.tensor_tensor(ex[:, :, :], lg[:, :, :], mx8[:, :, 0:1].broadcast_to([P, NB, NE]), ALU.subtract).then_inc(s_e0, 1)
                    v.wait_ge(s_m, 2 * NB)
                    nc.vector.tensor_copy(ixf[:, :], ix8[:, :, 0]).then_inc(s_pr, 1)
                    v.wait_ge(s_e1, 1)
                    nc.vector.tensor_reduce(sm[:, :], ex[:, :, :], AX.X, ALU.add).then_inc(s_pr, 1)
                    v.wait_ge(s_pr, 2)
                    nc.vector.reciprocal(sm[:, :], sm[:, :]).then_inc(s_pr, 1)
                    pr3 = pr[:, :].rearrange("p (b e) -> p b e", e=NE)
                    nc.vector.tensor_tensor(pr3, C.iota[:, 0:NE].unsqueeze(1).broadcast_to([P, NB, NE]),
                                            ixf[:, :].unsqueeze(2).broadcast_to([P, NB, NE]), ALU.is_equal).then_inc(s_pr, 1)
                    v.wait_ge(s_pr, 4)
                    nc.vector.tensor_tensor(pr3, pr3, sm[:, :].unsqueeze(2).broadcast_to([P, NB, NE]), ALU.mult).then_inc(s_pr, 1)

                @block.scalar
                def _(act):
                    act.wait_ge(s_wd, 80)

                    def back(b, k):
                        act.wait_ge(s_t, b + 1)
                        nc.scalar.copy(xT[:, :], p_t[:, 0:KC * P]).then_inc(s_tc, 1)
                        for a in range(2):
                            act.wait_ge(s_h, b * 2 + a + 1)
                            if a == 0 and (not isinstance(b, int) or b >= 2):
                                act.wait_ge(s_u[k], ((NB + 1) // 2 if k == 0 else NB // 2) * 16 + (b - k) * 8)
                            for c in range(4):
                                q = a * 4 + c
                                t = nc.scalar.activation(HT[k][:, q * P:q * P + P], p_h[:, a, c * P:c * P + P], ACT.Gelu, bias=b1[:, q:q + 1])
                            t.then_inc(s_hc, 1)

                    skewed(act, NB, 2, lambda b, k: None, back, peel=2)
                    act.wait_ge(s_e0, 1)
                    nc.scalar.activation(ex[:, :, :], ex[:, :, :], ACT.Exp).then_inc(s_e1, 1)

                @block.tensor
                def _(pe):
                    pe.wait_ge(s_wd, 80)

                    def back(b, k):
                        later = not isinstance(b, int) or b > 0
                        pe.wait_ge(s_xn, b + 1)
                        if later:
                            pe.wait_ge(s_tc, b)
                        for c in range(KC):
                            t = nc.tensor.transpose(p_t[:, c * P:c * P + P], xn[k][:, c * P:c * P + P], C.ident[:, :])
                        t.then_inc(s_t, 1)
                        pe.wait_ge(s_tc, b + 1)
                        for a in range(2):
                            if later:
                                pe.wait_ge(s_hc, b * 2 + a - 1)
                            for c in range(4):
                                q = a * 4 + c
                                for kc in range(KC):
                                    t = nc.tensor.matmul(p_h[:, a, c * P:c * P + P], w1[:, kc, q * P:q * P + P], xT[:, kc * P:kc * P + P], start=(kc == 0), stop=(kc == KC - 1))
                            t.then_inc(s_h, 1)
                        pe.wait_ge(s_hc, b * 2 + 2)
                        if later:
                            pe.wait_ge(s_lc, b)
                        for q in range(FC):
                            t = nc.tensor.matmul(p_l[:, 0:NE], HT[k][:, q * P:q * P + P], wgt[:, q, :], start=(q == 0), stop=(q == FC - 1))
                        t.then_inc(s_l, 1)

                    skewed(pe, NB, 2, lambda b, k: None, back, peel=2)

        with ExitStack() as c2:
            sb2, ps2, sem2 = alloc(nc, c2, "dense_")
            Wd = sb2("Wd", [P, NE // 2, FC, D])
            prT = [sb2(f"prT{k}", [NE, P]) for k in range(2)]
            prs = [sb2(f"prs{k}", [P, NE]) for k in range(2)]
            p_y = ps2("p_yd", [P, 4, 512]); p_p = ps2("p_pd", [P, 512])
            s_hl = [sem2(f"s_hl{k}") for k in range(2)]; s_wh = sem2("s_wh"); s_ps = sem2("s_ps")
            for half in range(2):
                with nc.Block() as block:
                    s_hl = [sem2(f"s_hl{half}{k}") for k in range(2)]; s_wh = sem2(f"s_wh{half}"); s_yy = sem2(f"s_yy{half}"); s_yc = sem2(f"s_yc{half}")
                    s_ps = sem2(f"s_ps{half}"); s_pT = sem2(f"s_pT{half}"); s_pTc = sem2(f"s_pTc{half}"); s_bb = sem2(f"s_bb{half}")

                    @block.sync
                    def _(sp):
                        sp.dma_start(Wd[:, :, :, :], A["fWd"][half * 4 * F:(half + 1) * 4 * F, :].rearrange("(e c p) d -> p e c d", c=FC, p=P)).then_inc(s_wh, 16)

                        def body(b, k):
                            if not isinstance(b, int) or b >= 2:
                                sp.wait_ge(s_yy, (b - 1) * 2)
                            sp.dma_start(HT[k][:, :], C.hT_d[ds(b * P, P), :]).then_inc(s_hl[k], 16)
                        skewed(sp, NB, 2, lambda b, k: None, body, peel=2)

                    @block.vector
                    def _(v):
                        def front(b, k):
                            nc.vector.tensor_scalar(prs[k][:, :], pr[:, ds(b * NE, NE)], 1.0, None, ALU.mult).then_inc(s_ps, 1)

                        def back(b, k):
                            x = C.X[:, ds(b * D, D)]
                            for m in range(2):
                                v.wait_ge(s_yy, b * 2 + m + 1)
                                for q in range(2):
                                    e = half * 4 + m * 2 + q
                                    nc.vector.scalar_tensor_tensor(out=x, in0=p_y[:, m, q * D:q * D + D], scalar=pr[:, ds(b * NE + e, 1)],
                                                                   in1=x, op0=ALU.mult, op1=ALU.add).then_inc(s_yc, 1)
                                    v.wait_ge(s_yc, b * 4 + m * 2 + q + 1)
                            if half == 0:
                                v.wait_ge(s_bb, b + 1)
                                nc.vector.tensor_tensor(x, x, p_y[:, 2, 0:D], ALU.add).then_inc(s_ya, 1)
                                v.wait_ge(s_ya, b + 1)

                        skewed(v, NB, 2, front, back)

                    @block.scalar
                    def _(act):
                        if half == 0:
                            def front(b, k):
                                act.wait_ge(s_pT, b + 1)
                                nc.scalar.copy(prT[k][:, :], p_p[0:NE, 0:P]).then_inc(s_pTc, 1)
                            skewed(act, NB, 2, front, lambda b, k: None)

                    @block.tensor
                    def _(pe):
                        pe.wait_ge(s_wh, 16)

                        def front(b, k):
                            if half:
                                return
                            pe.wait_ge(s_ps, b + 1)
                            if not isinstance(b, int) or b > 0:
                                pe.wait_ge(s_pTc, b)
                            nc.tensor.transpose(p_p[0:NE, 0:P], prs[k][:, :], C.ident[:, :]).then_inc(s_pT, 1)

                        def back(b, k):
                            later = not isinstance(b, int) or b > 0
                            pe.wait_ge(s_hl[k], (b - k) * 8 + 16)
                            for m in range(2):
                                if later:
                                    pe.wait_ge(s_yc, b * 4 - 2 + m * 2)
                                for c in range(FC):
                                    for q in range(2):
                                        t = nc.tensor.matmul(p_y[:, m, q * D:q * D + D], HT[k][:, c * P:c * P + P], Wd[:, m * 2 + q, c, :],
                                                             start=(c == 0 and q == 0), stop=(c == FC - 1), skip_group_check=True)
                                t.then_inc(s_yy, 1)
                            if half == 0:
                                pe.wait_ge(s_pTc, b + 1)
                                if later:
                                    pe.wait_ge(s_ya, b)
                                nc.tensor.matmul(p_y[:, 2, 0:D], prT[k][:, :], bd[:, :], start=True, stop=True).then_inc(s_bb, 1)

                        skewed(pe, NB, 2, front, back, peel=2)

        with nc.Block() as block:
            @block.sync
            def _(sp):
                sp.dma_start(out[0:(NB - 1) * P, :].rearrange("(b p) d -> p b d", p=P),
                             C.X[:, 0:(NB - 1) * D].rearrange("p (b d) -> p b d", d=D)).then_inc(s_out, 16)
                sp.dma_start(out[(NB - 1) * P:N, :], C.X[0:TAIL, (NB - 1) * D:NB * D]).then_inc(s_out, 16)
                sp.wait_ge(s_out, 32)


def build(nc, A, out):
    C = Consts()
    C.edge_rows = P * EC + EG

    def dram(name, shape, dt=F32):
        return nc.dram_tensor(name, shape, dt, kind="Internal").ap()

    C.edges = dram("edges_d", (C.edge_rows, 2), I32)
    C.gtab_d = dram("gtab_d", (2, GC * P), I32)
    C.tab1 = dram("tab1_d", (NP, TW))
    C.tab2 = dram("tab2_d", (NP, TW))
    C.tab3 = dram("tab3_d", (NP, 2 * D))
    C.u_d = dram("u_d", (NP, D))
    C.hT_d = dram("hT_d", (NP, F))
    C.ffn_in = dram("ffn_in_d", (NE * CS, D))
    C.ffn_out = dram("ffn_out_d", (NE * CS, D))
    with ExitStack() as ctx:
        sb, ps, sem = alloc(nc, ctx)
        C.X = sb("X", [P, NB * D])
        C.ident = sb("ident", [P, P]); C.bigi = sb("bigi", [P, P], BF16); C.identb = sb("identb", [P, P], BF16); C.iota = sb("iota", [P, P]); C.lab = sb("lab", [P, NB])
        C.gofs = sb("gofs", [1, GC * P], I32); C.gblk = sb("gblk_r", [1, GC * P], I32)
        C.gblkb = sb("gblkb", [P, GC * P], I32); C.gbase = sb("gbase", [P, GC * P])
        C.gate = sb("gate", [P, NB]); C.back = sb("back", [P, NB], I32)
        with ExitStack() as first:
            sb, ps, sem = alloc(nc, first)
            C.em = sb("em", [P, NB * 2 * H])
            C.ler = sb("ler", [P, NB * 2 * H])
            C.bg3 = sb("bg3", [P, NB * 3 * 2 * H], BF16)
            C.near = sb("near", [P, 1], I32)
            C.acc = sb("acc", [P, NB * H * HW])
            stage_setup(nc, C, A)
            stage_encode(nc, C, A)
            stage_scores(nc, C, C.tab1, 1)
            stage_attend_near(nc, C, C.tab1, 1)
            stage_attend(nc, C, C.tab1, 1)
            stage_between(nc, C, A)
            stage_scores(nc, C, C.tab2, 2)
            stage_attend_near(nc, C, C.tab2, 2)
            stage_attend(nc, C, C.tab2, 2)
            stage_route(nc, C, A)
        stage_experts(nc, C, A)
        with ExitStack() as second:
            sb, ps, sem = alloc(nc, second)
            C.acc3 = sb("acc3", [P, NB * 2 * D])
            with ExitStack() as third:
                sb, ps, sem = alloc(nc, third)
                C.wr = sb("wr", [P, NB * D])
                stage_gated_in(nc, C, A)
                stage_gated(nc, C)
            stage_dense(nc, C, A, out)


def laid_out(inputs):
    a = {k: np.asarray(v) for k, v in inputs.items()}

    def heads(al, ar):
        m = np.zeros((D, 2 * H), np.float32)
        for h in range(H):
            m[h * HD:(h + 1) * HD, h] = al[h]
            m[h * HD:(h + 1) * HD, H + h] = ar[h]
        return m

    return {
        "x": a["x"], "src": a["src"], "dst": a["dst"], "node_type_24": a["node_type_24"],
        "embT": a["L0_gnn_emb"].T, "le_W1T": a["L0_gnn_le_W1"].T, "le_b1": a["L0_gnn_le_b1"], "ln_g": a["L0_gnn_ln_g"],
        "ln_b": a["L0_gnn_ln_b"], "le_W2T": a["L0_gnn_le_W2"].T, "le_b2": a["L0_gnn_le_b2"],
        "W1": a["L0_gnn_W1"], "W1T": a["L0_gnn_W1"].T, "alr1": heads(a["L0_gnn_al1"], a["L0_gnn_ar1"]),
        "b1": a["L0_gnn_b1"], "W2": a["L0_gnn_W2"], "W2T": a["L0_gnn_W2"].T, "alr2": heads(a["L0_gnn_al2"], a["L0_gnn_ar2"]), "b2": a["L0_gnn_b2"],
        "gate_w": a["L0_ffn_gate_w"], "gate_b": a["L0_ffn_gate_b"], "ew1": a["L0_ffn_w1"].reshape(NE * D, F), "eb1": a["L0_ffn_b1"],
        "ew2": a["L0_ffn_w2"].reshape(NE * F, D), "eb2": a["L0_ffn_b2"],
        "w3": np.concatenate([a["L1_gnn_W_w"], a["L1_gnn_U_w"], a["L1_gnn_V_w"]], axis=1),
        "b3": np.concatenate([a["L1_gnn_W_b"], a["L1_gnn_U_b"], a["L1_gnn_V_b"]]),
        "attn_l": a["L1_gnn_attn_l"], "attn_r": a["L1_gnn_attn_r"], "gamma": a["L1_gnn_gamma"], "beta": a["L1_gnn_beta"],
        "fW1": a["L1_ffn_W1"], "fb1": a["L1_ffn_b1"], "fWg": a["L1_ffn_Wg"], "fbg": a["L1_ffn_bg"],
        "fWd": a["L1_ffn_Wd"].reshape(NE * F, D), "fbd": a["L1_ffn_bd"],
    }


def kernel(**inputs):
    import concourse.bacc as _bacc
    from concourse import mybir as _mybir
    from concourse.bass_utils import run_bass_kernel_spmd as _run

    nc = _bacc.Bacc("TRN2", target_bir_lowering=False, num_devices=1)
    arrays, args = {}, {}
    for name, a in laid_out(inputs).items():
        a = np.ascontiguousarray(a)
        arrays[f"in_{name}"] = a
        args[name] = nc.dram_tensor(f"in_{name}", a.shape, _mybir.dt.from_np(a.dtype), kind="ExternalInput").ap()
    out = nc.dram_tensor("out_0", (N, D), _mybir.dt.float32, kind="ExternalOutput").ap()
    build(nc, args, out)
    r = _run(nc, [arrays], core_ids=[0])
    return r.results[0]["out_0"]
```

```python
from contextlib import ExitStack

import numpy as np

import concourse.bass as bass
from concourse import mybir

F32 = mybir.dt.float32
BF16 = mybir.dt.bfloat16
I32 = mybir.dt.int32
U32 = mybir.dt.uint32
ALU = mybir.AluOpType
ACT = mybir.ActivationFunctionType
AX = mybir.AxisListType
ds = bass.ds

P = 128
N = 3125
D = 256
NB = -(-N // P)
NP = NB * P
TAIL = N - (NB - 1) * P
E = 100000
EC = -(-E // P)
ET = 4
EG = ET * P
NG = (E + NB * (EG - 1)) // EG
UN = 4
NG = -(-NG // UN) * UN
GC = -(-NG // P)
H = 4
HD = D // H
HW = HD + 1
NC = 24
F = 1024
FC = F // P
KC = D // P
NE = 8
CAP = max(1, -(-5 * N // (4 * NE)))
CS = -(-CAP // P) * P
NT = (N + NE * (P - 1)) // P
TW = D + 3 * H
SPREAD = 20.0
SLOPE = 0.2
BIG = float(2.0 ** 100)


def skewed(eng, count, unroll, front, back, peel=0):
    def step(n, k):
        front(n + 1, (k + 1) % unroll)
        back(n, k)

    front(0, 0)
    for n in range(peel):
        step(n, n % unroll)
    whole = (count - 1) // unroll
    with eng.Fori(peel // unroll, whole) as i:
        for k in range(unroll):
            step(i * unroll + k, k)
    for n in range(whole * unroll, count - 1):
        step(n, n % unroll)
    back(count - 1, (count - 1) % unroll)


def steps(eng, count, unroll, step):
    first = 2 * unroll
    rounds = (count - 2) // unroll
    for n in range(first):
        step(n, n % unroll)
    with eng.Fori(2, rounds) as i:
        for k in range(unroll):
            step(i * unroll + k, k)
    for n in range(rounds * unroll, count):
        step(n, n % unroll)


def from_step(n, eng, sem, g, value):
    if not isinstance(g, int) or g >= n:
        eng.wait_ge(sem, value)


def hold(eng, sem, value, gate):
    eng.wait_ge(sem, value)
    eng.sem_inc(gate, 1)


class Consts:
    pass


def alloc(nc, ctx, stage=""):
    def sb(name, shape, dt=F32):
        return ctx.enter_context(nc.sbuf_tensor(stage + name, shape, dt))

    def ps(name, shape, dt=F32):
        return ctx.enter_context(nc.psum_tensor(stage + name, shape, dt))

    sems = []

    def clear():
        if sems:
            nc.clear_and_free_semaphores(sems)
            nc.all_engine_barrier()

    ctx.callback(clear)

    def sem(name):
        sems.append(nc.alloc_semaphore(stage + name))
        return sems[-1]

    return sb, ps, sem


def ln_stats(nc, v, act_std, X, mv, st, rstd, s_st, s_var, s_std, eps):
    with v.Fori(0, NB) as b:
        nc.vector.bn_stats(st[:, ds(b * 6, 6)], X[:, ds(b * D, D)]).then_inc(s_st, 1)
    v.wait_ge(s_st, NB)
    ln_finish(nc, v, mv, st, rstd, s_st, s_var, s_std, eps, NB)


def ln_finish(nc, v, mv, st, rstd, s_st, s_var, s_std, eps, base=0):
    for b in range(NB):
        nc.vector.bn_aggr(mv[:, b * 2:b * 2 + 2], st[:, b * 6:b * 6 + 6]).then_inc(s_st, 1)
    v.wait_ge(s_st, base + NB)
    var = mv[:, :].rearrange("p (b t) -> p b t", t=2)[:, :, 1]
    nc.vector.tensor_scalar(rstd[:, :], var, float(eps), None, ALU.add).then_inc(s_var, 1)
    v.wait_ge(s_std, 1)
    nc.vector.reciprocal(rstd[:, :], rstd[:, :]).then_inc(s_var, 1)
    v.wait_ge(s_var, 2)


def ln_sqrt(nc, act, rstd, s_var, s_std):
    act.wait_ge(s_var, 1)
    nc.scalar.activation(rstd[:, :], rstd[:, :], ACT.Sqrt).then_inc(s_std, 1)


def stage_setup(nc, C, A):
    with ExitStack() as ctx:
        sb, ps, sem = alloc(nc, ctx, "setup_")
        srcs = sb("srcs", [P, EC], I32)
        dsts = sb("dsts", [P, EC], I32)
        pairs = sb("pairs", [P, EC, 2], I32)
        padpair = sb("padpair", [1, EG, 2], I32)
        dstf = sb("dstf", [P, EC])
        dstn = sb("dstn", [P, EC], I32)
        below = C.below
        junk = sb("junk", [P, 2, EC])
        onesq = sb("onesq", [P, P])
        first = C.first
        cnt = sb("cnt", [P, NB])
        cnti = sb("cnti", [P, NB], I32)
        ng = sb("ng", [P, NB])
        gend = sb("gend", [P, NB])
        gfirst = sb("gfirst", [P, NB])
        shift = sb("shift", [P, NB])
        gidi = sb("gidi", [P, GC], I32)
        gid = sb("gid", [P, GC])
        ge = sb("ge", [P, GC, NB])
        gblk = sb("gblk", [P, GC])
        goff = sb("goff", [P, GC])
        gtab = sb("gtab", [P, 2, GC], I32)
        iotai = sb("iotai", [P, P], I32)
        labi = sb("labi", [P, NB], I32)
        pt = ps("pt", [P, 512])
        s_x = sem("s_x"); s_e = sem("s_e"); s_lab = sem("s_lab"); s_pool = sem("s_pool")
        s_v = sem("s_v"); s_pr = sem("s_pr"); s_cnt = sem("s_cnt"); s_tot = sem("s_tot")
        s_pair = sem("s_pair"); s_gt = sem("s_gt"); s_gtd = sem("s_gtd"); s_tab = sem("s_tab")
        s_z = sem("s_z"); s_next = sem("s_next"); s_desc = sem("s_desc")
        full = E // EC
        rest = E - full * EC

        with nc.Block() as block:
            @block.sync
            def _(sp):
                sp.wait_ge(s_z, 4)
                sp.dma_start(dsts[0:full, :], A["dst"][0:full * EC].rearrange("(p c) -> p c", c=EC)).then_inc(s_e, 16)
                sp.dma_start(dsts[full:full + 1, 0:rest], A["dst"][full * EC:E].rearrange("(p c) -> p c", p=1)).then_inc(s_e, 16)
                sp.dma_start(srcs[0:full, :], A["src"][0:full * EC].rearrange("(p c) -> p c", c=EC)).then_inc(s_e, 16)
                sp.dma_start(srcs[full:full + 1, 0:rest], A["src"][full * EC:E].rearrange("(p c) -> p c", p=1)).then_inc(s_e, 16)
                sp.dma_start(dstn[0:full, :], A["dst"][1:full * EC + 1].rearrange("(p c) -> p c", c=EC)).then_inc(s_next, 16)
                sp.dma_start(dstn[full:full + 1, 0:rest - 1], A["dst"][full * EC + 1:E].rearrange("(p c) -> p c", p=1)).then_inc(s_next, 16)
                sp.wait_ge(s_pr, 2)
                sp.dma_start(C.edges[0:P * EC, :].rearrange("(p c) t -> p (c t)", c=EC), pairs[:, :, :].rearrange("p c t -> p (c t)")).then_inc(s_pair, 16)
                sp.dma_start(C.edges[P * EC:C.edge_rows, :].rearrange("(a c) t -> a (c t)", a=1), padpair[0:1, 0:C.edge_rows - P * EC, :].rearrange("p c t -> p (c t)")).then_inc(s_pair, 16)
                sp.wait_ge(s_gt, 1)
                for t in range(2):
                    sp.dma_start(C.gtab_d[t, :].rearrange("(c p) -> p c", p=P), gtab[:, t, :], allow_slow_non_contiguous=True).then_inc(s_gtd, 16)
                sp.wait_ge(s_gtd, 32)
                sp.dma_start(C.gofs[0:1, :], C.gtab_d[1:2, :]).then_inc(s_tab, 16)
                sp.dma_start(C.gblk[0:1, :], C.gtab_d[0:1, :]).then_inc(s_tab, 16)
                sp.dma_start(C.gblkb[:, :], C.gtab_d[0, :].partition_broadcast(P)).then_inc(s_tab, 16)
                sp.wait_ge(s_pair, 32)
                sp.wait_ge(s_tab, 48)

            @block.scalar
            def _(act):
                act.wait_ge(s_pool, 3)
                act.dma_start(C.X[:, 0:(NB - 1) * D].rearrange("p (b d) -> p b d", d=D),
                              A["x"][0:(NB - 1) * P, :].rearrange("(b p) d -> p b d", p=P)).then_inc(s_x, 16)
                act.dma_start(C.X[0:TAIL, (NB - 1) * D:NB * D], A["x"][(NB - 1) * P:N, :]).then_inc(s_x, 16)
                act.dma_start(labi[:, 0:NB - 1], A["node_type_24"][0:(NB - 1) * P].rearrange("(b p) -> p b", p=P), allow_slow_non_contiguous=True).then_inc(s_lab, 16)
                act.dma_start(labi[0:TAIL, NB - 1:NB], A["node_type_24"][(NB - 1) * P:N].rearrange("(p a) -> p a", a=1)).then_inc(s_lab, 16)
                act.wait_ge(s_x, 32)

            @block.gpsimd
            def _(gp):
                nc.gpsimd.memset(C.X[:, (NB - 1) * D:NB * D], 0.0).then_inc(s_pool, 1)
                nc.gpsimd.memset(labi[:, :], 0).then_inc(s_pool, 1)
                nc.gpsimd.memset(C.ident[:, :], 0.0).then_inc(s_pool, 1)
                nc.gpsimd.iota(iotai[:, :], pattern=[[1, P]], base=0, channel_multiplier=0).then_inc(s_pool, 1)
                nc.gpsimd.iota(gidi[:, :], pattern=[[P, GC]], base=0, channel_multiplier=1).then_inc(s_pool, 1)
                gp.wait_ge(s_pool, 5)
                nc.gpsimd.affine_select(out=C.ident[:, :], in_=C.ident[:, :], compare_op=ALU.not_equal, fill=1.0,
                                        base=0, pattern=[[-1, P]], channel_multiplier=1).then_inc(s_pool, 1)

            @block.vector
            def _(v):
                nc.vector.memset(dsts[:, :], -1).then_inc(s_z, 1)
                nc.vector.memset(srcs[:, :], 0).then_inc(s_z, 1)
                nc.vector.memset(padpair[:, :, :], -1).then_inc(s_z, 1)
                nc.vector.memset(dstn[:, :], N).then_inc(s_z, 1)
                nc.vector.memset(onesq[:, :], 1.0).then_inc(s_v, 1)
                nc.vector.memset(below[:, 0:1], 0.0).then_inc(s_v, 1)
                v.wait_ge(s_z, 3)
                nc.vector.memset(padpair[:, :, 0], 0).then_inc(s_pr, 1)
                v.wait_ge(s_pool, 6)
                nc.vector.tensor_copy(C.iota[:, :], iotai[:, :]).then_inc(s_v, 1)
                nc.vector.tensor_copy(gid[:, :], gidi[:, :]).then_inc(s_v, 1)
                nc.vector.tensor_scalar(C.bigi[:, :], C.ident[:, :], BIG, None, ALU.mult).then_inc(s_v, 1)
                v.wait_ge(s_lab, 32)
                nc.vector.tensor_copy(C.lab[:, :], labi[:, :]).then_inc(s_v, 1)
                v.wait_ge(s_e, 64)
                nc.vector.tensor_copy(dstf[:, :], dsts[:, :]).then_inc(s_v, 1)
                nc.vector.tensor_copy(pairs[:, :, 1], dsts[:, :]).then_inc(s_v, 1)
                v.wait_ge(s_v, 8)
                nc.vector.tensor_copy(pairs[:, :, 0], srcs[:, :]).then_inc(s_pr, 1)
                nc.vector.tensor_scalar(junk[:, 0, :], dstf[:, :], 0.0, 0.0, ALU.is_ge, ALU.add, accum_out=below[:, NB:NB + 1]).then_inc(s_v, 1)
                for b in range(1, NB):
                    v.wait_ge(s_v, 9 + (b - 1) // 1)
                    nc.vector.tensor_scalar(junk[:, 0, :], dstf[:, :], float(P * b), 0.0, ALU.is_ge, ALU.add,
                                            accum_out=below[:, b:b + 1]).then_inc(s_v, 1)
                v.wait_ge(s_v, 8 + NB)
                nc.vector.tensor_tensor(below[:, 1:NB], below[:, NB:NB + 1].broadcast_to([P, NB - 1]), below[:, 1:NB], ALU.subtract).then_inc(s_cnt, 1)
                v.wait_ge(s_next, 32)
                nc.vector.tensor_tensor(junk[:, 1, :], dsts[:, :], dstn[:, :], ALU.is_gt).then_inc(s_desc, 1)
                v.wait_ge(s_desc, 1)
                nc.vector.tensor_reduce(below[:, NB + 1:NB + 2], junk[:, 1, :], AX.X, ALU.add).then_inc(s_cnt, 1)
                v.wait_ge(s_tot, 1)
                nc.vector.tensor_scalar(C.unsorted[:, :], pt[:, NB + 1:NB + 2], 1.0, None, ALU.min).then_inc(s_desc, 1)
                nc.vector.tensor_copy(first[:, :], pt[:, 0:NB + 1]).then_inc(s_v, 1)
                base = 8 + NB
                v.wait_ge(s_v, base + 1)
                nc.vector.tensor_tensor(cnt[:, :], first[:, 1:NB + 1], first[:, 0:NB], ALU.subtract).then_inc(s_v, 1)
                v.wait_ge(s_v, base + 2)
                nc.vector.tensor_scalar(cnti[:, :], cnt[:, :], float(EG - 1), None, ALU.add).then_inc(s_v, 1)
                v.wait_ge(s_v, base + 3)
                nc.vector.tensor_scalar(cnti[:, :], cnti[:, :], EG.bit_length() - 1, None, ALU.arith_shift_right).then_inc(s_v, 1)
                v.wait_ge(s_v, base + 4)
                nc.vector.tensor_copy(ng[:, :], cnti[:, :]).then_inc(s_v, 1)
                v.wait_ge(s_v, base + 5)
                nc.vector.tensor_tensor_scan(gend[:, :], ng[:, :], ng[:, :], 0.0, ALU.add, ALU.bypass).then_inc(s_v, 1)
                v.wait_ge(s_v, base + 6)
                nc.vector.tensor_tensor(gfirst[:, :], gend[:, :], ng[:, :], ALU.subtract).then_inc(s_v, 1)
                v.wait_ge(s_v, base + 7)
                nc.vector.scalar_tensor_tensor(out=shift[:, :], in0=gfirst[:, :], scalar=float(-EG), in1=first[:, 0:NB],
                                               op0=ALU.mult, op1=ALU.add).then_inc(s_v, 1)
                v.wait_ge(s_v, base + 8)
                nc.vector.tensor_tensor(ge[:, :, :], gid[:, :].unsqueeze(2).broadcast_to([P, GC, NB]),
                                        gfirst[:, :].unsqueeze(1).broadcast_to([P, GC, NB]), ALU.is_ge).then_inc(s_v, 1)
                v.wait_ge(s_v, base + 9)
                nc.vector.tensor_reduce(gblk[:, :], ge[:, :, :], AX.X, ALU.add).then_inc(s_v, 1)
                nc.vector.tensor_tensor(cnt[:, 1:NB], shift[:, 1:NB], shift[:, 0:NB - 1], ALU.subtract).then_inc(s_v, 1)
                nc.vector.tensor_copy(cnt[:, 0:1], shift[:, 0:1]).then_inc(s_v, 1)
                v.wait_ge(s_v, base + 12)
                nc.vector.tensor_tensor(ge[:, :, :], ge[:, :, :], cnt[:, :].unsqueeze(1).broadcast_to([P, GC, NB]), ALU.mult).then_inc(s_v, 1)
                nc.vector.tensor_scalar(gtab[:, 0, :], gblk[:, :], -1.0, None, ALU.add).then_inc(s_v, 1)
                v.wait_ge(s_v, base + 14)
                nc.vector.tensor_reduce(goff[:, :], ge[:, :, :], AX.X, ALU.add).then_inc(s_v, 1)
                v.wait_ge(s_v, base + 15)
                nc.vector.scalar_tensor_tensor(out=goff[:, :], in0=gid[:, :], scalar=float(EG), in1=goff[:, :],
                                               op0=ALU.mult, op1=ALU.add).then_inc(s_v, 1)
                v.wait_ge(s_v, base + 16)
                nc.vector.tensor_scalar(gtab[:, 1, :], goff[:, :], float(E), None, ALU.min).then_inc(s_gt, 1)
                v.wait_ge(s_tab, 48)
                nc.vector.tensor_scalar(C.gbase[:, :], C.gblkb[:, :], float(P), None, ALU.mult).then_inc(s_v, 1)
                nc.vector.tensor_copy(C.identb[:, :], C.ident[:, :]).then_inc(s_v, 1)

            @block.tensor
            def _(pe):
                pe.wait_ge(s_v, 2)
                pe.wait_ge(s_cnt, 2)
                nc.tensor.matmul(pt[:, 0:NB + 2], onesq[:, :], below[:, :], start=True, stop=True).then_inc(s_tot, 1)


def stage_sort(nc, C, A):
    with ExitStack() as ctx:
        sb, ps, sem = alloc(nc, ctx, "sort_")
        pairs = sb("pairs", [P, EC, 2], I32)
        blki = sb("blki", [P, EC], I32); blk = sb("blk", [P, EC])
        ei = sb("ei", [P, EC], I32); place = sb("place", [P, EC]); placei = sb("placei", [P, EC], I32)
        mine = sb("mine", [P, EC]); run = sb("run", [P, EC])
        cnt = sb("cnt", [P, NB]); base = sb("base", [P, NB]); tri = sb("tri", [P, P])
        to = [sb(f"to{k}", [P, 1], I32) for k in range(2)]
        pair = [sb(f"pair{k}", [P, 2], I32) for k in range(2)]
        p_base = ps("p_base", [P, 512])
        s_pairs = sem("s_pairs"); s_e = sem("s_e"); s_tri = sem("s_tri"); s_cnt = sem("s_cnt"); s_base = sem("s_base"); s_v = sem("s_v")
        s_mine = sem("s_mine"); s_run = sem("s_run"); s_place = sem("s_place"); s_done = sem("s_done")
        s_cp = sem("s_cp"); s_sc = [sem(f"s_sc{k}") for k in range(2)]; s_go = sem("s_go")

        def if_unsorted(eng):
            return eng.If(eng.value_load(C.unsorted[0:1, 0:1], min_val=0, max_val=1) == 1)

        with nc.Block() as block:
            @block.sync
            def _(sp):
                with if_unsorted(sp):
                    sp.dma_start(pairs[:, :, :].rearrange("p c t -> p (c t)"), C.edges[0:P * EC, :].rearrange("(p c) t -> p (c t)", c=EC)).then_inc(s_pairs, 16)

            @block.gpsimd
            def _(gp):
                with if_unsorted(gp):
                    nc.gpsimd.iota(ei[:, :], pattern=[[1, EC]], base=0, channel_multiplier=EC).then_inc(s_e, 1)
                    nc.gpsimd.memset(tri[:, :], 1.0).then_inc(s_tri, 1)
                    gp.wait_ge(s_tri, 1)
                    nc.gpsimd.affine_select(out=tri[:, :], in_=tri[:, :], compare_op=ALU.is_gt, fill=0.0, base=0,
                                            pattern=[[1, P]], channel_multiplier=-1).then_inc(s_tri, 1)
                    gp.wait_ge(s_done, 1)

                    def scatter(c, k):
                        nc.gpsimd.tensor_copy(to[k][:, :], placei[:, ds(c, 1)]).then_inc(s_cp, 1)
                        nc.gpsimd.tensor_copy(pair[k][:, :], pairs[:, ds(c, 1), :].rearrange("p c t -> p (c t)")).then_inc(s_cp, 1)
                        hold(gp, s_cp, c * 2 + 2, s_go)
                        gp.indirect_dma_start(out=C.edges[:, :], out_offset=bass.IndirectOffsetOnAxis(ap=to[k][:, 0:1], axis=0),
                                              in_=pair[k][:, :], in_offset=None).then_inc(s_sc[k], 16)

                    scatter(0, 0)
                    scatter(1, 1)
                    with gp.Fori(1, EC // 2) as i:
                        for k in range(2):
                            hold(gp, s_sc[k], i * 16, s_go)
                            scatter(i * 2 + k, k)
                    for k in range(2):
                        gp.wait_ge(s_sc[k], 16 * (EC // 2))

            @block.vector
            def _(v):
                with if_unsorted(v):
                    nc.vector.tensor_tensor(cnt[:, :], C.below[:, 1:NB + 1], C.below[:, 0:NB], ALU.subtract).then_inc(s_cnt, 1)
                    v.wait_ge(s_base, 1)
                    nc.vector.scalar_tensor_tensor(out=base[:, :], in0=p_base[:, 0:NB], scalar=-1.0, in1=C.first[:, 0:NB],
                                                   op0=ALU.add, op1=ALU.add).then_inc(s_v, 1)
                    v.wait_ge(s_pairs, 16)
                    nc.vector.tensor_scalar(blki[:, :], pairs[:, :, 1], P.bit_length() - 1, None, ALU.arith_shift_right).then_inc(s_v, 1)
                    v.wait_ge(s_v, 2)
                    nc.vector.tensor_copy(blk[:, :], blki[:, :]).then_inc(s_v, 1)
                    v.wait_ge(s_e, 1)
                    nc.vector.tensor_copy(run[:, :], ei[:, :]).then_inc(s_v, 1)
                    v.wait_ge(s_v, 4)
                    nc.vector.scalar_tensor_tensor(out=place[:, :], in0=blk[:, :], scalar=0.0, in1=run[:, :], op0=ALU.is_lt, op1=ALU.mult).then_inc(s_place, 1)
                    v.wait_ge(s_place, 1)
                    with v.Fori(0, NB) as b:
                        nc.vector.tensor_scalar(mine[:, :], blk[:, :], C.iota[:, ds(b, 1)], None, ALU.is_equal).then_inc(s_mine, 1)
                        v.wait_ge(s_mine, b + 1)
                        nc.vector.tensor_tensor_scan(run[:, :], mine[:, :], mine[:, :], 0.0, ALU.add, ALU.bypass).then_inc(s_run, 1)
                        v.wait_ge(s_run, b * 2 + 1)
                        nc.vector.scalar_tensor_tensor(out=run[:, :], in0=run[:, :], scalar=base[:, ds(b, 1)], in1=mine[:, :],
                                                       op0=ALU.add, op1=ALU.mult).then_inc(s_run, 1)
                        v.wait_ge(s_run, b * 2 + 2)
                        nc.vector.tensor_tensor(place[:, :], place[:, :], run[:, :], ALU.add).then_inc(s_place, 1)
                        v.wait_ge(s_place, b + 2)
                    nc.vector.tensor_copy(placei[:, :], place[:, :]).then_inc(s_done, 1)

            @block.tensor
            def _(pe):
                with if_unsorted(pe):
                    pe.wait_ge(s_tri, 2)
                    pe.wait_ge(s_cnt, 1)
                    nc.tensor.matmul(p_base[:, 0:NB], tri[:, :], cnt[:, :], start=True, stop=True).then_inc(s_base, 1)


def stage_encode(nc, C, A):
    with ExitStack() as ctx:
        sb, ps, sem = alloc(nc, ctx, "encode_")
        w1 = sb("w1", [P, 2 * KC, F]); w2 = sb("w2", [P, FC, D]); wg = sb("wg", [P, KC, D + 2 * H])
        wgr = sb("wgr", [P, KC, D]); alr = sb("alr", [P, KC, 2 * H])
        embT = sb("embT", [P, KC, NC]); b1 = sb("b1", [1, F]); lab_w = sb("lab_w", [NC, F])
        gcol = sb("gcol", [P, FC]); bcol = sb("bcol", [P, FC]); b2 = sb("b2", [P, KC]); ones1 = sb("ones1", [1, P])
        st = sb("st", [P, NB * 6]); mv = sb("mv", [P, NB * 2]); rstd = sb("rstd", [P, NB])
        xn = [sb(f"xn{k}", [P, D]) for k in range(2)]
        oh = [sb(f"ohl{k}", [P, NC]) for k in range(2)]
        xT = [sb(f"xT{k}", [P, KC * P]) for k in range(2)]
        ohT = [sb(f"ohlT{k}", [NC, P]) for k in range(2)]
        st2 = sb("st2", [P, 2, 6]); mv2 = sb("mv2", [P, 2]); sd2 = sb("sd2", [P, 1]); rs2 = sb("rs2", [P, 1])
        z = sb("z", [P, F]); zT = sb("zT", [P, FC, P]); hT = sb("hT", [P, KC, P])
        row = [sb(f"row{k}", [P, D + H]) for k in range(2)]
        p_x = ps("p_x", [P, 512]); p_u = ps("p_u", [P, 2, 512]); p_z = ps("p_z", [P, 2, 512])
        p_h = ps("p_h", [P, 512]); p_f = ps("p_f", [P, 512])
        s_w = sem("s_w"); s_st = sem("s_st"); s_var = sem("s_var"); s_std = sem("s_std"); s_one = sem("s_one")
        s_lw = sem("s_lw"); s_lwc = sem("s_lwc"); s_wa = sem("s_wa"); s_wac = sem("s_wac")
        s_xn = sem("s_xn"); s_xT = sem("s_xT"); s_xTc = sem("s_xTc"); s_u = sem("s_u"); s_bn = sem("s_bn")
        s_sd = sem("s_sd"); s_rs = sem("s_rs"); s_z = sem("s_z"); s_zT = sem("s_zT"); s_zTc = sem("s_zTc")
        s_h = sem("s_h"); s_hc = sem("s_hc"); s_f = sem("s_f"); s_row = sem("s_row"); s_gate = sem("s_gate")
        s_rowd = [sem(f"s_rowd{k}") for k in range(2)]
        zero = sb("zero", [P, D]); s_zero = sem("s_zero"); s_zd = sem("s_zd")
        NW = 10

        def exists(b):
            return not isinstance(b, int) or b < NB

        with nc.Block() as block:
            @block.sync
            def _(sp):
                sp.dma_start(w1[:, :, :], A["le_W1T"].rearrange("(c p) f -> p c f", p=P)).then_inc(s_w, 16)
                sp.dma_start(embT[:, :, :], A["embT"].rearrange("(c p) f -> p c f", p=P)).then_inc(s_w, 16)
                sp.dma_start(b1[:, :], A["le_b1"].rearrange("(a f) -> a f", a=1)).then_inc(s_w, 16)
                sp.dma_start(w2[:, :, :], A["le_W2T"].rearrange("(c p) f -> p c f", p=P)).then_inc(s_w, 16)
                sp.dma_start(wg[:, :, 0:D], A["W1T"].rearrange("(c p) f -> p c f", p=P)).then_inc(s_w, 16)
                sp.dma_start(wgr[:, :, :], A["W1"].rearrange("(c p) f -> p c f", p=P)).then_inc(s_w, 16)
                sp.dma_start(alr[:, :, :], A["alr1"].rearrange("(c p) f -> p c f", p=P)).then_inc(s_w, 16)
                sp.dma_start(gcol[:, :], A["ln_g"].rearrange("(c p) -> p c", p=P), allow_slow_non_contiguous=True).then_inc(s_w, 16)
                sp.dma_start(bcol[:, :], A["ln_b"].rearrange("(c p) -> p c", p=P), allow_slow_non_contiguous=True).then_inc(s_w, 16)
                sp.dma_start(b2[:, :], A["le_b2"].rearrange("(c p) -> p c", p=P), allow_slow_non_contiguous=True).then_inc(s_w, 16)

                def front(b, k):
                    pass

                def back(b, k):
                    sp.wait_ge(s_row, b * 2 + 2)
                    sp.dma_start(C.tab1[ds(b * P, P), 0:D + H], row[k][:, :]).then_inc(s_rowd[k], 16)

                skewed(sp, NB, 2, front, back)
                sp.wait_ge(s_rowd[0], 16 * ((NB + 1) // 2))
                sp.wait_ge(s_rowd[1], 16 * (NB // 2))

            @block.gpsimd
            def _(gp):
                nc.gpsimd.memset(zero[:, :], 0.0).then_inc(s_zero, 1)
                gp.wait_ge(s_zero, 1)
                gp.wait_ge(s_w, 16 * NW)
                gp.dma_start(C.ffn_in[:, :].rearrange("(c p) d -> p c d", p=P), zero[:, :].unsqueeze(1).broadcast_to([P, NE * CS // P, D])).then_inc(s_zd, 16)
                gp.dma_start(C.xs_d[:, :].rearrange("(c p) d -> p c d", p=P), zero[:, :].unsqueeze(1).broadcast_to([P, NT, D])).then_inc(s_zd, 16)
                gp.wait_ge(s_zd, 32)

            @block.vector
            def _(v):
                nc.vector.memset(ones1[:, :], 1.0).then_inc(s_one, 1)
                ln_stats(nc, v, None, C.X, mv, st, rstd, s_st, s_var, s_std, 1e-5)
                v.wait_ge(s_wa, 1)
                nc.vector.tensor_copy(wg[:, :, D:D + 2 * H], p_h[:, 0:KC * 2 * H].rearrange("p (c h) -> p c h", c=KC)).then_inc(s_wac, 1)

                def normalise(b, k):
                    from_step(2, v, s_xT, b, b - 1)
                    nc.vector.tensor_scalar(xn[k][:, :], C.X[:, ds(b * D, D)], mv[:, ds(b * 2, 1)], rstd[:, ds(b, 1)],
                                            ALU.subtract, ALU.mult).then_inc(s_xn, 1)
                    nc.vector.tensor_scalar(oh[k][:, :], C.iota[:, 0:NC], C.lab[:, ds(b, 1)], None, ALU.is_equal).then_inc(s_xn, 1)

                def hidden_ln(b):
                    v.wait_ge(s_u, b * 2 + 1)
                    nc.vector.bn_stats(st2[:, 0, :], p_u[:, 0, :]).then_inc(s_bn, 1)
                    v.wait_ge(s_u, b * 2 + 2)
                    nc.vector.bn_stats(st2[:, 1, :], p_u[:, 1, :]).then_inc(s_bn, 1)
                    hold(v, s_bn, b * 4 + 2, s_gate)
                    nc.vector.bn_aggr(mv2[:, :], st2[:, :, :].rearrange("p a s -> p (a s)")).then_inc(s_bn, 1)
                    v.wait_ge(s_bn, b * 4 + 3)
                    nc.vector.tensor_scalar(sd2[:, :], mv2[:, 1:2], 1e-5, None, ALU.add).then_inc(s_bn, 1)
                    v.wait_ge(s_sd, b + 1)
                    nc.vector.reciprocal(rs2[:, :], sd2[:, :]).then_inc(s_rs, 1)
                    v.wait_ge(s_rs, b + 1)
                    from_step(1, v, s_zT, b, b * 2)
                    for c in range(2):
                        nc.vector.tensor_scalar(z[:, c * 512:c * 512 + 512], p_u[:, c, :], mv2[:, 0:1], rs2[:, 0:1],
                                                ALU.subtract, ALU.mult).then_inc(s_z, 1)

                def step(b, k):
                    if exists(b + 1):
                        hidden_ln(b + 1)
                    if exists(b + 3):
                        normalise(b + 3, 1 - k)
                    v.wait_ge(s_f, b + 1)
                    from_step(2, v, s_rowd[k], b, (b - k) * 8)
                    nc.vector.tensor_copy(row[k][:, :], p_f[:, 0:D + H]).then_inc(s_row, 1)
                    nc.vector.tensor_copy(C.ler[:, ds(b * 2 * H, 2 * H)], p_f[:, D:D + 2 * H]).then_inc(s_row, 1)

                for b in range(3):
                    normalise(b, b % 2)
                hidden_ln(0)
                steps(v, NB, 2, step)

            @block.scalar
            def _(act):
                ln_sqrt(nc, act, rstd, s_var, s_std)
                act.wait_ge(s_lw, 2)
                nc.scalar.copy(lab_w[:, :], p_u[0:NC, :, :].rearrange("p a f -> p (a f)")).then_inc(s_lwc, 1)

                def copy_x(b, k):
                    act.wait_ge(s_xT, b + 1)
                    from_step(2, act, s_u, b, b * 2 - 2)
                    nc.scalar.copy(xT[k][:, :], p_x[:, 0:KC * P]).then_inc(s_xTc, 1)
                    nc.scalar.copy(ohT[k][:, :], p_x[0:NC, KC * P:KC * P + P]).then_inc(s_xTc, 1)

                def root(b):
                    act.wait_ge(s_bn, b * 4 + 4)
                    nc.scalar.activation(sd2[:, :], sd2[:, :], ACT.Sqrt).then_inc(s_sd, 1)

                def step(b, k):
                    from_step(1, act, s_h, b, b)
                    for c in range(FC):
                        if c % 4 == 0:
                            act.wait_ge(s_zT, b * 2 + c // 4 + 1)
                        nc.scalar.activation(zT[:, c, :], p_z[:, c // 4, (c % 4) * P:(c % 4) * P + P], ACT.Relu,
                                             bias=bcol[:, c:c + 1], scale=gcol[:, c:c + 1]).then_inc(s_zTc, 1)
                    if exists(b + 1):
                        root(b + 1)
                    act.wait_ge(s_h, b + 1)
                    from_step(1, act, s_f, b, b)
                    for c in range(KC):
                        nc.scalar.activation(hT[:, c, :], p_h[:, c * P:c * P + P], ACT.Identity, bias=b2[:, c:c + 1]).then_inc(s_hc, 1)
                    if exists(b + 2):
                        copy_x(b + 2, k)

                copy_x(0, 0)
                copy_x(1, 1)
                root(0)
                steps(act, NB, 2, step)

            @block.tensor
            def _(pe):
                pe.wait_ge(s_w, 16 * NW)
                pe.wait_ge(s_one, 1)
                for c in range(2):
                    for kc in range(KC):
                        nc.tensor.matmul(p_u[0:NC, c, :], embT[:, kc, :], w1[:, KC + kc, c * 512:c * 512 + 512], start=(kc == 0), stop=False)
                    nc.tensor.matmul(p_u[0:NC, c, :], ones1[0:1, 0:NC], b1[0:1, c * 512:c * 512 + 512], start=False, stop=True).then_inc(s_lw, 1)
                project_attention_vectors(nc, p_h, wgr, alr, s_wa)
                pe.wait_ge(s_lwc, 1)
                pe.wait_ge(s_wac, 1)

                def turn_x(b, k):
                    pe.wait_ge(s_xn, b * 2 + 2)
                    from_step(1, pe, s_xTc, b, b * 2)
                    for c in range(KC):
                        nc.tensor.transpose(p_x[:, c * P:c * P + P], xn[k][:, c * P:c * P + P], C.ident[:, :])
                    nc.tensor.transpose(p_x[0:NC, KC * P:KC * P + P], oh[k][:, :], C.ident[:, :]).then_inc(s_xT, 1)

                def hidden(b, k):
                    pe.wait_ge(s_xTc, b * 2 + 2)
                    for c in range(2):
                        from_step(1, pe, s_z, b, (b - 1) * 2 + c + 1)
                        for kc in range(KC):
                            nc.tensor.matmul(p_u[:, c, :], xT[k][:, kc * P:kc * P + P], w1[:, kc, c * 512:c * 512 + 512], start=(kc == 0), stop=False)
                        nc.tensor.matmul(p_u[:, c, :], ohT[k][:, :], lab_w[:, c * 512:c * 512 + 512], start=False, stop=True).then_inc(s_u, 1)

                def step(b, k):
                    for c in range(FC):
                        if c % 4 == 0:
                            pe.wait_ge(s_z, b * 2 + c // 4 + 1)
                            from_step(1, pe, s_zTc, b, b * FC - FC + c + 4)
                        t = nc.tensor.transpose(p_z[:, c // 4, (c % 4) * P:(c % 4) * P + P], z[:, c * P:c * P + P], C.ident[:, :])
                        if c % 4 == 3:
                            t.then_inc(s_zT, 1)
                    if exists(b + 1):
                        hidden(b + 1, 1 - k)
                    pe.wait_ge(s_zTc, b * FC + FC)
                    from_step(1, pe, s_hc, b, b * KC)
                    for m in range(KC):
                        for c in range(FC):
                            t = nc.tensor.matmul(p_h[:, m * P:m * P + P], w2[:, c, m * P:m * P + P], zT[:, c, :], start=(c == 0), stop=(c == FC - 1))
                    t.then_inc(s_h, 1)
                    if exists(b + 2):
                        turn_x(b + 2, k)
                    pe.wait_ge(s_hc, b * KC + KC)
                    from_step(1, pe, s_row, b, b * 2)
                    for kc in range(KC):
                        t = nc.tensor.matmul(p_f[:, 0:D + 2 * H], hT[:, kc, :], wg[:, kc, :], start=(kc == 0), stop=(kc == KC - 1))
                    t.then_inc(s_f, 1)

                turn_x(0, 0)
                turn_x(1, 1)
                hidden(0, 0)
                steps(pe, NB, 2, step)


def project_attention_vectors(nc, p, w_rows, alr, s_done):
    for m in range(KC):
        for kc in range(KC):
            t = nc.tensor.matmul(p[:, m * 2 * H:(m + 1) * 2 * H], w_rows[:, kc, m * P:m * P + P], alr[:, kc, :], start=(kc == 0), stop=(kc == KC - 1))
    t.then_inc(s_done, 1)


def when_near(C, eng, want):
    return eng.If(eng.value_load(C.near[0:1, 0:1], min_val=0, max_val=1) == want)


def stage_scores(nc, C, table, layer):
    with ExitStack() as ctx:
        sb, ps, sem = alloc(nc, ctx, f"scores{layer}_")
        ext = sb("ext", [P, 2 * H]); top = sb("top", [2 * H, 1]); diag = sb("diag", [2 * H, 2 * H]); ones = sb("ones", [2 * H, P])
        lim = sb("lim", [P, 2 * H]); span = sb("span", [P, H]); fits = sb("fits", [P, 1])
        dd = sb("dd", [P, NB, H]); y = sb("y", [P, NB, H]); lk = sb("lk", [P, NB, H])
        ac = sb("ac", [P, NB, 2 * H]); bg = sb("bg", [P, NB, 2 * H])
        p_t = ps("p_t", [P, 512]); p_b = ps("p_b", [P, 512])
        s_v = sem("s_v"); s_t = sem("s_t"); s_bc = sem("s_bc"); s_arg = sem("s_arg"); s_ac = sem("s_ac"); s_bg = sem("s_bg"); s_tab = sem("s_tab")
        ler = C.ler[:, :].rearrange("p (b t) -> p b t", t=2 * H)
        bg3 = C.bg3[:, :].rearrange("p (b s t) -> p b s t", s=3, t=2 * H)

        with nc.Block() as block:
            @block.sync
            def _(sp):
                sp.wait_ge(s_ac, 2)
                sp.dma_start(table[:, D + H:TW].rearrange("(b p) t -> p b t", p=P), ac[:, :, :], allow_slow_non_contiguous=True).then_inc(s_tab, 16)
                sp.wait_ge(s_tab, 16)

            @block.vector
            def _(v):
                nc.vector.memset(ones[:, :], 1.0).then_inc(s_v, 1)
                nc.vector.tensor_copy(C.em[:, :].rearrange("p (b t) -> p b t", t=2 * H)[:, :, 0:H], ler[:, :, H:2 * H]).then_inc(s_v, 1)
                by_head = C.ler[:, :].rearrange("p (b t) -> p t b", t=2 * H)[:, 0:H, :]
                nc.vector.tensor_reduce(ext[:, 0:H], by_head, AX.X, ALU.max).then_inc(s_v, 1)
                nc.vector.tensor_reduce(ext[:, H:2 * H], by_head, AX.X, ALU.min).then_inc(s_v, 1)
                v.wait_ge(s_v, 4)
                nc.vector.tensor_scalar(ext[:, H:2 * H], ext[:, H:2 * H], -1.0, None, ALU.mult).then_inc(s_v, 1)
                v.wait_ge(s_t, 1)
                nc.vector.tensor_reduce(top[:, :], p_t[0:2 * H, 0:P], AX.X, ALU.max).then_inc(s_v, 1)
                v.wait_ge(s_v, 6)
                nc.vector.tensor_scalar(diag[:, :], C.ident[0:2 * H, 0:2 * H], top[:, 0:1], None, ALU.mult).then_inc(s_v, 1)
                v.wait_ge(s_bc, 1)
                nc.vector.tensor_copy(lim[:, :], p_b[:, 0:2 * H]).then_inc(s_v, 1)
                v.wait_ge(s_v, 8)
                most = lim[:, 0:H].unsqueeze(1).broadcast_to([P, NB, H])
                nc.vector.tensor_tensor(dd[:, :, :], ler[:, :, 0:H], most, ALU.subtract).then_inc(s_arg, 1)
                nc.vector.tensor_tensor(y[:, :, :], ler[:, :, H:2 * H], most, ALU.add).then_inc(s_v, 1)
                nc.vector.tensor_tensor(span[:, :], lim[:, 0:H], lim[:, H:2 * H], ALU.add).then_inc(s_v, 1)
                v.wait_ge(s_v, 10)
                nc.vector.scalar_tensor_tensor(out=lk[:, :, :], in0=y[:, :, :], scalar=SLOPE, in1=y[:, :, :], op0=ALU.mult, op1=ALU.max).then_inc(s_v, 1)
                nc.vector.tensor_scalar(span[:, :], span[:, :], SPREAD, None, ALU.is_le).then_inc(s_v, 1)
                v.wait_ge(s_v, 12)
                nc.vector.tensor_tensor(bg[:, :, 0:H], y[:, :, :], lk[:, :, :], ALU.subtract).then_inc(s_arg, 1)
                nc.vector.scalar_tensor_tensor(out=bg[:, :, H:2 * H], in0=y[:, :, :], scalar=SLOPE, in1=lk[:, :, :], op0=ALU.mult, op1=ALU.subtract).then_inc(s_arg, 1)
                nc.vector.tensor_reduce(fits[:, :], span[:, :], AX.X, ALU.min).then_inc(s_v, 1)
                v.wait_ge(s_v, 13)
                nc.vector.tensor_copy(C.near[:, :], fits[:, :]).then_inc(s_v, 1)
                v.wait_ge(s_bg, 1)
                for s in range(3):
                    nc.vector.tensor_copy(bg3[:, :, s, :], bg[:, :, :]).then_inc(s_v, 1)
                    v.wait_ge(s_v, 15 + 2 * s)
                    if s < 2:
                        nc.vector.tensor_tensor(bg[:, :, :], bg[:, :, :], bg3[:, :, s, :], ALU.subtract).then_inc(s_v, 1)
                        v.wait_ge(s_v, 16 + 2 * s)

            @block.scalar
            def _(act):
                act.wait_ge(s_arg, 1)
                nc.scalar.activation(ac[:, :, 0:H], dd[:, :, :], ACT.Exp).then_inc(s_ac, 1)
                nc.scalar.activation(ac[:, :, H:2 * H], dd[:, :, :], ACT.Exp, scale=SLOPE).then_inc(s_ac, 1)
                act.wait_ge(s_arg, 3)
                nc.scalar.activation(bg[:, :, :], bg[:, :, :], ACT.Exp).then_inc(s_bg, 1)

            @block.tensor
            def _(pe):
                pe.wait_ge(s_v, 5)
                nc.tensor.transpose(p_t[0:2 * H, 0:P], ext[:, :], C.ident[:, :]).then_inc(s_t, 1)
                pe.wait_ge(s_v, 7)
                nc.tensor.matmul(p_b[:, 0:2 * H], ones[:, :], diag[:, :], start=True, stop=True).then_inc(s_bc, 1)


def stage_attend_near(nc, C, table, layer):
    with ExitStack() as ctx:
        sb, ps, sem = alloc(nc, ctx, f"near{layer}_")
        ix = [sb(f"ix{k}", [P, ET, 2], I32) for k in range(UN)]
        G = [sb(f"G{k}", [P, ET, TW]) for k in range(UN)]
        dl = [sb(f"dl{k}", [P, ET]) for k in range(2)]
        ohb = [sb(f"ohb{k}", [P, ET, P], BF16) for k in range(2)]
        oh = [sb(f"oh{k}", [P, ET, P]) for k in range(2)]
        ohT = [sb(f"ohT{k}", [P, EG], BF16) for k in range(2)]
        w2 = sb("w2", [P, ET, 2 * H])
        Gw = [sb(f"Gw{k}", [P, ET, H, HW]) for k in range(2)]
        p_oT = [ps(f"p_oT{k}", [P, 1024], BF16) for k in range(2)]; p_ex = [ps(f"p_ex{k}", [P, 512]) for k in range(2)]
        p_sg = [ps(f"p_sg{k}", [P, H * HW]) for k in range(2)]
        s_ix = [sem(f"s_ix{k}") for k in range(UN)]; s_g = [sem(f"s_g{k}") for k in range(UN)]
        s_go = sem("s_go"); s_init = sem("s_init"); s_dl = sem("s_dl"); s_ohb = sem("s_ohb"); s_oh = sem("s_oh"); s_T = sem("s_T"); s_cp = sem("s_cp")
        s_ex = sem("s_ex"); s_w = sem("s_w"); s_p = sem("s_p"); s_use = sem("s_use"); s_sg = sem("s_sg"); s_acc = sem("s_acc")
        HD4 = H * HW

        def block_of(eng, g):
            return eng.value_load(C.gblk[0:1, ds(g, 1)], min_val=0, max_val=NB - 1)

        with nc.Block() as block:
            @block.sync
            def _(sp):
                with when_near(C, sp, 1):
                    def load(g, k):
                        off = sp.value_load(C.gofs[0:1, ds(g, 1)], min_val=0, max_val=E)
                        sp.dma_start(ix[k][:, :, :].rearrange("p c t -> p (c t)"),
                                     C.edges[ds(off, EG), :].rearrange("(p c) t -> p (c t)", c=ET)).then_inc(s_ix[k], 16)
                    for k in range(UN):
                        load(k, k)
                    with sp.Fori(1, NG // UN) as i:
                        for k in range(UN):
                            sp.wait_ge(s_use, i * UN + k - UN + 1)
                            load(i * UN + k, k)

            @block.gpsimd
            def _(gp):
                with when_near(C, gp, 1):
                    with gp.Fori(0, NG // UN) as i:
                        for k in range(UN):
                            hold(gp, s_ix[k], i * 16 + 16, s_go)
                            for j in range(ET):
                                gp.indirect_dma_start(out=G[k][:, j, :], out_offset=None, in_=table[:, :],
                                                      in_offset=bass.IndirectOffsetOnAxis(ap=ix[k][:, j, 0:1], axis=0)).then_inc(s_g[k], 16)

            @block.vector
            def _(v):
                with when_near(C, v, 1):
                    nc.vector.memset(C.acc[:, :], 0.0).then_inc(s_init, 1)
                    v.wait_ge(s_init, 1)

                    def one_hot(g, k):
                        v.wait_ge(s_ix[k], (g - k) * 4 + 16)
                        nc.vector.tensor_scalar(dl[k % 2][:, :], ix[k][:, :, 1], C.gbase[:, ds(g, 1)], None, ALU.subtract).then_inc(s_dl, 1)
                        v.wait_ge(s_dl, g + 1)
                        from_step(1, v, s_oh, g, g)
                        nc.vector.tensor_tensor(ohb[k % 2][:, :, :], C.iota[:, :].unsqueeze(1).broadcast_to([P, ET, P]),
                                                dl[k % 2][:, :].unsqueeze(2).broadcast_to([P, ET, P]), ALU.is_equal).then_inc(s_ohb, 1)

                    def accumulate(g, k, blk):
                        a = C.acc[:, ds(blk * HD4, HD4)]
                        v.wait_ge(s_sg, g + 1)
                        nc.vector.tensor_tensor(a, a, p_sg[k % 2][:, :], ALU.add).then_inc(s_acc, 1)
                        v.wait_ge(s_acc, g + 1)

                    def step(g, k, last=False):
                        v.wait_ge(s_g[k], (g - k) * 16 + 64)
                        v.wait_ge(s_ex, g + 1)
                        nc.vector.tensor_tensor(w2[:, :, :], G[k][:, :, D + H:TW], p_ex[k % 2][:, 0:ET * 2 * H].rearrange("p (c t) -> p c t", c=ET), ALU.mult).then_inc(s_w, 1)
                        if not last:
                            one_hot(g + 1, (k + 1) % UN)
                        v.wait_ge(s_w, g + 1)
                        nc.vector.tensor_tensor(Gw[k % 2][:, :, :, HD], w2[:, :, 0:H], w2[:, :, H:2 * H], ALU.max).then_inc(s_p, 1)
                        if not isinstance(g, int) or g > 0:
                            accumulate(g - 1, (k - 1) % UN, block_of(v, g - 1))
                        v.wait_ge(s_p, g + 1)
                        nc.vector.tensor_tensor(Gw[k % 2][:, :, :, 0:HD], G[k][:, :, 0:D].rearrange("p c (h d) -> p c h d", h=H),
                                                Gw[k % 2][:, :, :, HD:HW].broadcast_to([P, ET, H, HD]), ALU.mult).then_inc(s_use, 1)

                    one_hot(0, 0)
                    for g in range(UN):
                        step(g, g)
                    with v.Fori(1, NG // UN - 1) as i:
                        for k in range(UN):
                            step(i * UN + k, k)
                    for g in range(NG - UN, NG):
                        step(g, g % UN, last=g == NG - 1)
                    accumulate(NG - 1, (NG - 1) % UN, block_of(v, NG - 1))

            @block.scalar
            def _(act):
                with when_near(C, act, 1):
                    def step(g, k):
                        act.wait_ge(s_T, g + 1)
                        nc.scalar.copy(ohT[k % 2][:, :], p_oT[k % 2][:, 0:EG]).then_inc(s_cp, 1)
                        if not isinstance(g, int) or g >= 2:
                            act.wait_ge(s_sg, g - 1)
                        nc.scalar.copy(oh[k % 2][:, :, :], ohb[k % 2][:, :, :]).then_inc(s_oh, 1)

                    for g in range(UN):
                        step(g, g)
                    with act.Fori(1, NG // UN) as i:
                        for k in range(UN):
                            step(i * UN + k, k)

            @block.tensor
            def _(pe):
                with when_near(C, pe, 1):
                    def transposes(g, k):
                        pe.wait_ge(s_ohb, g + 1)
                        for j in range(ET):
                            t = nc.tensor.transpose(p_oT[k % 2][:, j * P:j * P + P], ohb[k % 2][:, j, :], C.identb[:, :])
                        t.then_inc(s_T, 1)

                    def expand(g, k, blk):
                        pe.wait_ge(s_cp, g + 1)
                        if not isinstance(g, int) or g >= 2:
                            pe.wait_ge(s_w, g - 1)
                        for j in range(ET):
                            for s in range(3):
                                t = nc.tensor.matmul(p_ex[k % 2][:, j * 2 * H:(j + 1) * 2 * H], ohT[k % 2][:, j * P:j * P + P],
                                                     C.bg3[:, ds(blk * 6 * H + s * 2 * H, 2 * H)], start=(s == 0), stop=(s == 2))
                        t.then_inc(s_ex, 1)

                    def sums(g, k):
                        pe.wait_ge(s_use, g + 1)
                        if not isinstance(g, int) or g >= 2:
                            pe.wait_ge(s_acc, g - 1)
                        for j in range(ET):
                            t = nc.tensor.matmul(p_sg[k % 2][:, :], oh[k % 2][:, j, :], Gw[k % 2][:, j, :, :].rearrange("p h d -> p (h d)"),
                                                 start=(j == 0), stop=(j == ET - 1))
                        t.then_inc(s_sg, 1)

                    def step(g, k, last=False):
                        if not last:
                            transposes(g + 1, (k + 1) % UN)
                            expand(g + 1, (k + 1) % UN, block_of(pe, g + 1))
                        pe.wait_ge(s_oh, g + 1)
                        sums(g, k)

                    transposes(0, 0)
                    expand(0, 0, block_of(pe, 0))
                    for g in range(UN):
                        step(g, g)
                    with pe.Fori(1, NG // UN - 1) as i:
                        for k in range(UN):
                            step(i * UN + k, k)
                    for g in range(NG - UN, NG):
                        step(g, g % UN, last=g == NG - 1)


def stage_attend(nc, C, table, layer):
    with ExitStack() as ctx:
        sb, ps, sem = alloc(nc, ctx, f"attend{layer}_")
        ix = [sb(f"ix{k}", [P, ET, 2], I32) for k in range(UN)]
        G = [sb(f"G{k}", [P, ET, TW]) for k in range(UN)]
        dl = [sb(f"dl{k}", [P, ET]) for k in range(2)]
        oh = [sb(f"oh{k}", [P, ET, P]) for k in range(2)]
        ohT = [sb(f"ohT{k}", [P, EG]) for k in range(2)]
        pen = [sb(f"pen{k}", [P, EG], BF16) for k in range(2)]
        elT = [sb(f"elT{k}", [H, EG]) for k in range(2)]
        selh = sb("selh", [H, H, P])
        mx = sb("mx", [P, NB * H])
        gm = [sb(f"gm{k}", [P, H]) for k in range(2)]
        e1 = sb("e1", [P, NB * H]); mn = sb("mn", [P, NB * H]); dm = sb("dm", [P, H])
        resc = [sb(f"resc{k}", [P, H]) for k in range(2)]
        sc = sb("sc", [P, ET, H]); sl = sb("sl", [P, ET, H])
        Gw = [sb(f"Gw{k}", [P, ET, H, HW]) for k in range(2)]
        p_oT = ps("p_oT", [P, 512]); p_eT = ps("p_eT", [P, 512]); p_bc = ps("p_bc", [P, 2, 512])
        p_ex = ps("p_ex", [P, ET, 2 * H]); p_sg = [ps(f"p_sg{k}", [P, H * HW]) for k in range(2)]
        s_ix = [sem(f"s_ix{k}") for k in range(UN)]
        s_g = [sem(f"s_g{k}") for k in range(UN)]
        s_use = sem("s_use"); s_init = sem("s_init"); s_sel = sem("s_sel"); s_go = sem("s_go")
        s_dl = sem("s_dl"); s_oh = sem("s_oh"); s_T = sem("s_T"); s_cp = sem("s_cp"); s_bc = sem("s_bc")
        s_red = sem("s_red"); s_m = sem("s_m"); s_em = sem("s_em"); s_dm = sem("s_dm"); s_rc = sem("s_rc")
        s_ex = sem("s_ex"); s_sc = sem("s_sc"); s_sl = sem("s_sl"); s_p = sem("s_p"); s_pm = sem("s_pm"); s_gw = sem("s_gw")
        s_sg = sem("s_sg"); s_acc = sem("s_acc")
        HD4 = H * HW
        em3 = C.em[:, :].rearrange("p (b t) -> p b t", t=2 * H)

        with nc.Block() as block:
            @block.sync
            def _(sp):
                with when_near(C, sp, 0):
                    def load(g, k, i):
                        off = sp.value_load(C.gofs[0:1, ds(g, 1)], min_val=0, max_val=E)
                        sp.dma_start(ix[k][:, :, :].rearrange("p c t -> p (c t)"),
                                     C.edges[ds(off, EG), :].rearrange("(p c) t -> p (c t)", c=ET)).then_inc(s_ix[k], 16)
                    for k in range(UN):
                        load(k, k, 0)
                    with sp.Fori(1, NG // UN) as i:
                        for k in range(UN):
                            g = i * UN + k
                            sp.wait_ge(s_use, g - UN + 1)
                            load(g, k, i)

            @block.gpsimd
            def _(gp):
                with when_near(C, gp, 0):
                    nc.gpsimd.memset(selh[:, :, :], 0.0).then_inc(s_sel, 1)
                    gp.wait_ge(s_sel, 1)
                    nc.gpsimd.affine_select(out=selh[:, :, :], in_=selh[:, :, :], compare_op=ALU.not_equal, fill=1.0, base=0,
                                            pattern=[[-1, H], [0, P]], channel_multiplier=1).then_inc(s_sel, 1)
                    with gp.Fori(0, NG // UN) as i:
                        for k in range(UN):
                            hold(gp, s_ix[k], i * 16 + 16, s_go)
                            for j in range(ET):
                                gp.indirect_dma_start(out=G[k][:, j, :], out_offset=None, in_=table[:, :],
                                                      in_offset=bass.IndirectOffsetOnAxis(ap=ix[k][:, j, 0:1], axis=0)).then_inc(s_g[k], 16)

            @block.vector
            def _(v):
                with when_near(C, v, 0):
                    nc.vector.memset(mx[:, :], -BIG).then_inc(s_init, 1)
                    nc.vector.memset(C.acc[:, :], 0.0).then_inc(s_init, 1)
                    v.wait_ge(s_init, 2)
                    mx3 = mx[:, :].rearrange("p (b h) -> p b h", h=H)
                    e13 = e1[:, :].rearrange("p (b h) -> p b h", h=H)
                    nc.vector.tensor_tensor(e13, mx3, em3[:, :, 0:H], ALU.add).then_inc(s_init, 1)
                    v.wait_ge(s_init, 3)
                    nc.vector.scalar_tensor_tensor(out=em3[:, :, H:2 * H], in0=e13, scalar=SLOPE, in1=e13, op0=ALU.mult, op1=ALU.max).then_inc(s_init, 1)
                    v.wait_ge(s_init, 4)
                    v.sem_inc(s_red, 2)

                    def i_of(g, k):
                        return (g - k) * 4

                    def one_hot(g, k):
                        v.wait_ge(s_ix[k], i_of(g, k) + 16)
                        nc.vector.tensor_scalar(dl[k % 2][:, :], ix[k][:, :, 1], C.gbase[:, ds(g, 1)], None, ALU.subtract).then_inc(s_dl, 1)
                        v.wait_ge(s_dl, g + 1)
                        nc.vector.tensor_tensor(oh[k % 2][:, :, :], C.iota[:, :].unsqueeze(1).broadcast_to([P, ET, P]),
                                                dl[k % 2][:, :].unsqueeze(2).broadcast_to([P, ET, P]), ALU.is_equal).then_inc(s_oh, 1)

                    def group_max(g, k):
                        for h in range(H):
                            v.wait_ge(s_bc, g * H + h + 1)
                            nc.vector.tensor_reduce(gm[k % 2][:, h:h + 1], p_bc[:, h % 2, :], AX.X, ALU.max).then_inc(s_red, 1)

                    def new_max(g, k, blk):
                        mxb = mx[:, ds(blk * H, H)]
                        erb = C.em[:, ds(blk * 2 * H, H)]
                        mb = C.em[:, ds(blk * 2 * H + H, H)]
                        v.wait_ge(s_red, g * H + H + 2)
                        nc.vector.tensor_tensor(mxb, mxb, gm[k % 2][:, :], ALU.max).then_inc(s_m, 1)
                        v.wait_ge(s_m, g * 4 + 1)
                        nc.vector.tensor_tensor(e1[:, 0:H], mxb, erb, ALU.add).then_inc(s_m, 1)
                        v.wait_ge(s_m, g * 4 + 2)
                        nc.vector.scalar_tensor_tensor(out=mn[:, 0:H], in0=e1[:, 0:H], scalar=SLOPE, in1=e1[:, 0:H], op0=ALU.mult, op1=ALU.max).then_inc(s_m, 1)
                        v.wait_ge(s_m, g * 4 + 3)
                        if not isinstance(g, int) or g > 0:
                            v.wait_ge(s_rc, g)
                        nc.vector.tensor_tensor(dm[:, :], mb, mn[:, 0:H], ALU.subtract).then_inc(s_m, 1)
                        v.wait_ge(s_m, g * 4 + 4)
                        nc.vector.tensor_scalar(mb, mn[:, 0:H], 1.0, None, ALU.mult).then_inc(s_em, 1)

                    def scores(g, k):
                        v.wait_ge(s_ex, g + 1)
                        nc.vector.tensor_tensor(sc[:, :, :], G[k][:, :, D:D + H], p_ex[:, :, 0:H], ALU.add).then_inc(s_sc, 1)
                        v.wait_ge(s_sc, g + 1)
                        nc.vector.scalar_tensor_tensor(out=sl[:, :, :], in0=sc[:, :, :], scalar=SLOPE, in1=sc[:, :, :], op0=ALU.mult, op1=ALU.max).then_inc(s_sl, 1)
                        v.wait_ge(s_sl, g * 2 + 1)
                        nc.vector.tensor_tensor(sl[:, :, :], sl[:, :, :], p_ex[:, :, H:2 * H], ALU.subtract).then_inc(s_sl, 1)

                    def weigh(g, k):
                        v.wait_ge(s_p, g + 1)
                        pk = Gw[k % 2][:, :, :, HD]
                        nc.vector.tensor_scalar(pk, pk, 1.0, None, ALU.min).then_inc(s_pm, 1)
                        v.wait_ge(s_pm, g + 1)
                        nc.vector.tensor_tensor(Gw[k % 2][:, :, :, 0:HD], G[k][:, :, 0:D].rearrange("p c (h d) -> p c h d", h=H),
                                                Gw[k % 2][:, :, :, HD:HW].broadcast_to([P, ET, H, HD]), ALU.mult).then_inc(s_use, 1)

                    def accumulate(g, k, blk):
                        a = C.acc[:, ds(blk * HD4, HD4)]
                        v.wait_ge(s_rc, g + 1)
                        nc.vector.tensor_tensor(a.rearrange("p (h d) -> p h d", h=H), a.rearrange("p (h d) -> p h d", h=H),
                                                resc[k % 2][:, :].unsqueeze(2).broadcast_to([P, H, HW]), ALU.mult).then_inc(s_acc, 1)
                        v.wait_ge(s_acc, g * 2 + 1)
                        v.wait_ge(s_sg, g + 1)
                        nc.vector.tensor_tensor(a, a, p_sg[k % 2][:, :], ALU.add).then_inc(s_acc, 1)

                    def block_of(g):
                        return v.value_load(C.gblk[0:1, ds(g, 1)], min_val=0, max_val=NB - 1)

                    def step(g, k, last=False):
                        new_max(g, k, block_of(g))
                        if not last:
                            one_hot(g + 1, (k + 1) % UN)
                        scores(g, k)
                        if not isinstance(g, int) or g > 0:
                            accumulate(g - 1, (k - 1) % UN, block_of(g - 1))
                        weigh(g, k)
                        if not last:
                            group_max(g + 1, (k + 1) % UN)

                    one_hot(0, 0)
                    group_max(0, 0)
                    for g in range(UN):
                        step(g, g)
                    with v.Fori(1, NG // UN - 1) as i:
                        for k in range(UN):
                            step(i * UN + k, k)
                    for g in range(NG - UN, NG):
                        step(g, g % UN, last=g == NG - 1)
                    accumulate(NG - 1, (NG - 1) % UN, block_of(NG - 1))

            @block.scalar
            def _(act):
                with when_near(C, act, 0):
                    def front(g, k):
                        act.wait_ge(s_T, g + 1)
                        nc.scalar.copy(ohT[k % 2][:, :], p_oT[:, :]).then_inc(s_cp, 1)
                        nc.scalar.copy(elT[k % 2][:, :], p_eT[0:H, :]).then_inc(s_cp, 1)
                        nc.scalar.activation(pen[k % 2][:, :], p_oT[:, :], ACT.Copy, bias=-1.0).then_inc(s_cp, 1)

                    def back(g, k):
                        act.wait_ge(s_m, g * 4 + 4)
                        nc.scalar.activation(resc[k % 2][:, :], dm[:, :], ACT.Exp).then_inc(s_rc, 1)
                        act.wait_ge(s_sl, g * 2 + 2)
                        nc.scalar.activation(Gw[k % 2][:, :, :, HD], sl[:, :, :], ACT.Exp).then_inc(s_p, 1)

                    front(0, 0)
                    with act.Fori(0, NG // UN - 1) as i:
                        for k in range(UN):
                            g = i * UN + k
                            back(g, k)
                            front(g + 1, (k + 1) % UN)
                    for g in range(NG - UN, NG):
                        back(g, g % UN)
                        if g + 1 < NG:
                            front(g + 1, (g + 1) % UN)

            @block.tensor
            def _(pe):
                with when_near(C, pe, 0):
                    pe.wait_ge(s_sel, 2)

                    def transposes(g, k):
                        pe.wait_ge(s_oh, g + 1)
                        if not isinstance(g, int) or g > 0:
                            pe.wait_ge(s_cp, g * 3)
                        for j in range(ET):
                            nc.tensor.transpose(p_oT[:, j * P:j * P + P], oh[k % 2][:, j, :], C.ident[:, :])
                        pe.wait_ge(s_g[k], (g - k) * 16 + 64)
                        for j in range(ET):
                            t = nc.tensor.transpose(p_eT[0:H, j * P:j * P + P], G[k][:, j, D:D + H], C.ident[:, :])
                        t.then_inc(s_T, 1)

                    def spread(g, k, h):
                        if h == 0:
                            pe.wait_ge(s_cp, g * 3 + 3)
                        pe.wait_ge(s_red, g * H + h + 1)
                        nc.tensor.matmul(p_bc[:, h % 2, :], C.bigi[:, :], pen[k % 2][:, :], start=True, stop=False)
                        nc.tensor.matmul(p_bc[:, h % 2, :], selh[:, h, :], elT[k % 2][:, :], start=False, stop=True).then_inc(s_bc, 1)

                    def expand(g, k, blk):
                        pe.wait_ge(s_em, g + 1)
                        for j in range(ET):
                            t = nc.tensor.matmul(p_ex[:, j, :], ohT[k % 2][:, j * P:j * P + P], C.em[:, ds(blk * 2 * H, 2 * H)], start=True, stop=True)
                        t.then_inc(s_ex, 1)

                    def sums(g, k):
                        pe.wait_ge(s_use, g + 1)
                        for j in range(ET):
                            t = nc.tensor.matmul(p_sg[k % 2][:, :], oh[k % 2][:, j, :], Gw[k % 2][:, j, :, :].rearrange("p h d -> p (h d)"),
                                                 start=(j == 0), stop=(j == ET - 1))
                        t.then_inc(s_sg, 1)

                    def step(g, k, last=False):
                        expand(g, k, pe.value_load(C.gblk[0:1, ds(g, 1)], min_val=0, max_val=NB - 1))
                        if not last:
                            transposes(g + 1, (k + 1) % UN)
                            spread(g + 1, (k + 1) % UN, 0)
                            spread(g + 1, (k + 1) % UN, 1)
                        sums(g, k)
                        if not last:
                            spread(g + 1, (k + 1) % UN, 2)
                            spread(g + 1, (k + 1) % UN, 3)

                    transposes(0, 0)
                    for h in range(H):
                        spread(0, 0, h)
                    with pe.Fori(0, NG // UN - 1) as i:
                        for k in range(UN):
                            step(i * UN + k, k)
                    for g in range(NG - UN, NG):
                        step(g, g % UN, last=g == NG - 1)


def stage_between(nc, C, A):
    with ExitStack() as ctx:
        sb, ps, sem = alloc(nc, ctx, "between_")
        wg = sb("wg2", [P, KC, D + 2 * H]); wgr = sb("wgr2", [P, KC, D]); alr = sb("alr2", [P, KC, 2 * H])
        bias = sb("bias1", [P, D]); den = sb("den", [P, NB * H])
        h1 = [sb(f"h1_{k}", [P, D]) for k in range(2)]
        hT = sb("h1T", [P, KC * P])
        row = [sb(f"rowb{k}", [P, D + H]) for k in range(2)]
        p_a = ps("p_a", [P, 512]); p_t = ps("p_t", [P, 512]); p_f = ps("p_fb", [P, 512])
        s_w = sem("s_w"); s_wa = sem("s_wa"); s_wac = sem("s_wac"); s_den = sem("s_den"); s_h = sem("s_h"); s_hs = sem("s_hs")
        s_t = sem("s_t"); s_tc = sem("s_tc"); s_f = sem("s_f"); s_row = sem("s_row")
        s_rowd = [sem(f"s_rowd{k}") for k in range(2)]

        with nc.Block() as block:
            @block.sync
            def _(sp):
                sp.dma_start(wg[:, :, 0:D], A["W2T"].rearrange("(c p) f -> p c f", p=P)).then_inc(s_w, 16)
                sp.dma_start(wgr[:, :, :], A["W2"].rearrange("(c p) f -> p c f", p=P)).then_inc(s_w, 16)
                sp.dma_start(alr[:, :, :], A["alr2"].rearrange("(c p) f -> p c f", p=P)).then_inc(s_w, 16)
                sp.dma_start(bias[:, :], A["b1"].partition_broadcast(P)).then_inc(s_w, 16)

                def back(b, k):
                    sp.wait_ge(s_row, b * 2 + 2)
                    sp.dma_start(C.tab2[ds(b * P, P), 0:D + H], row[k][:, :]).then_inc(s_rowd[k], 16)

                skewed(sp, NB, 2, lambda b, k: None, back)
                sp.wait_ge(s_rowd[0], 16 * ((NB + 1) // 2))
                sp.wait_ge(s_rowd[1], 16 * (NB // 2))

            @block.vector
            def _(v):
                acc4 = C.acc[:, :].rearrange("p (b h d) -> p b h d", h=H, d=HW)
                nc.vector.tensor_scalar(den[:, :].rearrange("p (b h) -> p b h", h=H), acc4[:, :, :, HD], 1e-9, None, ALU.max).then_inc(s_den, 1)
                v.wait_ge(s_den, 1)
                nc.vector.reciprocal(den[:, :], den[:, :]).then_inc(s_den, 1)
                v.wait_ge(s_w, 64)
                v.wait_ge(s_wa, 1)
                nc.vector.tensor_copy(wg[:, :, D:D + 2 * H], p_a[:, 0:KC * 2 * H].rearrange("p (c h) -> p c h", c=KC)).then_inc(s_wac, 1)
                v.wait_ge(s_den, 2)

                def front(b, k):
                    a = C.acc[:, ds(b * H * HW, H * HW)].rearrange("p (h d) -> p h d", h=H)[:, :, 0:HD]
                    h4 = h1[k][:, :].rearrange("p (h d) -> p h d", h=H)
                    nc.vector.tensor_tensor(h4, a, den[:, ds(b * H, H)].unsqueeze(2).broadcast_to([P, H, HD]), ALU.mult).then_inc(s_hs, 1)
                    v.wait_ge(s_hs, b * 2 + 1)
                    nc.vector.tensor_tensor(h1[k][:, :], h1[k][:, :], bias[:, :], ALU.add).then_inc(s_hs, 1)
                    v.wait_ge(s_hs, b * 2 + 2)
                    nc.vector.tensor_scalar(h1[k][:, :], h1[k][:, :], 0.0, None, ALU.max).then_inc(s_h, 1)

                def back(b, k):
                    v.wait_ge(s_f, b + 1)
                    if not isinstance(b, int) or b >= 2:
                        v.wait_ge(s_rowd[k], (b - k) * 8)
                    nc.vector.tensor_copy(row[k][:, :], p_f[:, 0:D + H]).then_inc(s_row, 1)
                    nc.vector.tensor_copy(C.ler[:, ds(b * 2 * H, 2 * H)], p_f[:, D:D + 2 * H]).then_inc(s_row, 1)

                skewed(v, NB, 2, front, back, peel=2)

            @block.scalar
            def _(act):
                def back(b, k):
                    act.wait_ge(s_t, b + 1)
                    nc.scalar.copy(hT[:, :], p_t[:, 0:KC * P]).then_inc(s_tc, 1)

                skewed(act, NB, 2, lambda b, k: None, back)

            @block.tensor
            def _(pe):
                pe.wait_ge(s_w, 64)
                project_attention_vectors(nc, p_a, wgr, alr, s_wa)
                pe.wait_ge(s_wac, 1)

                def back(b, k):
                    pe.wait_ge(s_h, b + 1)
                    if not isinstance(b, int) or b > 0:
                        pe.wait_ge(s_tc, b)
                    for c in range(KC):
                        t = nc.tensor.transpose(p_t[:, c * P:c * P + P], h1[k][:, c * P:c * P + P], C.ident[:, :])
                    t.then_inc(s_t, 1)
                    pe.wait_ge(s_tc, b + 1)
                    if not isinstance(b, int) or b > 0:
                        pe.wait_ge(s_row, b * 2)
                    for kc in range(KC):
                        t = nc.tensor.matmul(p_f[:, 0:D + 2 * H], hT[:, kc * P:kc * P + P], wg[:, kc, :], start=(kc == 0), stop=(kc == KC - 1))
                    t.then_inc(s_f, 1)

                skewed(pe, NB, 2, lambda b, k: None, back)


def stage_route(nc, C, A):
    with ExitStack() as ctx:
        sb, ps, sem = alloc(nc, ctx, "route_")
        bias = sb("bias2", [P, D]); den = sb("den2", [P, NB * H])
        gw = sb("gw", [P, KC, NE]); gb = sb("gb", [P, NE])
        t1 = sb("t1", [P, D])
        st = sb("st", [P, NB * 6]); mv = sb("mv", [P, NB * 2]); rstd = sb("rstd", [P, NB])
        xa = [sb(f"xa{b}", [P, D]) for b in range(NB)]
        xT = sb("xTr", [P, KC * P])
        lg = sb("lg", [P, NB, NE]); mx8 = sb("mx8", [P, NB, 8]); ix8 = sb("ix8", [P, NB, 8], U32)
        ixf = sb("ixf", [P, NB]); ex = sb("ex", [P, NB, NE]); sm = sb("sm", [P, NB])
        one = sb("one", [P, NB, NE]); up = sb("up", [P, P]); onesq = sb("onesq2", [P, P])
        tot = sb("tot", [P, NB, NE]); run = sb("run", [P, NE, NB]); pos3 = sb("pos3", [P, NB, NE]); pos = sb("pos", [P, NB])
        kept = sb("kept", [P, NB]); drop = sb("drop", [P, NB]); base = sb("base", [P, NB])
        slf = sb("slf", [P, NB]); sloti = sb("sloti", [P, NB], I32); vali = sb("vali", [P, NB], I32); val = sb("val", [P, NB])
        p_t = ps("p_tr", [P, 512]); p_l = ps("p_l", [P, 512]); p_c = ps("p_c", [P, 2, 512])
        s_w = sem("s_w"); s_pl = sem("s_pl"); s_v = sem("s_v"); s_a = sem("s_a"); s_st = sem("s_st"); s_var = sem("s_var"); s_std = sem("s_std")
        s_xa = sem("s_xa"); s_t = sem("s_t"); s_tc = sem("s_tc"); s_l = sem("s_l"); s_lc = sem("s_lc"); s_one = sem("s_one"); s_cs = sem("s_cs")
        s_ex0 = sem("s_ex0"); s_ex1 = sem("s_ex1"); s_slot = sem("s_slot"); s_sc = sem("s_sc")

        with nc.Block() as block:
            @block.sync
            def _(sp):
                sp.dma_start(bias[:, :], A["b2"].partition_broadcast(P)).then_inc(s_w, 16)
                sp.dma_start(gw[:, :, :], A["gate_w"].rearrange("(c p) e -> p c e", p=P)).then_inc(s_w, 16)
                sp.dma_start(gb[:, :], A["gate_b"].partition_broadcast(P)).then_inc(s_w, 16)

            @block.gpsimd
            def _(gp):
                nc.gpsimd.memset(up[:, :], 1.0).then_inc(s_pl, 1)
                nc.gpsimd.iota(vali[:, :], pattern=[[P, NB]], base=0, channel_multiplier=1).then_inc(s_pl, 1)
                gp.wait_ge(s_pl, 2)
                nc.gpsimd.affine_select(out=up[:, :], in_=up[:, :], compare_op=ALU.is_gt, fill=0.0, base=0,
                                        pattern=[[1, P]], channel_multiplier=-1).then_inc(s_pl, 1)
                gp.wait_ge(s_slot, 1)
                for b in range(NB):
                    gp.indirect_dma_start(out=C.ffn_in[:, :], out_offset=bass.IndirectOffsetOnAxis(ap=sloti[:, b:b + 1], axis=0),
                                          in_=xa[b][:, :], in_offset=None, bounds_check=NE * CS - 1, oob_is_err=False).then_inc(s_sc, 16)
                gp.wait_ge(s_sc, 16 * NB)

            @block.vector
            def _(v):
                acc4 = C.acc[:, :].rearrange("p (b h d) -> p b h d", h=H, d=HW)
                nc.vector.tensor_scalar(den[:, :].rearrange("p (b h) -> p b h", h=H), acc4[:, :, :, HD], 1e-9, None, ALU.max).then_inc(s_v, 1)
                v.wait_ge(s_v, 1)
                nc.vector.reciprocal(den[:, :], den[:, :]).then_inc(s_v, 1)
                nc.vector.memset(onesq[:, :], 1.0).then_inc(s_v, 1)
                v.wait_ge(s_w, 48)
                v.wait_ge(s_v, 3)
                with v.Fori(0, NB) as b:
                    a = C.acc[:, ds(b * H * HW, H * HW)].rearrange("p (h d) -> p h d", h=H)[:, :, 0:HD]
                    x = C.X[:, ds(b * D, D)]
                    v.wait_ge(s_a, b * 4)
                    nc.vector.tensor_tensor(t1[:, :].rearrange("p (h d) -> p h d", h=H), a, den[:, ds(b * H, H)].unsqueeze(2).broadcast_to([P, H, HD]), ALU.mult).then_inc(s_a, 1)
                    v.wait_ge(s_a, b * 4 + 1)
                    nc.vector.tensor_tensor(t1[:, :], t1[:, :], bias[:, :], ALU.add).then_inc(s_a, 1)
                    v.wait_ge(s_a, b * 4 + 2)
                    nc.vector.scalar_tensor_tensor(out=x, in0=t1[:, :], scalar=0.0, in1=x, op0=ALU.max, op1=ALU.add).then_inc(s_a, 1)
                    v.wait_ge(s_a, b * 4 + 3)
                    nc.vector.bn_stats(st[:, ds(b * 6, 6)], x).then_inc(s_a, 1)
                v.wait_ge(s_a, 4 * NB)
                ln_finish(nc, v, mv, st, rstd, s_st, s_var, s_std, 1e-5)
                for b in range(NB):
                    nc.vector.tensor_scalar(xa[b][:, :], C.X[:, b * D:b * D + D], mv[:, 2 * b:2 * b + 1], rstd[:, b:b + 1], ALU.subtract, ALU.mult).then_inc(s_xa, 1)
                v.wait_ge(s_pl, 3)
                nc.vector.tensor_scalar(val[:, :], vali[:, :], float(N), None, ALU.is_lt).then_inc(s_v, 1)
                v.wait_ge(s_l, NB)
                nc.vector.tensor_tensor(lg[:, :, :], p_l[:, 0:NB * NE].rearrange("p (b e) -> p b e", e=NE),
                                        gb[:, :].unsqueeze(1).broadcast_to([P, NB, NE]), ALU.add).then_inc(s_lc, NB)
                v.wait_ge(s_lc, NB)
                for b in range(NB):
                    nc.vector.max(mx8[:, b, :], lg[:, b, :]).then_inc(s_lc, 1)
                v.wait_ge(s_lc, 2 * NB)
                for b in range(NB):
                    nc.vector.max_index(ix8[:, b, :], mx8[:, b, :], lg[:, b, :]).then_inc(s_lc, 1)
                nc.vector.tensor_tensor(ex[:, :, :], lg[:, :, :], mx8[:, :, 0:1].broadcast_to([P, NB, NE]), ALU.subtract).then_inc(s_ex0, 1)
                v.wait_ge(s_lc, 3 * NB)
                nc.vector.tensor_copy(ixf[:, :], ix8[:, :, 0]).then_inc(s_v, 1)
                v.wait_ge(s_v, 5)
                nc.vector.tensor_tensor(one[:, :, :], C.iota[:, 0:NE].unsqueeze(1).broadcast_to([P, NB, NE]),
                                        ixf[:, :].unsqueeze(2).broadcast_to([P, NB, NE]), ALU.is_equal).then_inc(s_v, 1)
                v.wait_ge(s_v, 6)
                nc.vector.tensor_tensor(one[:, :, :], one[:, :, :], val[:, :].unsqueeze(2).broadcast_to([P, NB, NE]), ALU.mult).then_inc(s_one, 1)
                v.wait_ge(s_ex1, 1)
                nc.vector.tensor_reduce(sm[:, :], ex[:, :, :], AX.X, ALU.add).then_inc(s_v, 1)
                v.wait_ge(s_v, 7)
                nc.vector.reciprocal(sm[:, :], sm[:, :]).then_inc(s_v, 1)
                v.wait_ge(s_cs, 1)
                nc.vector.tensor_copy(tot[:, :, :], p_c[:, 1, 0:NB * NE].rearrange("p (b e) -> p b e", e=NE)).then_inc(s_v, 1)
                v.wait_ge(s_v, 9)
                for e in range(NE):
                    nc.vector.tensor_tensor_scan(run[:, e, :], tot[:, :, e], tot[:, :, e], 0.0, ALU.add, ALU.bypass).then_inc(s_v, 1)
                v.wait_ge(s_v, 9 + NE)
                nc.vector.tensor_tensor(pos3[:, :, :], run[:, :, :].rearrange("p e b -> p b e"), tot[:, :, :], ALU.subtract).then_inc(s_v, 1)
                v.wait_ge(s_v, 10 + NE)
                nc.vector.tensor_tensor(pos3[:, :, :], pos3[:, :, :], p_c[:, 0, 0:NB * NE].rearrange("p (b e) -> p b e", e=NE), ALU.add).then_inc(s_v, 1)
                v.wait_ge(s_v, 11 + NE)
                nc.vector.tensor_tensor(pos3[:, :, :], pos3[:, :, :], one[:, :, :], ALU.mult).then_inc(s_v, 1)
                v.wait_ge(s_v, 12 + NE)
                nc.vector.tensor_reduce(pos[:, :], pos3[:, :, :], AX.X, ALU.add).then_inc(s_v, 1)
                nc.vector.tensor_scalar(base[:, :], ixf[:, :], float(CS), None, ALU.mult).then_inc(s_v, 1)
                v.wait_ge(s_v, 14 + NE)
                nc.vector.scalar_tensor_tensor(out=kept[:, :], in0=pos[:, :], scalar=float(CAP), in1=val[:, :], op0=ALU.is_lt, op1=ALU.mult).then_inc(s_v, 1)
                nc.vector.tensor_tensor(slf[:, :], base[:, :], pos[:, :], ALU.add).then_inc(s_v, 1)
                v.wait_ge(s_v, 16 + NE)
                nc.vector.tensor_scalar(drop[:, :], kept[:, :], float(-NE * CS), float(NE * CS), ALU.mult, ALU.add).then_inc(s_v, 1)
                nc.vector.tensor_tensor(C.gate[:, :], sm[:, :], kept[:, :], ALU.mult).then_inc(s_v, 1)
                v.wait_ge(s_v, 18 + NE)
                nc.vector.tensor_tensor(sloti[:, :], slf[:, :], drop[:, :], ALU.add).then_inc(s_slot, 1)
                nc.vector.tensor_scalar(pos[:, :], pos[:, :], float(CAP - 1), None, ALU.min).then_inc(s_v, 1)
                v.wait_ge(s_v, 19 + NE)
                nc.vector.tensor_tensor(C.back[:, :], base[:, :], pos[:, :], ALU.add).then_inc(s_v, 1)

            @block.scalar
            def _(act):
                ln_sqrt(nc, act, rstd, s_var, s_std)
                for b in range(NB):
                    act.wait_ge(s_t, b + 1)
                    nc.scalar.copy(xT[:, :], p_t[:, 0:KC * P]).then_inc(s_tc, 1)
                act.wait_ge(s_ex0, 1)
                nc.scalar.activation(ex[:, :, :], ex[:, :, :], ACT.Exp).then_inc(s_ex1, 1)

            @block.tensor
            def _(pe):
                pe.wait_ge(s_w, 48)
                for b in range(NB):
                    pe.wait_ge(s_xa, b + 1)
                    if b > 0:
                        pe.wait_ge(s_tc, b)
                    for c in range(KC):
                        t = nc.tensor.transpose(p_t[:, c * P:c * P + P], xa[b][:, c * P:c * P + P], C.ident[:, :])
                    t.then_inc(s_t, 1)
                    pe.wait_ge(s_tc, b + 1)
                    for kc in range(KC):
                        t = nc.tensor.matmul(p_l[:, b * NE:b * NE + NE], xT[:, kc * P:kc * P + P], gw[:, kc, :], start=(kc == 0), stop=(kc == KC - 1))
                    t.then_inc(s_l, 1)
                pe.wait_ge(s_pl, 3)
                pe.wait_ge(s_v, 3)
                pe.wait_ge(s_one, 1)
                o = one[:, :, :].rearrange("p b e -> p (b e)")
                nc.tensor.matmul(p_c[:, 0, 0:NB * NE], up[:, :], o, start=True, stop=True)
                nc.tensor.matmul(p_c[:, 1, 0:NB * NE], onesq[:, :], o, start=True, stop=True).then_inc(s_cs, 1)


def stage_experts(nc, C, A):
    with ExitStack() as ctx:
        sb, ps, sem = alloc(nc, ctx, "experts_")
        TS = CS // P
        w1 = [sb(f"ew1_{k}", [P, KC, F]) for k in range(2)]
        w2 = [sb(f"ew2_{k}", [P, FC, D]) for k in range(2)]
        b1 = sb("eb1", [P, NE, FC]); b2 = sb("eb2", [P, NE * D])
        xi = [sb(f"xi{k}", [P, TS, D]) for k in range(2)]
        xT = sb("xTe", [P, KC, CS]); hT = sb("hTe", [P, FC, CS])
        y = [sb(f"ye{k}", [P, TS, D]) for k in range(2)]
        p_t = ps("p_te", [P, KC, CS]); p_h = ps("p_he", [P, 2, 512]); p_y = ps("p_ye", [P, 2, 512])
        s_b = sem("s_b"); s_in = [sem(f"s_in{k}") for k in range(2)]; s_t = sem("s_t"); s_tc = sem("s_tc")
        s_h = sem("s_h"); s_hc = sem("s_hc"); s_y = sem("s_y"); s_yc = sem("s_yc"); s_yd = [sem(f"s_yd{k}") for k in range(2)]

        def experts(eng, body):
            for e in range(2):
                body(e, e)
            with eng.Fori(1, NE // 2) as i:
                for k in range(2):
                    body(i * 2 + k, k)

        with nc.Block() as block:
            @block.sync
            def _(sp):
                sp.dma_start(b1[:, :, :], A["eb1"].rearrange("e (c p) -> p e c", p=P), allow_slow_non_contiguous=True).then_inc(s_b, 16)
                sp.dma_start(b2[:, :], A["eb2"].rearrange("e d -> (e d)").partition_broadcast(P)).then_inc(s_b, 16)

                def body(e, k):
                    if not isinstance(e, int) or e >= 2:
                        sp.wait_ge(s_yc, (e - 1) * TS)
                    sp.dma_start(w1[k][:, :, :], A["ew1"][ds(e * D, D), :].rearrange("(c p) f -> p c f", p=P)).then_inc(s_in[k], 16)
                    sp.dma_start(w2[k][:, :, :], A["ew2"][ds(e * F, F), :].rearrange("(c p) f -> p c f", p=P)).then_inc(s_in[k], 16)
                    sp.dma_start(xi[k][:, :, :], C.ffn_in[ds(e * CS, CS), :].rearrange("(t p) d -> p t d", p=P)).then_inc(s_in[k], 16)

                experts(sp, body)

            @block.gpsimd
            def _(gp):
                def body(e, k):
                    gp.wait_ge(s_yc, e * TS + TS)
                    gp.dma_start(C.ffn_out[ds(e * CS, CS), :].rearrange("(t p) d -> p t d", p=P), y[k][:, :, :]).then_inc(s_yd[k], 16)
                for e in range(NE):
                    body(e, e % 2)
                gp.wait_ge(s_yd[0], 16 * NE // 2)
                gp.wait_ge(s_yd[1], 16 * NE // 2)

            @block.vector
            def _(v):
                v.wait_ge(s_b, 32)

                def body(e, k):
                    if not isinstance(e, int) or e >= 2:
                        v.wait_ge(s_yd[k], (e - k) * 8)
                    for t in range(TS):
                        v.wait_ge(s_y, e * TS + t + 1)
                        nc.vector.tensor_tensor(y[k][:, t, :], p_y[:, t % 2, 0:D], b2[:, ds(e * D, D)], ALU.add).then_inc(s_yc, 1)

                experts(v, body)

            @block.scalar
            def _(act):
                act.wait_ge(s_b, 32)

                def body(e, k):
                    act.wait_ge(s_t, e + 1)
                    nc.scalar.copy(xT[:, :, :], p_t[:, :, :]).then_inc(s_tc, 1)
                    for c in range(FC):
                        act.wait_ge(s_h, e * FC + c + 1)
                        nc.scalar.activation(hT[:, c, :], p_h[:, c % 2, :], ACT.Relu, bias=b1[:, ds(e, 1), c:c + 1].rearrange("p a b -> p (a b)")).then_inc(s_hc, 1)

                experts(act, body)

            @block.tensor
            def _(pe):
                def body(e, k):
                    later = not isinstance(e, int) or e > 0
                    pe.wait_ge(s_in[k], (e - k) * 24 + 48)
                    if later:
                        pe.wait_ge(s_tc, e)
                    for t in range(TS):
                        for c in range(KC):
                            m = nc.tensor.transpose(p_t[:, c, t * P:t * P + P], xi[k][:, t, c * P:c * P + P], C.ident[:, :])
                    m.then_inc(s_t, 1)
                    pe.wait_ge(s_tc, e + 1)
                    for c in range(FC):
                        if later or c >= 2:
                            pe.wait_ge(s_hc, e * FC + c - 1)
                        for kc in range(KC):
                            m = nc.tensor.matmul(p_h[:, c % 2, :], w1[k][:, kc, c * P:c * P + P], xT[:, kc, :], start=(kc == 0), stop=(kc == KC - 1))
                        m.then_inc(s_h, 1)
                    pe.wait_ge(s_hc, e * FC + FC)
                    for t in range(TS):
                        if later or t >= 2:
                            pe.wait_ge(s_yc, e * TS + t - 1)
                        for c in range(FC):
                            m = nc.tensor.matmul(p_y[:, t % 2, 0:D], hT[:, c, t * P:t * P + P], w2[k][:, c, :], start=(c == 0), stop=(c == FC - 1))
                        m.then_inc(s_y, 1)

                experts(pe, body)


def stage_gated_in(nc, C, A):
    with ExitStack() as ctx:
        sb, ps, sem = alloc(nc, ctx, "gated_in_")
        w3 = sb("w3", [P, KC, 3 * D]); b3 = sb("b3", [1, 3 * D]); al = sb("al", [P, D]); ar = sb("ar", [P, D]); ones1 = sb("ones1g", [1, P])
        yb = [sb(f"yb{k}", [P, D]) for k in range(4)]
        fin = sb("fin", [P, D], U32); nn = sb("nn", [P, D], U32); cl = sb("cl", [P, D]); ysafe = sb("ysafe", [P, D])
        st = sb("st", [P, NB * 6]); mv = sb("mv", [P, NB * 2]); rstd = sb("rstd", [P, NB])
        xn = [sb(f"xng{k}", [P, D]) for k in range(2)]; xT = sb("xTg", [P, KC * P])
        row = [sb(f"rowg{k}", [P, 2 * D]) for k in range(2)]; us = [sb(f"us{k}", [P, D]) for k in range(2)]
        wf = [sb(f"wf{k}", [P, D]) for k in range(2)]
        p_t = ps("p_tg", [P, 512]); p_a = ps("p_ag", [P, 2, 512])
        s_rs = sem("s_rs"); s_sp = sem("s_sp"); s_spg = sem("s_spg")
        s_w = sem("s_w"); s_yb = [sem(f"s_yb{k}") for k in range(4)]; s_y = sem("s_y"); s_ya = sem("s_ya"); s_st = sem("s_st"); s_var = sem("s_var"); s_std = sem("s_std")
        s_one = sem("s_one"); s_xn = sem("s_xn"); s_t = sem("s_t"); s_tc = sem("s_tc"); s_a = sem("s_a"); s_row = sem("s_row"); s_x = sem("s_x")
        s_rowd = [sem(f"s_rowd{k}") for k in range(2)]

        with nc.Block() as block:
            @block.sync
            def _(sp):
                sp.dma_start(w3[:, :, :], A["w3"].rearrange("(c p) f -> p c f", p=P)).then_inc(s_w, 16)
                sp.dma_start(b3[:, :], A["b3"].rearrange("(a f) -> a f", a=1)).then_inc(s_w, 16)
                sp.dma_start(al[:, :], A["attn_l"].partition_broadcast(P)).then_inc(s_w, 16)
                sp.dma_start(ar[:, :], A["attn_r"].partition_broadcast(P)).then_inc(s_w, 16)

                def back(b, k):
                    sp.wait_ge(s_row, b * 4 + 4)
                    sp.dma_start(C.tab3[ds(b * P, P), :], row[k][:, :]).then_inc(s_rowd[k], 16)
                    sp.dma_start(C.u_d[ds(b * P, P), :], us[k][:, :]).then_inc(s_rowd[k], 16)

                skewed(sp, NB, 2, lambda b, k: None, back)
                sp.wait_ge(s_rowd[0], 32 * ((NB + 1) // 2))
                sp.wait_ge(s_rowd[1], 32 * (NB // 2))

            @block.gpsimd
            def _(gp):
                def split(b, k):
                    gp.wait_ge(s_row, b * 4 + 2)
                    for s in range(3):
                        part = C.wr3[:, ds(b * 3 * D + s * D, D)]
                        nc.gpsimd.tensor_copy(part, wf[k][:, :]).then_inc(s_sp, 1)
                        if s < 2:
                            hold(gp, s_sp, b * 5 + s * 2 + 1, s_spg)
                            nc.gpsimd.tensor_tensor(wf[k][:, :], wf[k][:, :], part, ALU.subtract).then_inc(s_sp, 1)
                            gp.wait_ge(s_sp, b * 5 + s * 2 + 2)

                def gather(b):
                    from_step(4, gp, s_ya, b, b - 3)
                    gp.indirect_dma_start(out=yb[b % 4][:, :], out_offset=None, in_=C.ffn_out[:, :],
                                          in_offset=bass.IndirectOffsetOnAxis(ap=C.back[:, b:b + 1], axis=0)).then_inc(s_yb[b % 4], 16)

                late = 6
                for b in range(NB + late):
                    if b < NB:
                        gather(b)
                    if b >= late:
                        split(b - late, (b - late) % 2)

            @block.vector
            def _(v):
                nc.vector.memset(ones1[:, :], 1.0).then_inc(s_one, 1)
                def add_experts(b):
                    yk = yb[b % 4]
                    x = C.X[:, b * D:b * D + D]
                    v.wait_ge(s_yb[b % 4], 16 * (b // 4 + 1))
                    nc.vector.tensor_scalar(yk[:, :], yk[:, :], C.gate[:, b:b + 1], None, ALU.mult).then_inc(s_y, 1)
                    nc.vector.memset(ysafe[:, :], 0.0).then_inc(s_y, 1)
                    v.wait_ge(s_y, 8 * b + 2)
                    nc.vector.tensor_scalar(fin[:, :], yk[:, :], 0.0, 0.0, ALU.mult, ALU.is_equal).then_inc(s_y, 1)
                    nc.vector.tensor_tensor(nn[:, :], yk[:, :], yk[:, :], ALU.is_equal).then_inc(s_y, 1)
                    nc.vector.tensor_scalar(cl[:, :], yk[:, :], -1e4, 1e4, ALU.max, ALU.min).then_inc(s_y, 1)
                    v.wait_ge(s_y, 8 * b + 5)
                    nc.vector.copy_predicated(ysafe[:, :], nn[:, :], cl[:, :]).then_inc(s_y, 1)
                    v.wait_ge(s_y, 8 * b + 6)
                    nc.vector.copy_predicated(ysafe[:, :], fin[:, :], yk[:, :]).then_inc(s_y, 1)
                    v.wait_ge(s_y, 8 * b + 7)
                    nc.vector.tensor_tensor(x, x, ysafe[:, :], ALU.add).then_inc(s_ya, 1)
                    v.wait_ge(s_ya, b + 1)
                    nc.vector.bn_stats(st[:, b * 6:b * 6 + 6], x).then_inc(s_y, 1)
                    v.wait_ge(s_y, 8 * b + 8)
                    nc.vector.bn_aggr(mv[:, b * 2:b * 2 + 2], st[:, b * 6:b * 6 + 6]).then_inc(s_st, 1)
                    v.wait_ge(s_st, b + 1)
                    nc.vector.tensor_scalar(rstd[:, b:b + 1], mv[:, b * 2 + 1:b * 2 + 2], 1e-5, None, ALU.add).then_inc(s_var, 1)

                def front(b, k):
                    v.wait_ge(s_std, b + 1)
                    nc.vector.reciprocal(rstd[:, b:b + 1], rstd[:, b:b + 1]).then_inc(s_rs, 1)
                    v.wait_ge(s_rs, b + 1)
                    from_step(2, v, s_x, b, b - 1)
                    nc.vector.tensor_scalar(xn[k][:, :], C.X[:, ds(b * D, D)], mv[:, ds(b * 2, 1)], rstd[:, ds(b, 1)],
                                            ALU.subtract, ALU.mult).then_inc(s_xn, 1)

                def back(b, k):
                    x = C.X[:, ds(b * D, D)]
                    v.wait_ge(s_xn, b + 1)
                    nc.vector.tensor_tensor(x, x, xn[k][:, :], ALU.add).then_inc(s_x, 1)
                    v.wait_ge(s_a, b * 2 + 1)
                    if not isinstance(b, int) or b >= 2:
                        v.wait_ge(s_rowd[k], (b - k) * 16)
                    nc.vector.tensor_tensor(row[k][:, 0:D], p_a[:, 0, 0:D], al[:, :], ALU.mult).then_inc(s_row, 1)
                    if not isinstance(b, int) or b >= 2:
                        v.wait_ge(s_sp, b * 5 - 5)
                    nc.vector.tensor_tensor(wf[k][:, :], p_a[:, 0, 0:D], ar[:, :], ALU.mult).then_inc(s_row, 1)
                    v.wait_ge(s_a, b * 2 + 2)
                    nc.vector.tensor_copy(us[k][:, :], p_a[:, 0, D:2 * D]).then_inc(s_row, 1)
                    nc.vector.tensor_copy(row[k][:, D:2 * D], p_a[:, 1, 0:D]).then_inc(s_row, 1)

                for b in range(NB + 2):
                    if b < NB:
                        add_experts(b)
                    if 1 <= b <= NB:
                        front(b - 1, (b - 1) % 2)
                    if b == 1:
                        v.wait_ge(s_w, 64)
                    if b >= 2:
                        back(b - 2, b % 2)

            @block.scalar
            def _(act):
                def front(b, k):
                    act.wait_ge(s_var, b + 1)
                    nc.scalar.activation(rstd[:, ds(b, 1)], rstd[:, ds(b, 1)], ACT.Sqrt).then_inc(s_std, 1)

                def back(b, k):
                    act.wait_ge(s_t, b + 1)
                    nc.scalar.copy(xT[:, :], p_t[:, 0:KC * P]).then_inc(s_tc, 1)

                skewed(act, NB, 2, front, back)

            @block.tensor
            def _(pe):
                pe.wait_ge(s_w, 64)
                pe.wait_ge(s_one, 1)

                def back(b, k):
                    later = not isinstance(b, int) or b > 0
                    pe.wait_ge(s_xn, b + 1)
                    if later:
                        pe.wait_ge(s_tc, b)
                    for c in range(KC):
                        t = nc.tensor.transpose(p_t[:, c * P:c * P + P], xn[k][:, c * P:c * P + P], C.ident[:, :])
                    t.then_inc(s_t, 1)
                    pe.wait_ge(s_tc, b + 1)
                    if later:
                        pe.wait_ge(s_row, b * 4)
                    for a, lo, w in ((0, 0, 2 * D), (1, 2 * D, D)):
                        for kc in range(KC):
                            nc.tensor.matmul(p_a[:, a, 0:w], xT[:, kc * P:kc * P + P], w3[:, kc, lo:lo + w], start=(kc == 0), stop=False)
                        nc.tensor.matmul(p_a[:, a, 0:w], ones1[0:1, :], b3[0:1, lo:lo + w], start=False, stop=True).then_inc(s_a, 1)

                skewed(pe, NB, 2, lambda b, k: None, back)


def stage_gated(nc, C):
    with ExitStack() as ctx:
        sb, ps, sem = alloc(nc, ctx, "gated_")
        ix = [sb(f"ix{k}", [P, ET, 2], I32) for k in range(UN)]
        G = [sb(f"G{k}", [P, ET, 2 * D]) for k in range(UN)]
        dl = [sb(f"dl{k}", [P, ET]) for k in range(2)]
        ohb = [sb(f"ohb{k}", [P, ET, P], BF16) for k in range(2)]
        oh = [sb(f"oh{k}", [P, ET, P]) for k in range(UN)]
        ohT = [sb(f"ohT{k}", [P, EG], BF16) for k in range(2)]
        tv = sb("tv", [P, ET, D])
        sv = [sb(f"sv{k}", [P, ET, 2 * D]) for k in range(2)]
        p_oT = [ps(f"p_oT{k}", [P, 1024], BF16) for k in range(2)]; p_b = [ps(f"p_b{k}", [P, ET, D]) for k in range(2)]
        p_sg = [ps(f"p_sg{k}", [P, 2 * D]) for k in range(2)]
        s_ix = [sem(f"s_ix{k}") for k in range(UN)]; s_g = [sem(f"s_g{k}") for k in range(UN)]
        s_go = sem("s_go"); s_init = sem("s_init"); s_dl = sem("s_dl"); s_ohb = sem("s_ohb"); s_oh = sem("s_oh"); s_T = sem("s_T"); s_cp = sem("s_cp")
        s_b = sem("s_b"); s_t = sem("s_t"); s_s = sem("s_s"); s_use = sem("s_use"); s_sg = sem("s_sg"); s_acc = sem("s_acc")

        def block_of(eng, g):
            return eng.value_load(C.gblk[0:1, ds(g, 1)], min_val=0, max_val=NB - 1)

        def all_groups(eng, step):
            for g in range(UN):
                step(g, g)
            with eng.Fori(1, NG // UN - 1) as i:
                for k in range(UN):
                    step(i * UN + k, k)
            for g in range(NG - UN, NG):
                step(g, g % UN)

        def exists(g):
            return not isinstance(g, int) or g < NG

        with nc.Block() as block:
            @block.sync
            def _(sp):
                def load(g, k):
                    off = sp.value_load(C.gofs[0:1, ds(g, 1)], min_val=0, max_val=E)
                    sp.dma_start(ix[k][:, :, :].rearrange("p c t -> p (c t)"),
                                 C.edges[ds(off, EG), :].rearrange("(p c) t -> p (c t)", c=ET)).then_inc(s_ix[k], 16)
                for k in range(UN):
                    load(k, k)
                with sp.Fori(1, NG // UN) as i:
                    for k in range(UN):
                        sp.wait_ge(s_use, i * UN + k - UN + 1)
                        load(i * UN + k, k)

            @block.gpsimd
            def _(gp):
                with gp.Fori(0, NG // UN) as i:
                    for k in range(UN):
                        hold(gp, s_ix[k], i * 16 + 16, s_go)
                        for j in range(ET):
                            gp.indirect_dma_start(out=G[k][:, j, :], out_offset=None, in_=C.tab3[:, :],
                                                  in_offset=bass.IndirectOffsetOnAxis(ap=ix[k][:, j, 0:1], axis=0)).then_inc(s_g[k], 16)

            @block.vector
            def _(v):
                nc.vector.memset(C.acc3[:, :], 0.0).then_inc(s_init, 1)
                v.wait_ge(s_init, 1)

                def one_hot(g, k):
                    v.wait_ge(s_ix[k], (g - k) * 4 + 16)
                    nc.vector.tensor_scalar(dl[k % 2][:, :], ix[k][:, :, 1], C.gbase[:, ds(g, 1)], None, ALU.subtract).then_inc(s_dl, 1)
                    v.wait_ge(s_dl, g + 1)
                    from_step(2, v, s_T, g, g - 1)
                    from_step(2, v, s_oh, g, g - 1)
                    nc.vector.tensor_tensor(ohb[k % 2][:, :, :], C.iota[:, :].unsqueeze(1).broadcast_to([P, ET, P]),
                                            dl[k % 2][:, :].unsqueeze(2).broadcast_to([P, ET, P]), ALU.is_equal).then_inc(s_ohb, 1)

                def accumulate(g, k, blk):
                    a = C.acc3[:, ds(blk * 2 * D, 2 * D)]
                    v.wait_ge(s_sg, g + 1)
                    nc.vector.tensor_tensor(a, a, p_sg[k % 2][:, :], ALU.add).then_inc(s_acc, 1)
                    v.wait_ge(s_acc, g + 1)

                def step(g, k):
                    v.wait_ge(s_g[k], (g - k) * 16 + 64)
                    v.wait_ge(s_b, g + 1)
                    from_step(1, v, s_s, g, g)
                    nc.vector.tensor_tensor(tv[:, :, :], G[k][:, :, 0:D], p_b[k % 2][:, :, :], ALU.add).then_inc(s_t, 1)
                    if exists(g + 2):
                        one_hot(g + 2, (k + 2) % UN)
                    v.wait_ge(s_s, g + 1)
                    nc.vector.tensor_tensor(sv[k % 2][:, :, 0:D], G[k][:, :, D:2 * D], sv[k % 2][:, :, D:2 * D], ALU.mult).then_inc(s_use, 1)
                    if not isinstance(g, int) or g > 0:
                        accumulate(g - 1, (k - 1) % UN, block_of(v, g - 1))

                one_hot(0, 0)
                one_hot(1, 1)
                all_groups(v, step)
                accumulate(NG - 1, (NG - 1) % UN, block_of(v, NG - 1))

            @block.scalar
            def _(act):
                def columns(g, k):
                    act.wait_ge(s_T, g + 1)
                    from_step(2, act, s_b, g, g - 1)
                    nc.scalar.copy(ohT[k % 2][:, :], p_oT[k % 2][:, 0:EG]).then_inc(s_cp, 1)
                    from_step(UN, act, s_sg, g, g - UN + 1)
                    nc.scalar.copy(oh[k][:, :, :], ohb[k % 2][:, :, :]).then_inc(s_oh, 1)

                def step(g, k):
                    act.wait_ge(s_t, g + 1)
                    from_step(2, act, s_sg, g, g - 1)
                    nc.scalar.activation(sv[k % 2][:, :, D:2 * D], tv[:, :, :], ACT.Sigmoid).then_inc(s_s, 1)
                    if exists(g + 2):
                        columns(g + 2, (k + 2) % UN)

                columns(0, 0)
                columns(1, 1)
                all_groups(act, step)

            @block.tensor
            def _(pe):
                def transposes(g, k):
                    pe.wait_ge(s_ohb, g + 1)
                    from_step(2, pe, s_cp, g, g - 1)
                    for j in range(ET):
                        t = nc.tensor.transpose(p_oT[k % 2][:, j * P:j * P + P], ohb[k % 2][:, j, :], C.identb[:, :])
                    t.then_inc(s_T, 1)

                def expand(g, k, blk):
                    pe.wait_ge(s_cp, g + 1)
                    from_step(2, pe, s_t, g, g - 1)
                    for j in range(ET):
                        for s in range(3):
                            t = nc.tensor.matmul(p_b[k % 2][:, j, :], ohT[k % 2][:, j * P:j * P + P],
                                                 C.wr3[:, ds(blk * 3 * D + s * D, D)], start=(s == 0), stop=(s == 2))
                    t.then_inc(s_b, 1)

                def sums(g, k):
                    pe.wait_ge(s_use, g + 1)
                    pe.wait_ge(s_oh, g + 1)
                    from_step(2, pe, s_acc, g, g - 1)
                    for j in range(ET):
                        t = nc.tensor.matmul(p_sg[k % 2][:, :], oh[k][:, j, :], sv[k % 2][:, j, :], start=(j == 0), stop=(j == ET - 1))
                    t.then_inc(s_sg, 1)

                def step(g, k):
                    if exists(g + 2):
                        transposes(g + 2, (k + 2) % UN)
                    if exists(g + 1):
                        expand(g + 1, (k + 1) % UN, block_of(pe, g + 1))
                    sums(g, k)

                transposes(0, 0)
                transposes(1, 1)
                expand(0, 0, block_of(pe, 0))
                all_groups(pe, step)


def stage_dense(nc, C, A, out):
    with ExitStack() as ctx:
        sb, ps, sem = alloc(nc, ctx, "dense_")
        w1 = sb("w1", [P, KC, F]); b1 = sb("b1", [P, FC]); wgt = sb("wg", [P, FC, NE]); bg = sb("bg", [P, NE])
        Wd = sb("Wd", [P, NE * FC * D]); bd = sb("bd", [1, NE * D]); ones1 = sb("ones1", [1, P])
        pr = sb("pr", [P, NB]); slot = sb("slot", [P, NB], I32); expert = sb("expert", [P, NT], I32)
        gam = sb("gam", [P, D]); bet = sb("bet", [P, D])
        U = [sb(f"U{k}", [P, D]) for k in range(2)]; t1 = sb("t1d", [P, D]); t2 = sb("t2d", [P, D])
        st = sb("st", [P, NB * 6]); mv = sb("mv", [P, NB * 2]); rstd = sb("rstd", [P, NB])
        st2 = sb("st2d", [P, NB * 6]); mv2 = sb("mv2d", [P, NB * 2]); rstd2 = sb("rstd2", [P, NB])
        s_w = sem("s_w"); s_u = [sem(f"s_u{k}") for k in range(2)]; s_r = sem("s_r"); s_c = sem("s_c"); s_ur = sem("s_ur")
        s_st = sem("s_st"); s_var = sem("s_var"); s_std = sem("s_std"); s_st2 = sem("s_st2"); s_var2 = sem("s_var2"); s_std2 = sem("s_std2"); s_n = sem("s_n")
        s_wd = sem("s_wd")

        with nc.Block() as block:
            @block.sync
            def _(sp):
                sp.dma_start(gam[:, :], A["gamma"].partition_broadcast(P)).then_inc(s_w, 16)
                sp.dma_start(bet[:, :], A["beta"].partition_broadcast(P)).then_inc(s_w, 16)
                sp.dma_start(w1[:, :, :], A["fW1"].rearrange("(c p) f -> p c f", p=P)).then_inc(s_wd, 16)
                sp.dma_start(b1[:, :], A["fb1"].rearrange("(c p) -> p c", p=P), allow_slow_non_contiguous=True).then_inc(s_wd, 16)
                sp.dma_start(wgt[:, :, :], A["fWg"].rearrange("(c p) e -> p c e", p=P)).then_inc(s_wd, 16)
                sp.dma_start(bg[:, :], A["fbg"].partition_broadcast(P)).then_inc(s_wd, 16)
                sp.dma_start(bd[:, :], A["fbd"].rearrange("(a e) d -> a (e d)", a=1)).then_inc(s_wd, 16)

                def body(b, k):
                    if not isinstance(b, int) or b >= 2:
                        sp.wait_ge(s_ur, b - 1)
                    sp.dma_start(U[k][:, :], C.u_d[ds(b * P, P), :]).then_inc(s_u[k], 16)
                skewed(sp, NB, 2, lambda b, k: None, body, peel=2)

            @block.vector
            def _(v):
                v.wait_ge(s_w, 32)

                def body(b, k):
                    a = C.acc3[:, ds(b * 2 * D, D)]
                    d = C.acc3[:, ds(b * 2 * D + D, D)]
                    v.wait_ge(s_u[k], (b - k) * 8 + 16)
                    nc.vector.tensor_scalar(t1[:, :], d, 1e-6, None, ALU.add).then_inc(s_r, 1)
                    v.wait_ge(s_r, b * 4 + 1)
                    nc.vector.reciprocal(t1[:, :], t1[:, :]).then_inc(s_r, 1)
                    v.wait_ge(s_r, b * 4 + 2)
                    nc.vector.tensor_tensor(a, a, t1[:, :], ALU.mult).then_inc(s_r, 1)
                    v.wait_ge(s_r, b * 4 + 3)
                    nc.vector.tensor_tensor(a, a, U[k][:, :], ALU.add).then_inc(s_ur, 1)
                    v.wait_ge(s_ur, b + 1)
                    nc.vector.bn_stats(st[:, ds(b * 6, 6)], a).then_inc(s_r, 1)

                skewed(v, NB, 2, lambda b, k: None, body)
                v.wait_ge(s_r, 4 * NB)
                ln_finish(nc, v, mv, st, rstd, s_st, s_var, s_std, 1e-6)

                with v.Fori(0, NB) as b:
                    a = C.acc3[:, ds(b * 2 * D, D)]
                    x = C.X[:, ds(b * D, D)]
                    nc.vector.tensor_scalar(a, a, mv[:, ds(b * 2, 1)], rstd[:, ds(b, 1)], ALU.subtract, ALU.mult).then_inc(s_c, 1)
                    v.wait_ge(s_c, b * 5 + 1)
                    nc.vector.tensor_tensor(a, a, gam[:, :], ALU.mult).then_inc(s_c, 1)
                    v.wait_ge(s_c, b * 5 + 2)
                    nc.vector.tensor_tensor(a, a, bet[:, :], ALU.add).then_inc(s_c, 1)
                    v.wait_ge(s_c, b * 5 + 3)
                    nc.vector.scalar_tensor_tensor(out=x, in0=a, scalar=0.0, in1=x, op0=ALU.max, op1=ALU.add).then_inc(s_c, 1)
                    v.wait_ge(s_c, b * 5 + 4)
                    nc.vector.bn_stats(st2[:, ds(b * 6, 6)], x).then_inc(s_c, 1)
                v.wait_ge(s_c, 5 * NB)
                ln_finish(nc, v, mv2, st2, rstd2, s_st2, s_var2, s_std2, 1e-5)
                with v.Fori(0, NB) as b:
                    nc.vector.tensor_scalar(C.acc3[:, ds(b * 2 * D, D)], C.X[:, ds(b * D, D)], mv2[:, ds(b * 2, 1)], rstd2[:, ds(b, 1)],
                                            ALU.subtract, ALU.mult).then_inc(s_n, 1)
                v.wait_ge(s_n, NB)

            @block.scalar
            def _(act):
                act.dma_start(Wd[:, :].rearrange("p (c d) -> p c d", d=D), A["fWd"].rearrange("(c p) d -> p c d", p=P)).then_inc(s_wd, 16)
                ln_sqrt(nc, act, rstd, s_var, s_std)
                ln_sqrt(nc, act, rstd2, s_var2, s_std2)

        dense_gate(nc, C, w1, b1, wgt, bg, pr, slot, expert, s_wd)
        dense_tiles(nc, C, w1, b1, Wd, bd, ones1, expert, s_wd)
        dense_out(nc, C, pr, slot, out)


def hidden_loops(nc, w1, b1, xT, HT, p_t, p_h, s_t, s_tc, s_h, s_hc, s_used):
    def matmuls(pe, b, k):
        pe.wait_ge(s_tc, b + 1)
        for a in range(2):
            from_step(2, pe, s_hc, b, b * 2 - 3 + a)
            for c in range(4):
                q = a * 4 + c
                for kc in range(KC):
                    t = nc.tensor.matmul(p_h[k % 2][:, a, c * P:c * P + P], w1[:, kc, q * P:q * P + P], xT[k % 2][:, kc * P:kc * P + P],
                                         start=(kc == 0), stop=(kc == KC - 1))
            t.then_inc(s_h, 1)

    def copy_x(act, b, k):
        act.wait_ge(s_t, b + 1)
        from_step(2, act, s_h, b, b * 2 - 2)
        nc.scalar.copy(xT[k % 2][:, :], p_t[k % 2][:, 0:KC * P]).then_inc(s_tc, 1)

    def gelu(act, b, k):
        from_step(2, act, s_used, b, b - 1)
        for a in range(2):
            act.wait_ge(s_h, b * 2 + a + 1)
            for c in range(4):
                q = a * 4 + c
                t = nc.scalar.activation(HT[k % 2][:, q * P:q * P + P], p_h[k % 2][:, a, c * P:c * P + P], ACT.Gelu, bias=b1[:, q:q + 1])
            t.then_inc(s_hc, 1)

    return matmuls, copy_x, gelu


def dense_gate(nc, C, w1, b1, wgt, bg, pr, slot, expert, s_wd):
    with ExitStack() as ctx:
        sb, ps, sem = alloc(nc, ctx, "gate_")
        xn = [sb(f"xn{k}", [P, D]) for k in range(2)]; xT = [sb(f"xT{k}", [P, KC * P]) for k in range(2)]
        HT = [sb(f"HT{k}", [P, FC * P]) for k in range(2)]
        lg = sb("lg", [P, NB, NE]); mx8 = sb("mx8", [P, NB, 8]); ix8 = sb("ix8", [P, NB, 8], U32); ixf = sb("ixf", [P, NB])
        ex = sb("ex", [P, NB, NE]); sm = sb("sm", [P, NB])
        up = sb("up", [P, P]); onesq = sb("onesq", [P, P]); vali = sb("vali", [P, NB], I32); val = sb("val", [P, NB])
        one = sb("one", [P, NB, NE]); tot = sb("tot", [P, NB, NE]); run = sb("run", [P, NE, NB]); pos3 = sb("pos3", [P, NB, NE])
        tilesi = sb("tilesi", [P, NE], I32); tiles = sb("tiles", [P, NE]); tend = sb("tend", [P, NE]); start = sb("start", [P, NE])
        past = sb("past", [P, NT, NE]); pastn = sb("pastn", [P, NT])
        pos = sb("pos", [P, NB]); away = sb("away", [P, NB]); to = sb("to", [P, NB], I32)
        p_t = [ps(f"p_t{k}", [P, 512]) for k in range(2)]; p_h = [ps(f"p_h{k}", [P, 2, 512]) for k in range(2)]; p_l = ps("p_l", [P, 512]); p_c = ps("p_c", [P, 512])
        s_xn = sem("s_xn"); s_t = sem("s_t"); s_tc = sem("s_tc"); s_h = sem("s_h"); s_hc = sem("s_hc"); s_l = sem("s_l"); s_lc = sem("s_lc")
        s_m = sem("s_m"); s_e0 = sem("s_e0"); s_e1 = sem("s_e1"); s_v = sem("s_v"); s_pl = sem("s_pl"); s_one = sem("s_one"); s_cs = sem("s_cs")
        s_slot = sem("s_slot"); s_sc = sem("s_sc")
        matmuls, copy_x, gelu = hidden_loops(nc, w1, b1, xT, HT, p_t, p_h, s_t, s_tc, s_h, s_hc, s_l)

        with nc.Block() as block:
            @block.gpsimd
            def _(gp):
                nc.gpsimd.memset(up[:, :], 1.0).then_inc(s_pl, 1)
                nc.gpsimd.iota(vali[:, :], pattern=[[P, NB]], base=0, channel_multiplier=1).then_inc(s_pl, 1)
                gp.wait_ge(s_pl, 2)
                nc.gpsimd.affine_select(out=up[:, :], in_=up[:, :], compare_op=ALU.is_gt, fill=0.0, base=0,
                                        pattern=[[1, P]], channel_multiplier=-1).then_inc(s_pl, 1)
                gp.wait_ge(s_slot, 1)
                for b in range(NB):
                    gp.indirect_dma_start(out=C.xs_d[:, :], out_offset=bass.IndirectOffsetOnAxis(ap=to[:, b:b + 1], axis=0),
                                          in_=C.acc3[:, b * 2 * D:b * 2 * D + D], in_offset=None, bounds_check=NT * P - 1, oob_is_err=False).then_inc(s_sc, 16)
                gp.wait_ge(s_sc, 16 * NB)

            @block.vector
            def _(v):
                def front(b, k):
                    from_step(2, v, s_t, b, b - 1)
                    nc.vector.tensor_scalar(xn[k][:, :], C.acc3[:, ds(b * 2 * D, D)], 1.0, None, ALU.mult).then_inc(s_xn, 1)

                def logits(b):
                    v.wait_ge(s_l, b + 1)
                    nc.vector.tensor_tensor(lg[:, ds(b, 1), :].rearrange("p a e -> p (a e)"), p_l[:, 0:NE], bg[:, :], ALU.add).then_inc(s_lc, 1)

                def back(b, k):
                    if not isinstance(b, int) or b >= 1:
                        logits(b - 1)

                v.wait_ge(s_wd, 96)
                nc.vector.memset(onesq[:, :], 1.0).then_inc(s_v, 1)
                v.wait_ge(s_pl, 3)
                nc.vector.tensor_scalar(val[:, :], vali[:, :], float(N), None, ALU.is_lt).then_inc(s_v, 1)
                skewed(v, NB, 2, front, back, peel=2)
                logits(NB - 1)
                v.wait_ge(s_lc, NB)
                for b in range(NB):
                    nc.vector.max(mx8[:, b, :], lg[:, b, :]).then_inc(s_m, 1)
                v.wait_ge(s_m, NB)
                for b in range(NB):
                    nc.vector.max_index(ix8[:, b, :], mx8[:, b, :], lg[:, b, :]).then_inc(s_m, 1)
                nc.vector.tensor_tensor(ex[:, :, :], lg[:, :, :], mx8[:, :, 0:1].broadcast_to([P, NB, NE]), ALU.subtract).then_inc(s_e0, 1)
                v.wait_ge(s_m, 2 * NB)
                nc.vector.tensor_copy(ixf[:, :], ix8[:, :, 0]).then_inc(s_v, 1)
                v.wait_ge(s_v, 3)
                nc.vector.tensor_tensor(one[:, :, :], C.iota[:, 0:NE].unsqueeze(1).broadcast_to([P, NB, NE]),
                                        ixf[:, :].unsqueeze(2).broadcast_to([P, NB, NE]), ALU.is_equal).then_inc(s_v, 1)
                v.wait_ge(s_v, 4)
                nc.vector.tensor_tensor(one[:, :, :], one[:, :, :], val[:, :].unsqueeze(2).broadcast_to([P, NB, NE]), ALU.mult).then_inc(s_one, 1)
                v.wait_ge(s_e1, 1)
                nc.vector.tensor_reduce(sm[:, :], ex[:, :, :], AX.X, ALU.add).then_inc(s_v, 1)
                v.wait_ge(s_v, 5)
                nc.vector.reciprocal(pr[:, :], sm[:, :]).then_inc(s_v, 1)
                v.wait_ge(s_cs, 1)
                nc.vector.tensor_copy(tot[:, :, :], p_c[:, 256:256 + NB * NE].rearrange("p (b e) -> p b e", e=NE)).then_inc(s_v, 1)
                v.wait_ge(s_v, 7)
                for e in range(NE):
                    nc.vector.tensor_tensor_scan(run[:, e, :], tot[:, :, e], tot[:, :, e], 0.0, ALU.add, ALU.bypass).then_inc(s_v, 1)
                base = 7 + NE
                v.wait_ge(s_v, base)
                nc.vector.tensor_tensor(pos3[:, :, :], run[:, :, :].rearrange("p e b -> p b e"), tot[:, :, :], ALU.subtract).then_inc(s_v, 1)
                nc.vector.tensor_scalar(tilesi[:, :], run[:, :, NB - 1], float(P - 1), None, ALU.add).then_inc(s_v, 1)
                v.wait_ge(s_v, base + 2)
                nc.vector.tensor_tensor(pos3[:, :, :], pos3[:, :, :], p_c[:, 0:NB * NE].rearrange("p (b e) -> p b e", e=NE), ALU.add).then_inc(s_v, 1)
                nc.vector.tensor_scalar(tilesi[:, :], tilesi[:, :], P.bit_length() - 1, None, ALU.arith_shift_right).then_inc(s_v, 1)
                v.wait_ge(s_v, base + 4)
                nc.vector.tensor_copy(tiles[:, :], tilesi[:, :]).then_inc(s_v, 1)
                v.wait_ge(s_v, base + 5)
                nc.vector.tensor_tensor_scan(tend[:, :], tiles[:, :], tiles[:, :], 0.0, ALU.add, ALU.bypass).then_inc(s_v, 1)
                v.wait_ge(s_v, base + 6)
                nc.vector.tensor_tensor(start[:, :], tend[:, :], tiles[:, :], ALU.subtract).then_inc(s_v, 1)
                nc.vector.tensor_tensor(past[:, :, :], C.iota[:, 0:NT].unsqueeze(2).broadcast_to([P, NT, NE]),
                                        tend[:, :].unsqueeze(1).broadcast_to([P, NT, NE]), ALU.is_ge).then_inc(s_v, 1)
                v.wait_ge(s_v, base + 8)
                nc.vector.tensor_reduce(pastn[:, :], past[:, :, :], AX.X, ALU.add).then_inc(s_v, 1)
                nc.vector.tensor_scalar(start[:, :], start[:, :], float(P), None, ALU.mult).then_inc(s_v, 1)
                v.wait_ge(s_v, base + 10)
                nc.vector.tensor_scalar(expert[:, :], pastn[:, :], float(NE - 1), None, ALU.min).then_inc(s_v, 1)
                nc.vector.tensor_tensor(pos3[:, :, :], pos3[:, :, :], start[:, :].unsqueeze(1).broadcast_to([P, NB, NE]), ALU.add).then_inc(s_v, 1)
                v.wait_ge(s_v, base + 12)
                nc.vector.tensor_tensor(pos3[:, :, :], pos3[:, :, :], one[:, :, :], ALU.mult).then_inc(s_v, 1)
                nc.vector.tensor_scalar(away[:, :], val[:, :], float(-NT * P), float(NT * P), ALU.mult, ALU.add).then_inc(s_v, 1)
                v.wait_ge(s_v, base + 14)
                nc.vector.tensor_reduce(pos[:, :], pos3[:, :, :], AX.X, ALU.add).then_inc(s_v, 1)
                v.wait_ge(s_v, base + 15)
                nc.vector.tensor_tensor(to[:, :], pos[:, :], away[:, :], ALU.add).then_inc(s_slot, 1)
                nc.vector.tensor_copy(slot[:, :], pos[:, :]).then_inc(s_v, 1)

            @block.scalar
            def _(act):
                act.wait_ge(s_wd, 96)
                skewed(act, NB, 2, lambda b, k: copy_x(act, b, k), lambda b, k: gelu(act, b, k), peel=2)
                act.wait_ge(s_e0, 1)
                nc.scalar.activation(ex[:, :, :], ex[:, :, :], ACT.Exp).then_inc(s_e1, 1)

            @block.tensor
            def _(pe):
                pe.wait_ge(s_wd, 96)

                def front(b, k):
                    pe.wait_ge(s_xn, b + 1)
                    from_step(2, pe, s_tc, b, b - 1)
                    for c in range(KC):
                        t = nc.tensor.transpose(p_t[k][:, c * P:c * P + P], xn[k][:, c * P:c * P + P], C.ident[:, :])
                    t.then_inc(s_t, 1)

                def gate(b, k):
                    pe.wait_ge(s_hc, b * 2 + 2)
                    from_step(1, pe, s_lc, b, b)
                    for q in range(FC):
                        t = nc.tensor.matmul(p_l[:, 0:NE], HT[k][:, q * P:q * P + P], wgt[:, q, :], start=(q == 0), stop=(q == FC - 1))
                    t.then_inc(s_l, 1)

                def back(b, k):
                    matmuls(pe, b, k)
                    if not isinstance(b, int) or b >= 1:
                        gate(b - 1, 1 - k)

                skewed(pe, NB, 2, front, back, peel=2)
                gate(NB - 1, (NB - 1) % 2)
                pe.wait_ge(s_pl, 3)
                pe.wait_ge(s_v, 1)
                pe.wait_ge(s_one, 1)
                o = one[:, :, :].rearrange("p b e -> p (b e)")
                nc.tensor.matmul(p_c[:, 0:NB * NE], up[:, :], o, start=True, stop=True)
                nc.tensor.matmul(p_c[:, 256:256 + NB * NE], onesq[:, :], o, start=True, stop=True).then_inc(s_cs, 1)


def dense_tiles(nc, C, w1, b1, Wd, bd, ones1, expert, s_wd):
    with ExitStack() as ctx:
        sb, ps, sem = alloc(nc, ctx, "tiles_")
        xt = [sb(f"xt{k}", [P, D]) for k in range(4)]; xT = [sb(f"xT{k}", [P, KC * P]) for k in range(2)]
        HT = [sb(f"HT{k}", [P, FC * P]) for k in range(2)]; y = [sb(f"y{k}", [P, D]) for k in range(2)]
        p_t = [ps(f"p_t{k}", [P, 512]) for k in range(2)]; p_h = [ps(f"p_h{k}", [P, 2, 512]) for k in range(2)]
        p_y = [ps(f"p_y{k}", [P, 512]) for k in range(2)]
        s_x = [sem(f"s_x{k}") for k in range(4)]; s_t = sem("s_t"); s_tc = sem("s_tc"); s_h = sem("s_h"); s_hc = sem("s_hc")
        s_one = sem("s_one"); s_y = sem("s_y"); s_yc = sem("s_yc"); s_yd = [sem(f"s_yd{k}") for k in range(2)]
        matmuls, copy_x, gelu = hidden_loops(nc, w1, b1, xT, HT, p_t, p_h, s_t, s_tc, s_h, s_hc, s_y)

        with nc.Block() as block:
            @block.sync
            def _(sp):
                def load(t, k):
                    from_step(4, sp, s_t, t, t - 3)
                    sp.dma_start(xt[k][:, :], C.xs_d[ds(t * P, P), :]).then_inc(s_x[k], 16)

                skewed(sp, NT, 4, lambda t, k: None, load, peel=4)

            @block.gpsimd
            def _(gp):
                def store(t, k):
                    gp.wait_ge(s_yc, t + 1)
                    gp.dma_start(C.ys_d[ds(t * P, P), :], y[k][:, :]).then_inc(s_yd[k], 16)

                skewed(gp, NT, 2, lambda t, k: None, store)
                for k in range(2):
                    gp.wait_ge(s_yd[k], 16 * ((NT + 1 - k) // 2))

            @block.vector
            def _(v):
                nc.vector.memset(ones1[:, :], 1.0).then_inc(s_one, 1)

                def take(t, k):
                    v.wait_ge(s_y, t + 1)
                    from_step(2, v, s_yd[k], t, (t - k) * 8)
                    nc.vector.tensor_copy(y[k][:, :], p_y[k][:, 0:D]).then_inc(s_yc, 1)

                skewed(v, NT, 2, lambda t, k: None, take, peel=2)

            @block.scalar
            def _(act):
                skewed(act, NT, 2, lambda t, k: copy_x(act, t, k), lambda t, k: gelu(act, t, k), peel=2)

            @block.tensor
            def _(pe):
                pe.wait_ge(s_one, 1)

                def front(t, k):
                    pe.wait_ge(s_x[k], (t - k) * 4 + 16)
                    from_step(2, pe, s_tc, t, t - 1)
                    for c in range(KC):
                        m = nc.tensor.transpose(p_t[k % 2][:, c * P:c * P + P], xt[k][:, c * P:c * P + P], C.ident[:, :])
                    m.then_inc(s_t, 1)

                def outputs(t, k):
                    e = pe.value_load(expert[0:1, ds(t, 1)], min_val=0, max_val=NE - 1)
                    pe.wait_ge(s_hc, t * 2 + 2)
                    from_step(2, pe, s_yc, t, t - 1)
                    for q in range(FC):
                        nc.tensor.matmul(p_y[k % 2][:, 0:D], HT[k % 2][:, q * P:q * P + P], Wd[:, ds(e * (FC * D) + q * D, D)], start=(q == 0), stop=False)
                    nc.tensor.matmul(p_y[k % 2][:, 0:D], ones1[0:1, :], bd[0:1, ds(e * D, D)], start=False, stop=True).then_inc(s_y, 1)

                def back(t, k):
                    matmuls(pe, t, k)
                    if not isinstance(t, int) or t >= 1:
                        outputs(t - 1, (k - 1) % 4)

                skewed(pe, NT, 4, front, back, peel=4)
                outputs(NT - 1, (NT - 1) % 4)


def dense_out(nc, C, pr, slot, out):
    with ExitStack() as ctx:
        sb, ps, sem = alloc(nc, ctx, "out_")
        y = [sb(f"y{b}", [P, D]) for b in range(4)]
        s_y = [sem(f"s_y{k}") for k in range(4)]; s_x = sem("s_x"); s_out = sem("s_out")
        part = 5

        with nc.Block() as block:
            @block.gpsimd
            def _(gp):
                for b in range(NB):
                    if b >= 4:
                        gp.wait_ge(s_x, b - 3)
                    gp.indirect_dma_start(out=y[b % 4][:, :], out_offset=None, in_=C.ys_d[:, :],
                                          in_offset=bass.IndirectOffsetOnAxis(ap=slot[:, b:b + 1], axis=0)).then_inc(s_y[b % 4], 16)

            @block.vector
            def _(v):
                for b in range(NB):
                    x = C.X[:, b * D:b * D + D]
                    v.wait_ge(s_y[b % 4], 16 * (b // 4 + 1))
                    nc.vector.scalar_tensor_tensor(out=x, in0=y[b % 4][:, :], scalar=pr[:, b:b + 1], in1=x, op0=ALU.mult, op1=ALU.add).then_inc(s_x, 1)

            @block.sync
            def _(sp):
                stores = 0
                for lo in range(0, NB - 1, part):
                    hi = min(lo + part, NB - 1)
                    sp.wait_ge(s_x, hi)
                    sp.dma_start(out[lo * P:hi * P, :].rearrange("(b p) d -> p b d", p=P),
                                 C.X[:, lo * D:hi * D].rearrange("p (b d) -> p b d", d=D)).then_inc(s_out, 16)
                    stores += 1
                sp.wait_ge(s_x, NB)
                sp.dma_start(out[(NB - 1) * P:N, :], C.X[0:TAIL, (NB - 1) * D:NB * D]).then_inc(s_out, 16)
                sp.wait_ge(s_out, 16 * (stores + 1))


def build(nc, A, out):
    C = Consts()
    C.edge_rows = P * EC + EG

    def dram(name, shape, dt=F32):
        return nc.dram_tensor(name, shape, dt, kind="Internal").ap()

    C.edges = dram("edges_d", (C.edge_rows, 2), I32)
    C.gtab_d = dram("gtab_d", (2, GC * P), I32)
    C.tab1 = dram("tab1_d", (NP, TW))
    C.tab2 = dram("tab2_d", (NP, TW))
    C.tab3 = dram("tab3_d", (NP, 2 * D))
    C.u_d = dram("u_d", (NP, D))
    C.xs_d = dram("xs_d", (NT * P, D))
    C.ys_d = dram("ys_d", (NT * P, D))
    C.ffn_in = dram("ffn_in_d", (NE * CS, D))
    C.ffn_out = dram("ffn_out_d", (NE * CS, D))
    with ExitStack() as ctx:
        sb, ps, sem = alloc(nc, ctx)
        C.X = sb("X", [P, NB * D])
        C.ident = sb("ident", [P, P]); C.bigi = sb("bigi", [P, P], BF16); C.identb = sb("identb", [P, P], BF16); C.iota = sb("iota", [P, P]); C.lab = sb("lab", [P, NB])
        C.gofs = sb("gofs", [1, GC * P], I32); C.gblk = sb("gblk_r", [1, GC * P], I32)
        C.gblkb = sb("gblkb", [P, GC * P], I32); C.gbase = sb("gbase", [P, GC * P])
        C.gate = sb("gate", [P, NB]); C.back = sb("back", [P, NB], I32)
        with ExitStack() as first:
            sb, ps, sem = alloc(nc, first)
            C.em = sb("em", [P, NB * 2 * H])
            C.ler = sb("ler", [P, NB * 2 * H])
            C.bg3 = sb("bg3", [P, NB * 3 * 2 * H], BF16)
            C.near = sb("near", [P, 1], I32)
            C.below = sb("below", [P, NB + 2]); C.first = sb("first", [P, NB + 1]); C.unsorted = sb("unsorted", [P, 1], I32)
            C.acc = sb("acc", [P, NB * H * HW])
            stage_setup(nc, C, A)
            stage_sort(nc, C, A)
            stage_encode(nc, C, A)
            stage_scores(nc, C, C.tab1, 1)
            stage_attend_near(nc, C, C.tab1, 1)
            stage_attend(nc, C, C.tab1, 1)
            stage_between(nc, C, A)
            stage_scores(nc, C, C.tab2, 2)
            stage_attend_near(nc, C, C.tab2, 2)
            stage_attend(nc, C, C.tab2, 2)
            stage_route(nc, C, A)
        stage_experts(nc, C, A)
        with ExitStack() as second:
            sb, ps, sem = alloc(nc, second)
            C.acc3 = sb("acc3", [P, NB * 2 * D])
            with ExitStack() as third:
                sb, ps, sem = alloc(nc, third)
                C.wr3 = sb("wr3", [P, NB * 3 * D], BF16)
                stage_gated_in(nc, C, A)
                stage_gated(nc, C)
            stage_dense(nc, C, A, out)


def laid_out(inputs):
    a = {k: np.asarray(v) for k, v in inputs.items()}

    def heads(al, ar):
        m = np.zeros((D, 2 * H), np.float32)
        for h in range(H):
            m[h * HD:(h + 1) * HD, h] = al[h]
            m[h * HD:(h + 1) * HD, H + h] = ar[h]
        return m

    return {
        "x": a["x"], "src": a["src"], "dst": a["dst"], "node_type_24": a["node_type_24"],
        "embT": a["L0_gnn_emb"].T, "le_W1T": a["L0_gnn_le_W1"].T, "le_b1": a["L0_gnn_le_b1"], "ln_g": a["L0_gnn_ln_g"],
        "ln_b": a["L0_gnn_ln_b"], "le_W2T": a["L0_gnn_le_W2"].T, "le_b2": a["L0_gnn_le_b2"],
        "W1": a["L0_gnn_W1"], "W1T": a["L0_gnn_W1"].T, "alr1": heads(a["L0_gnn_al1"], a["L0_gnn_ar1"]),
        "b1": a["L0_gnn_b1"], "W2": a["L0_gnn_W2"], "W2T": a["L0_gnn_W2"].T, "alr2": heads(a["L0_gnn_al2"], a["L0_gnn_ar2"]), "b2": a["L0_gnn_b2"],
        "gate_w": a["L0_ffn_gate_w"], "gate_b": a["L0_ffn_gate_b"], "ew1": a["L0_ffn_w1"].reshape(NE * D, F), "eb1": a["L0_ffn_b1"],
        "ew2": a["L0_ffn_w2"].reshape(NE * F, D), "eb2": a["L0_ffn_b2"],
        "w3": np.concatenate([a["L1_gnn_W_w"], a["L1_gnn_U_w"], a["L1_gnn_V_w"]], axis=1),
        "b3": np.concatenate([a["L1_gnn_W_b"], a["L1_gnn_U_b"], a["L1_gnn_V_b"]]),
        "attn_l": a["L1_gnn_attn_l"], "attn_r": a["L1_gnn_attn_r"], "gamma": a["L1_gnn_gamma"], "beta": a["L1_gnn_beta"],
        "fW1": a["L1_ffn_W1"], "fb1": a["L1_ffn_b1"], "fWg": a["L1_ffn_Wg"], "fbg": a["L1_ffn_bg"],
        "fWd": a["L1_ffn_Wd"].reshape(NE * F, D), "fbd": a["L1_ffn_bd"],
    }


def kernel(**inputs):
    import concourse.bacc as _bacc
    from concourse import mybir as _mybir
    from concourse.bass_utils import run_bass_kernel_spmd as _run

    nc = _bacc.Bacc("TRN2", target_bir_lowering=False, num_devices=1)
    arrays, args = {}, {}
    for name, a in laid_out(inputs).items():
        a = np.ascontiguousarray(a)
        arrays[f"in_{name}"] = a
        args[name] = nc.dram_tensor(f"in_{name}", a.shape, _mybir.dt.from_np(a.dtype), kind="ExternalInput").ap()
    out = nc.dram_tensor("out_0", (N, D), _mybir.dt.float32, kind="ExternalOutput").ap()
    build(nc, args, out)
    r = _run(nc, [arrays], core_ids=[0])
    return r.results[0]["out_0"]
```
